# Optimizing a Trainium2 kernel written in Bass

```python
import numpy as np
import jax
import jax.numpy as jnp

def _softmax(x, axis=-1):
    return jax.nn.softmax(x, axis=axis)

def _gelu(x):
    return jax.nn.gelu(x, approximate=True)

def _silu(x):
    return jax.nn.silu(x)

def _sigmoid(x):
    return jax.nn.sigmoid(x)

def _layernorm(x, axis=-1, eps=1e-05):
    m = jnp.mean(x, axis=axis, keepdims=True)
    v = jnp.var(x, axis=axis, keepdims=True)
    return (x - m) / jnp.sqrt(v + eps)

def _scatter_add(tgt, idx, src, axis=0):
    return tgt.at[idx].add(src)

def _segment_sum(src, seg, n):
    return jax.ops.segment_sum(src, seg, n)
kernel_name = 'mk_metaformer_d1_conv_nchw1024_r2_1088f7'

def setup_inputs(seed: int=0):
    np.random.seed(seed)
    _w = jnp.asarray

    def _rec_inputs():
        import jax
        import jax.numpy as jnp
        _gk = jax.random.key(seed)
        x = -0.0006537 + 1.001 * jax.random.normal(jax.random.fold_in(_gk, 1), (4, 512, 24, 24), jnp.float32)
        return x
    x = _rec_inputs()

    def _L0_conv_setup():
        import jax, jax.numpy as jnp
        import numpy as np
        DIM = 512
        R = 2
        D_MODEL = DIM // (R * R)
        D_INNER = 2 * D_MODEL
        D_STATE = 16
        D_CONV = 4
        DT_RANK = (D_MODEL + 15) // 16
        NUM_TOKENS = 1

        def pixel_shuffle(x, r):
            B, C, H, W = x.shape
            c = C // (r * r)
            x = x.reshape(B, c, r, r, H, W)
            x = x.transpose(0, 1, 4, 2, 5, 3)
            return x.reshape(B, c, H * r, W * r)

        def pixel_unshuffle(x, r):
            B, C, Hr, Wr = x.shape
            H, W = (Hr // r, Wr // r)
            x = x.reshape(B, C, H, r, W, r)
            x = x.transpose(0, 1, 3, 5, 2, 4)
            return x.reshape(B, C * r * r, H, W)

        def mamba_block(seq, in_proj_w, conv_w, conv_b, x_proj_w, dt_proj_w, dt_proj_b, A_log, D, out_proj_w):
            B, L, _ = seq.shape
            xz = jnp.einsum('bld,ed->ble', seq, in_proj_w)
            u, z = jnp.split(xz, 2, axis=-1)
            up = jnp.pad(u, ((0, 0), (D_CONV - 1, 0), (0, 0)))
            u = sum((up[:, k:k + L, :] * conv_w[:, k] for k in range(D_CONV))) + conv_b
            u = jax.nn.silu(u)
            x_dbl = jnp.einsum('bld,ed->ble', u, x_proj_w)
            dt, Bm, Cm = jnp.split(x_dbl, [DT_RANK, DT_RANK + D_STATE], axis=-1)
            dt = jax.nn.softplus(jnp.einsum('blr,dr->bld', dt, dt_proj_w) + dt_proj_b)
            A = -jnp.exp(A_log)

            def step(h, inputs):
                dt_t, B_t, C_t, u_t = inputs
                dA = jnp.exp(dt_t[:, :, None] * A)
                h = dA * h + (dt_t * u_t)[:, :, None] * B_t[:, None, :]
                y = jnp.einsum('bdn,bn->bd', h, C_t)
                return (h, y)
            h0 = jnp.zeros((B, D_INNER, D_STATE), dtype=seq.dtype)
            xs = (dt.transpose(1, 0, 2), Bm.transpose(1, 0, 2), Cm.transpose(1, 0, 2), u.transpose(1, 0, 2))
            _, ys = jax.lax.scan(step, h0, xs)
            y = ys.transpose(1, 0, 2) + u * D
            y = y * jax.nn.silu(z)
            return jnp.einsum('bld,ed->ble', y, out_proj_w)
        key = jax.random.key(seed)
        ks = jax.random.split(key, 12)
        s = lambda k, shape, scale=0.02: jax.random.normal(k, shape, dtype=jnp.float32) * scale
        inp = {'x': jax.random.normal(ks[0], (4, DIM, 24, 24), dtype=jnp.float32), 'global_token': jnp.zeros((1, NUM_TOKENS, D_MODEL), dtype=jnp.float32), 'in_proj_w': s(ks[1], (2 * D_INNER, D_MODEL)), 'conv_w': s(ks[2], (D_INNER, D_CONV), 0.1), 'conv_b': jnp.zeros((D_INNER,), dtype=jnp.float32), 'x_proj_w': s(ks[3], (DT_RANK + 2 * D_STATE, D_INNER)), 'dt_proj_w': s(ks[4], (D_INNER, DT_RANK), 0.1), 'dt_proj_b': jax.random.uniform(ks[5], (D_INNER,), dtype=jnp.float32, minval=-4.0, maxval=-2.0), 'A_log': jnp.log(jnp.broadcast_to(jnp.arange(1, D_STATE + 1, dtype=jnp.float32), (D_INNER, D_STATE))), 'D': jnp.ones((D_INNER,), dtype=jnp.float32), 'out_proj_w': s(ks[6], (D_MODEL, D_INNER))}
        return inp
    _L0_conv_all = _L0_conv_setup()
    _L0_conv_in = {k: v for k, v in _L0_conv_all.items() if k in ('global_token', 'in_proj_w', 'conv_w', 'conv_b', 'x_proj_w', 'dt_proj_w', 'dt_proj_b', 'A_log', 'D', 'out_proj_w')}
    del _L0_conv_all

    def _L0_ffn_setup():
        import jax, jax.numpy as jnp
        import numpy as np
        B, S, H = (2, 512, 512)
        E, K, I = (8, 2, 1024)
        NUM_SHARED = 1
        NORM_TOPK = True

        def _moe_forward(x, gate_w, w1, w2, w3, sw1, sw2, sw3):
            Bq, Sq, Hq = x.shape
            xf = x.reshape(-1, Hq)
            scores = jax.nn.softmax(xf @ gate_w.T, axis=-1)
            topk_w, topk_idx = jax.lax.top_k(scores, K)
            if NORM_TOPK:
                topk_w = topk_w / (jnp.sum(topk_w, axis=-1, keepdims=True) + 1e-20)
            combine = jnp.sum(jax.nn.one_hot(topk_idx, E, dtype=xf.dtype) * topk_w[..., None], axis=1)
            h1 = jnp.einsum('th,ehi->tei', xf, w1)
            h3 = jnp.einsum('th,ehi->tei', xf, w3)
            act = jax.nn.silu(h1) * h3
            y = jnp.einsum('tei,te,eih->th', act, combine, w2)
            s1 = jnp.einsum('th,nhi->tni', xf, sw1)
            s3 = jnp.einsum('th,nhi->tni', xf, sw3)
            shared = jnp.einsum('tni,nih->th', jax.nn.silu(s1) * s3, sw2) / NUM_SHARED
            return (y + shared).reshape(Bq, Sq, Hq)
        key = jax.random.key(seed)
        ks = jax.random.split(key, 8)
        s_h = 1.0 / np.sqrt(H)
        s_i = 1.0 / np.sqrt(I)
        return {'x': jax.random.normal(ks[0], (B, S, H), jnp.float32), 'gate_w': jax.random.normal(ks[1], (E, H), jnp.float32) * s_h, 'w1': jax.random.normal(ks[2], (E, H, I), jnp.float32) * s_h, 'w2': jax.random.normal(ks[3], (E, I, H), jnp.float32) * s_i, 'w3': jax.random.normal(ks[4], (E, H, I), jnp.float32) * s_h, 'sw1': jax.random.normal(ks[5], (NUM_SHARED, H, I), jnp.float32) * s_h, 'sw2': jax.random.normal(ks[6], (NUM_SHARED, I, H), jnp.float32) * s_i, 'sw3': jax.random.normal(ks[7], (NUM_SHARED, H, I), jnp.float32) * s_h}
    _L0_ffn_all = _L0_ffn_setup()
    _L0_ffn_in = {k: v for k, v in _L0_ffn_all.items() if k in ('gate_w', 'w1', 'w2', 'w3', 'sw1', 'sw2', 'sw3')}
    del _L0_ffn_all
    return {'x': x, 'L0_conv_global_token': _L0_conv_in['global_token'], 'L0_conv_in_proj_w': _L0_conv_in['in_proj_w'], 'L0_conv_conv_w': _L0_conv_in['conv_w'], 'L0_conv_conv_b': _L0_conv_in['conv_b'], 'L0_conv_x_proj_w': _L0_conv_in['x_proj_w'], 'L0_conv_dt_proj_w': _L0_conv_in['dt_proj_w'], 'L0_conv_dt_proj_b': _L0_conv_in['dt_proj_b'], 'L0_conv_A_log': _L0_conv_in['A_log'], 'L0_conv_D': _L0_conv_in['D'], 'L0_conv_out_proj_w': _L0_conv_in['out_proj_w'], 'L0_ffn_gate_w': _L0_ffn_in['gate_w'], 'L0_ffn_w1': _L0_ffn_in['w1'], 'L0_ffn_w2': _L0_ffn_in['w2'], 'L0_ffn_w3': _L0_ffn_in['w3'], 'L0_ffn_sw1': _L0_ffn_in['sw1'], 'L0_ffn_sw2': _L0_ffn_in['sw2'], 'L0_ffn_sw3': _L0_ffn_in['sw3']}

def reference(x, L0_conv_global_token, L0_conv_in_proj_w, L0_conv_conv_w, L0_conv_conv_b, L0_conv_x_proj_w, L0_conv_dt_proj_w, L0_conv_dt_proj_b, L0_conv_A_log, L0_conv_D, L0_conv_out_proj_w, L0_ffn_gate_w, L0_ffn_w1, L0_ffn_w2, L0_ffn_w3, L0_ffn_sw1, L0_ffn_sw2, L0_ffn_sw3):
    import jax
    import jax.numpy as jnp

    def _L0_conv_ref(x, global_token, in_proj_w, conv_w, conv_b, x_proj_w, dt_proj_w, dt_proj_b, A_log, D, out_proj_w):
        import jax, jax.numpy as jnp
        import numpy as np
        DIM = 512
        R = 2
        D_MODEL = DIM // (R * R)
        D_INNER = 2 * D_MODEL
        D_STATE = 16
        D_CONV = 4
        DT_RANK = (D_MODEL + 15) // 16
        NUM_TOKENS = 1

        def pixel_shuffle(x, r):
            B, C, H, W = x.shape
            c = C // (r * r)
            x = x.reshape(B, c, r, r, H, W)
            x = x.transpose(0, 1, 4, 2, 5, 3)
            return x.reshape(B, c, H * r, W * r)

        def pixel_unshuffle(x, r):
            B, C, Hr, Wr = x.shape
            H, W = (Hr // r, Wr // r)
            x = x.reshape(B, C, H, r, W, r)
            x = x.transpose(0, 1, 3, 5, 2, 4)
            return x.reshape(B, C * r * r, H, W)

        def mamba_block(seq, in_proj_w, conv_w, conv_b, x_proj_w, dt_proj_w, dt_proj_b, A_log, D, out_proj_w):
            B, L, _ = seq.shape
            xz = jnp.einsum('bld,ed->ble', seq, in_proj_w)
            u, z = jnp.split(xz, 2, axis=-1)
            up = jnp.pad(u, ((0, 0), (D_CONV - 1, 0), (0, 0)))
            u = sum((up[:, k:k + L, :] * conv_w[:, k] for k in range(D_CONV))) + conv_b
            u = jax.nn.silu(u)
            x_dbl = jnp.einsum('bld,ed->ble', u, x_proj_w)
            dt, Bm, Cm = jnp.split(x_dbl, [DT_RANK, DT_RANK + D_STATE], axis=-1)
            dt = jax.nn.softplus(jnp.einsum('blr,dr->bld', dt, dt_proj_w) + dt_proj_b)
            A = -jnp.exp(A_log)

            def step(h, inputs):
                dt_t, B_t, C_t, u_t = inputs
                dA = jnp.exp(dt_t[:, :, None] * A)
                h = dA * h + (dt_t * u_t)[:, :, None] * B_t[:, None, :]
                y = jnp.einsum('bdn,bn->bd', h, C_t)
                return (h, y)
            h0 = jnp.zeros((B, D_INNER, D_STATE), dtype=seq.dtype)
            xs = (dt.transpose(1, 0, 2), Bm.transpose(1, 0, 2), Cm.transpose(1, 0, 2), u.transpose(1, 0, 2))
            _, ys = jax.lax.scan(step, h0, xs)
            y = ys.transpose(1, 0, 2) + u * D
            y = y * jax.nn.silu(z)
            return jnp.einsum('bld,ed->ble', y, out_proj_w)
        B, C, H, W = x.shape
        xs = pixel_shuffle(x, R)
        seq = xs.reshape(B, D_MODEL, -1).transpose(0, 2, 1)
        tok = jnp.broadcast_to(global_token, (B, NUM_TOKENS, D_MODEL))
        seq = jnp.concatenate([tok, seq], axis=1)
        seq = mamba_block(seq, in_proj_w, conv_w, conv_b, x_proj_w, dt_proj_w, dt_proj_b, A_log, D, out_proj_w)
        seq = seq[:, -H * W * R * R:, :]
        out = seq.reshape(B, H * R, W * R, D_MODEL).transpose(0, 3, 1, 2)
        return pixel_unshuffle(out, R)

    def _L0_ffn_ref(x, gate_w, w1, w2, w3, sw1, sw2, sw3):
        import jax, jax.numpy as jnp
        import numpy as np
        B, S, H = (2, 512, 512)
        E, K, I = (8, 2, 1024)
        NUM_SHARED = 1
        NORM_TOPK = True

        def _moe_forward(x, gate_w, w1, w2, w3, sw1, sw2, sw3):
            Bq, Sq, Hq = x.shape
            xf = x.reshape(-1, Hq)
            scores = jax.nn.softmax(xf @ gate_w.T, axis=-1)
            topk_w, topk_idx = jax.lax.top_k(scores, K)
            if NORM_TOPK:
                topk_w = topk_w / (jnp.sum(topk_w, axis=-1, keepdims=True) + 1e-20)
            combine = jnp.sum(jax.nn.one_hot(topk_idx, E, dtype=xf.dtype) * topk_w[..., None], axis=1)
            h1 = jnp.einsum('th,ehi->tei', xf, w1)
            h3 = jnp.einsum('th,ehi->tei', xf, w3)
            act = jax.nn.silu(h1) * h3
            y = jnp.einsum('tei,te,eih->th', act, combine, w2)
            s1 = jnp.einsum('th,nhi->tni', xf, sw1)
            s3 = jnp.einsum('th,nhi->tni', xf, sw3)
            shared = jnp.einsum('tni,nih->th', jax.nn.silu(s1) * s3, sw2) / NUM_SHARED
            return (y + shared).reshape(Bq, Sq, Hq)
        return _moe_forward(x, gate_w, w1, w2, w3, sw1, sw2, sw3)

    def _gn(v, G=32, eps=1e-05):
        B_, C_, H_, W_ = v.shape
        g = v.reshape(B_, G, C_ // G, H_, W_)
        m = jnp.mean(g, axis=(2, 3, 4), keepdims=True)
        s = jnp.var(g, axis=(2, 3, 4), keepdims=True)
        return ((g - m) / jnp.sqrt(s + eps)).reshape(v.shape)

    def _ln_c(v, eps=1e-06):
        m = jnp.mean(v, axis=1, keepdims=True)
        s = jnp.var(v, axis=1, keepdims=True)
        return (v - m) / jnp.sqrt(s + eps)

    def _ln_t(v, eps=1e-05):
        m = jnp.mean(v, axis=-1, keepdims=True)
        s = jnp.var(v, axis=-1, keepdims=True)
        return (v - m) / jnp.sqrt(s + eps)

    def _to_tokens(v):
        B_, C_, H_, W_ = v.shape
        return v.reshape(B_, C_, H_ * W_).transpose(0, 2, 1)

    def _from_tokens(t, like):
        B_, C_, H_, W_ = like.shape
        return t.transpose(0, 2, 1).reshape(B_, C_, H_, W_)
    x = x + _L0_conv_ref(_ln_c(x), L0_conv_global_token, L0_conv_in_proj_w, L0_conv_conv_w, L0_conv_conv_b, L0_conv_x_proj_w, L0_conv_dt_proj_w, L0_conv_dt_proj_b, L0_conv_A_log, L0_conv_D, L0_conv_out_proj_w)
    t = _to_tokens(x)
    t = t + _L0_ffn_ref(_ln_t(t), L0_ffn_gate_w, L0_ffn_w1, L0_ffn_w2, L0_ffn_w3, L0_ffn_sw1, L0_ffn_sw2, L0_ffn_sw3)
    x = _from_tokens(t, x)
    return x

_drawn_inputs = setup_inputs


def setup_inputs(seed=0):
    import zlib

    import numpy as np

    out = dict(_drawn_inputs(seed))
    spreads = {'L0_conv_global_token': (0.0, 2.0),
     'L0_conv_conv_b': (0.0, 0.696),
     'L0_conv_D': (1.0, 0.6)}
    factors = {'L0_conv_in_proj_w': 6.539,
     'L0_conv_conv_w': 8.0,
     'L0_conv_x_proj_w': 8.0,
     'L0_conv_dt_proj_w': 8.0,
     'L0_conv_dt_proj_b': 8.0,
     'L0_conv_A_log': 8.0,
     'L0_conv_out_proj_w': 5.062,
     'L0_ffn_gate_w': 8.0,
     'L0_ffn_w1': 8.0,
     'L0_ffn_w2': 8.0,
     'L0_ffn_w3': 8.0,
     'L0_ffn_sw1': 8.0,
     'L0_ffn_sw2': 8.0,
     'L0_ffn_sw3': 8.0}
    for name, (base, spread) in spreads.items():
        noise = np.random.default_rng([zlib.crc32(name.encode()), seed]).standard_normal(out[name].shape)
        drawn = base * np.exp(spread * noise) if base else spread * noise
        out[name] = jnp.asarray(drawn.astype(out[name].dtype))
    for name, factor in factors.items():
        out[name] = (out[name] * factor).astype(out[name].dtype)
    return out
```

```python
import concourse.bass as bass
from concourse import mybir
from contextlib import ExitStack


def bass_metaformer_mamba_moe_kernel(nc, x, token, in_w, conv_w, conv_b, xp_w, dtp_w, dtp_b,
                                     A_log, D_skip, out_w, gate_w, w1, w2, w3, sw1, sw2, sw3, out):
    fp32, bf16, i32 = mybir.dt.float32, mybir.dt.bfloat16, mybir.dt.int32
    ALU, ACT, AX = mybir.AluOpType, mybir.ActivationFunctionType, mybir.AxisListType
    ds = bass.ds

    P = 128
    B, C, H, W = x.shape
    R = 2
    RR = R * R
    PIX = H * W
    HALF = in_w.shape[0] // 2 // P
    NS = A_log.shape[1]
    RANK = dtp_w.shape[1]
    TAPS = conv_w.shape[1]
    HIST = TAPS - 1
    JC = 6
    HC = H // JC
    CP = HC * W
    T = CP * RR
    NCH = B * JC
    BC = 2 * NS
    E = gate_w.shape[0]
    I = w1.shape[2]
    IK = I // P
    TOK = B * PIX
    SHT = TOK // P
    RTT = (2 * TOK + E * (P - 1)) // P
    NT = SHT + RTT
    SETW = 3 * I * RR
    EPS_C, EPS_T = 1e-6, 1e-5
    SETUP = 2 + 3 * HALF * TAPS + 2 * (5 * HALF + RR)
    TOKEN_DONE = SETUP + 19
    R_CHOSEN = 33

    xrows = nc.dram_tensor("xrows", (NT * P, C), fp32, kind="Internal").ap()
    yrows = nc.dram_tensor("yrows", (NT * P, C), fp32, kind="Internal").ap()

    ctx = ExitStack()
    with ctx:
        def sb(name, shape, dt=fp32):
            return ctx.enter_context(nc.sbuf_tensor(name, shape, dt))

        def sem(name):
            return ctx.enter_context(nc.semaphore(name))

        X = sb("X", [P, B * RR, PIX])
        WALL = sb("WALL", [P, 2 * SETW])
        WS0, WS1 = WALL[:, 0:SETW], WALL[:, SETW:2 * SETW]
        ident = sb("ident", [P, P])
        meanw = sb("meanw", [P, P])
        Lg = sb("Lg", [CP, NCH, E])
        gT = sb("gT", [P, RR, E])
        dsti = sb("dsti", [CP, 2, NCH], i32)
        wgt = sb("wgt", [CP, 2, NCH])
        tset = sb("tset", [1, NT], i32)
        toff = sb("toff", [1, NT], i32)
        twait = sb("twait", [1, NT], i32)
        endt = sb("endt", [1, E], i32)

        at = [0]

        def part(n):
            v = WS1[:, at[0]:at[0] + n]
            at[0] += n
            assert at[0] <= SETW
            return v
        dA = [part(HALF * T).rearrange("p (h t) -> p h t", h=HALF) for _ in range(3)]
        dBu = [part(HALF * T).rearrange("p (h t) -> p h t", h=HALF) for _ in range(3)]
        hs = [part(HALF * T).rearrange("p (h t) -> p h t", h=HALF) for _ in range(3)]
        hC = [part(HALF * T).rearrange("p (h t) -> p h t", h=HALF) for _ in range(3)]
        Cs = [part(T) for _ in range(2)]
        yd = part(HALF * T).rearrange("p (h t) -> p h t", h=HALF)
        cen = part(T).rearrange("p (r q) -> p r q", r=RR)
        sq = part(T).rearrange("p (r q) -> p r q", r=RR)
        cen2 = part(T).rearrange("p (r q) -> p r q", r=RR)
        sq2 = part(T).rearrange("p (r q) -> p r q", r=RR)
        u2 = sb("u2", [P, 2, HALF * T])
        u = [u2[:, k, :].rearrange("p (h t) -> p h t", h=HALF) for k in range(2)]
        z = [sb(f"z{k}", [P, HALF, T]) for k in range(2)]
        dt = [sb(f"dt{k}", [P, HALF, T]) for k in range(2)]
        dtu = [sb(f"dtu{k}", [P, HALF, T]) for k in range(2)]
        seq = [sb(f"seq{k}", [P, HIST + T]) for k in range(2)]
        S = [sb(f"S{k}", [3 * BC, T], bf16) for k in range(2)]
        Rm = sb("Rm", [2 * BC, T])
        dtr = sb("dtr", [RANK, T])
        absx = sb("absx", [P, HALF, T])
        relx = sb("relx", [P, HALF, T])
        expx = sb("expx", [P, HALF, T])
        lnx = sb("lnx", [P, HALF, T])
        onex = sb("onex", [P, HALF, T])
        st = sb("st", [P, 4, CP])
        st2 = sb("st2", [P, 4, CP])
        rows = [sb(f"rows{k}", [CP, C]) for k in range(2)]
        carry = sb("carry", [P, NS, HALF])
        h0 = sb("h0", [P, NS, HALF])
        tokh = sb("tokh", [P, HIST])
        sel = sb("sel", [3 * BC, BC, P], bf16)
        Wu = sb("Wu", [P, HALF, TAPS, P])
        Wz = sb("Wz", [P, HALF, P])
        Wx = sb("Wx", [P, HALF, 3 * BC])
        Wr = sb("Wr", [P, HALF, RANK])
        Wd = sb("Wd", [RANK, HALF, P])
        Wo = sb("Wo", [P, HALF, P])
        cb = sb("cb", [P, HALF])
        db = sb("db", [P, HALF])
        Dk = sb("Dk", [P, HALF])
        An = sb("An", [P, HALF, NS])
        in_raw = dA[0].rearrange("p h t -> p (h t)")[:, 0:512].rearrange("p (k d) -> p k d", k=4)
        wsc = dA[1].rearrange("p h t -> p (h t)")[:, 0:P]
        cw = dA[1].rearrange("p h t -> p (h t)")[:, P:P + 8].rearrange("p (h k) -> p h k", h=HALF)
        xp_raw = dA[2].rearrange("p h t -> p (h t)")[0:3 * BC, 0:256]
        xr_raw = dA[2].rearrange("p h t -> p (h t)")[0:RANK, 256:512]
        dp_raw = dBu[0].rearrange("p h t -> p (h t)")[:, 0:16].rearrange("p (h k) -> p h k", h=HALF)
        ow_raw = dBu[0].rearrange("p h t -> p (h t)")[:, 16:16 + 256]
        gw_raw = dBu[1].rearrange("p h t -> p (h t)")[0:E, 0:512]
        al_raw = hs[0].rearrange("p h t -> p (h t)")[:, 0:32].rearrange("p (h k) -> p h k", h=HALF)
        zrow = sb("zrow", [P, P])

        bank = [ctx.enter_context(nc.psum_tensor(f"bank{k}", [P, 512], fp32)) for k in range(8)]
        Yb = [bank[0], bank[1]]
        Bb = [bank[2], bank[3]]
        Cb = bank[4]
        M0, M2, M1 = bank[5], bank[6], bank[7]

        s_in = sem("inputs_loaded")
        s_const = sem("constants_made")
        s_setup = sem("setup_step")
        s_passed = sem("pool_passed_its_waits")
        s_zero = sem("zero_rows_written")
        s_x = sem("x_loaded")
        s_w = sem("expert_weights_loaded")
        f_mean, f_cen, f_sq, f_var, f_ln, f_rsq = (sem("f_" + n) for n in
                                                   "mean centred squared var ln rsqrt".split())
        f_st = sem("f_stat_step")
        f_seq = sem("f_seq_written")
        f_hist = sem("f_hist_copied")
        f_ups, f_zps = sem("f_u_in_psum"), sem("f_z_in_psum")
        f_u, f_z = sem("f_u_silu"), sem("f_z_silu")
        f_bcps, f_rps, f_dtps = sem("f_bc_in_psum"), sem("f_rank_in_psum"), sem("f_dt_in_psum")
        f_hi, f_res, f_mid, f_lo = (sem("f_bc_" + n) for n in "hi residue mid lo".split())
        f_rank = sem("f_rank_copied")
        f_abs = sem("f_abs_relu")
        f_exp = sem("f_exp")
        f_ln1 = sem("f_ln1p")
        f_nd = sem("f_rounding_of_1p")
        f_dt1 = sem("f_dt_small")
        f_dt, f_dtu = sem("f_dt"), sem("f_dtu")
        m_B, m_C = sem("m_B_in_psum"), sem("m_C_in_psum")
        m_dA, m_Cs = sem("m_dA"), sem("m_C_copied")
        m_dBu, m_h = sem("m_dBu"), sem("m_h_scanned")
        m_hC, m_carry = sem("m_hC"), sem("m_carry")
        m_y = sem("m_y_added")
        b_yd, b_ydz, b_ops, b_x = (sem("b_" + n) for n in "y_read gated out_in_psum residual".split())
        b_mean, b_cen, b_sq, b_var, b_ln, b_rsq = (sem("b_" + n) for n in
                                                   "mean centred squared var ln rsqrt".split())
        b_st = sem("b_stat_step")
        b_xn = sem("b_normalised")
        b_tr, b_rows, b_lps, b_log = (sem("b_" + n) for n in
                                      "transposed rows_copied logits_in_psum logits".split())
        b_out = [sem("b_rows_stored0"), sem("b_rows_stored1")]
        r_ch = sem("routing_step")
        r_exp = sem("r_exp")
        r_ps = sem("r_counts_in_psum")
        r_done = sem("routed")
        r_ld = [sem("r_rows_loaded0"), sem("r_rows_loaded1")]
        r_ix = sem("r_index_copied")
        r_sc = [sem("r_scattered0"), sem("r_scattered1")]
        t_x = [sem("t_x_loaded0"), sem("t_x_loaded1")]
        t_xps, t_xT = sem("t_x_transposed"), sem("t_xT_copied")
        t_h, t_silu, t_act = sem("t_h_in_psum"), sem("t_silu"), sem("t_act")
        t_aps, t_aT = sem("t_act_transposed"), sem("t_actT_copied")
        t_yps, t_y = sem("t_y_in_psum"), sem("t_y_copied")
        t_out = [sem("t_y_stored0"), sem("t_y_stored1")]
        c_sh = [sem("c_shared_loaded0"), sem("c_shared_loaded1")]
        c_ix = sem("c_index_copied")
        c_g = [sem("c_gathered0"), sem("c_gathered1")]
        c_a, c_s = sem("c_first_added"), sem("c_summed")
        c_ps, c_x = sem("c_transposed"), sem("c_added")
        c_out = sem("c_out_stored")

        def flat(t):
            return t[:, :, :].rearrange("p h t -> p (h t)")
        xin = [flat(u[k])[:, 0:C] for k in range(2)]
        xT = [flat(z[k])[:, 0:C].rearrange("p (r t) -> p r t", r=RR) for k in range(2)]
        sil = [flat(dt[k])[:, 0:512] for k in range(2)]
        act = [flat(dtu[k])[:, 0:512] for k in range(2)]
        actT = [flat(absx)[:, 0:512].rearrange("p (k t) -> p k t", k=4),
                flat(relx)[:, 0:512].rearrange("p (k t) -> p k t", k=4)]
        yout = [flat(expx)[:, 0:512], flat(lnx)[:, 0:512]]
        ysh = [flat(u[k])[0:CP, 0:C] for k in range(2)]
        y0 = [flat(z[k])[0:CP, 0:C] for k in range(2)]
        y1 = [flat(dt[k])[0:CP, 0:C] for k in range(2)]
        ysum = [flat(dtu[k])[0:CP, 0:C] for k in range(2)]
        ixc = sb("ixc", [CP, 2, 2], i32)
        rt = [flat(t)[0:CP, 0:NCH * E] for t in (absx, relx, expx, lnx, onex, dtu[0])]
        cmp3 = u2[0:CP, :, :].rearrange("p k t -> p (k t)")[:, 0:NCH * E * E]
        tri = sb("tri", [CP, CP])
        one96 = sb("one96", [CP, CP])
        low = sb("low", [CP, E, E])
        tileno = sb("tileno", [CP, RTT], i32)
        small = flat(dt[1])[0:CP, 0:8 * RTT].rearrange("p (a t) -> p a t", a=8)
        smalli = sb("smalli", [CP, E], i32)

        NLOAD = [0]
        NCONST = 9

        def weights_of(q, ws):
            a, b3, b2 = (sw1[0], sw3[0], sw2[0]) if q == 0 else (w1[q - 1], w3[q - 1], w2[q - 1])
            return ((ws[:, 0:4096].rearrange("p (r i) -> p r i", r=RR), a.rearrange("(c r) i -> c r i", r=RR)),
                    (ws[:, 4096:8192].rearrange("p (r i) -> p r i", r=RR), b3.rearrange("(c r) i -> c r i", r=RR)),
                    (ws[:, 8192:12288].rearrange("p (k n) -> p k n", k=IK), b2.rearrange("(k p) n -> p k n", p=P)))

        def peeled(eng, stop, body):
            body(0)
            with eng.Fori(1, stop) as i:
                body(i)

        def started(i):
            return not (isinstance(i, int) and i == 0)

        block = ctx.enter_context(nc.Block())

        def xchunk(b, j):
            return X[:, ds(b * RR, RR), j * CP:(j + 1) * CP] if not isinstance(b, int) else \
                X[:, b * RR:(b + 1) * RR, j * CP:(j + 1) * CP]

        def batches(eng, body):
            body(0, True, False)
            with eng.Fori(1, B - 1) as b:
                body(b, False, False)
            body(B - 1, False, True)

        @block.sync
        def _(sp):
            loads = [
                (in_raw, in_w.rearrange("(k e) d -> e k d", e=P)),
                (cw, conv_w.rearrange("(h p) k -> p h k", p=P)),
                (xp_raw[0:BC, :], xp_w[RANK:RANK + BC, :]),
                (xp_raw[BC:2 * BC, :], xp_w[RANK:RANK + BC, :]),
                (xp_raw[2 * BC:3 * BC, :], xp_w[RANK:RANK + BC, :]),
                (xr_raw, xp_w[0:RANK, :]),
                (dp_raw, dtp_w.rearrange("(h p) k -> p h k", p=P)),
                (ow_raw, out_w),
                (gw_raw, gate_w),
                (al_raw, A_log.rearrange("(h p) k -> p h k", p=P)),
                (cb[:, :], conv_b.rearrange("(h p) -> p h", p=P)),
                (db[:, :], dtp_b.rearrange("(h p) -> p h", p=P)),
                (Dk[:, :], D_skip.rearrange("(h p) -> p h", p=P)),
                (tokh[:, HIST - 1:HIST], token.rearrange("a b c -> c (a b)")),
            ]
            NLOAD[0] = 16 * len(loads)
            with nc.allow_non_contiguous_dma(reason="a few vectors of 256 entries"):
                for dst, src in loads:
                    sp.dma_start(dst, src).then_inc(s_in, 16)
            for b in range(B):
                sp.dma_start(X[:, b * RR:(b + 1) * RR, :].rearrange("p r q -> p (r q)"),
                             x[b].rearrange("(c r) h w -> c (r h w)", r=RR)).then_inc(s_x, 16)
            sp.wait_ge(s_const, NCONST)
            with sp.Fori(SHT, NT) as t:
                sp.dma_start(xrows[ds(t * P, P), :].rearrange("p (r c) -> p r c", r=RR),
                             zrow[:, :].unsqueeze(1).to_broadcast([P, RR, P])).then_inc(s_zero, 16)

            def batch(b, first, last):
                for j in range(JC):
                    g = b * JC + j
                    if first and j == 0:
                        continue
                    sp.wait_ge(b_rows, g)
                    sp.dma_start(xrows[ds((g - 1) * CP, CP), :], rows[(j + 1) % 2][:, :])\
                      .then_inc(b_out[(j + 1) % 2], 16)
            batches(sp, batch)
            sp.wait_ge(b_rows, NCH)
            sp.dma_start(xrows[(NCH - 1) * CP:NCH * CP, :], rows[1][:, :]).then_inc(b_out[1], 16)

            sp.wait_ge(b_out[0], 16 * (NCH // 2))
            sp.wait_ge(b_out[1], 16 * (NCH // 2))
            def load_rows(g2):
                for k in range(2):
                    if started(g2):
                        sp.wait_ge(r_sc[k], 32 * g2)
                    sp.dma_start(rows[k][:, :], xrows[ds((2 * g2 + k) * CP, CP), :]).then_inc(r_ld[k], 16)
            peeled(sp, NCH // 2, load_rows)
            sp.wait_ge(r_sc[0], 32 * (NCH // 2))
            sp.wait_ge(r_sc[1], 32 * (NCH // 2))
            sp.wait_ge(s_zero, 16 * RTT)


            def load_tile(t, k):
                sp.dma_start(xin[k], xrows[ds(t * P, P), :]).then_inc(t_x[k], 16)

            def store_tile(t, k):
                sp.wait_ge(t_y, t + 1)
                sp.dma_start(yrows[ds(t * P, P), :], yout[k]).then_inc(t_out[k], 16)
            load_tile(0, 0)
            load_tile(1, 1)
            with sp.Fori(0, (NT - 3) // 2) as t2:
                for k in range(2):
                    sp.wait_ge(t_xps, 2 * t2 + k + 1)
                    load_tile(2 * t2 + k + 2, k)
                    store_tile(2 * t2 + k, k)
            sp.wait_ge(t_xps, NT - 2)
            load_tile(NT - 1, 0)
            for t in range(NT - 3, NT):
                store_tile(t, t % 2)

            sp.wait_ge(t_out[0], 16 * ((NT + 1) // 2))
            sp.wait_ge(t_out[1], 16 * (NT // 2))
            sp.wait_ge(t_y, NT)
            def load_shared(b):
                for j in range(JC):
                    g = b * JC + j
                    k = j % 2
                    if started(b) or j > 1:
                        sp.wait_ge(c_s, g if j == 0 else g - 1)
                    sp.dma_start(ysh[k], yrows[ds(g * CP, CP), :]).then_inc(c_sh[k], 16)
                sp.wait_ge(c_x, (b + 1) * JC)
                sp.dma_start(out[ds(b, 1), :, :, :].rearrange("a (c r) h w -> c (a r h w)", r=RR),
                             X[:, ds(b * RR, RR), :].rearrange("p r q -> p (r q)")).then_inc(c_out, 16)
            peeled(sp, B, load_shared)
            sp.wait_ge(c_out, 16 * B)

        @block.gpsimd
        def _(pool):
            pool.memset(ident[:, :], 0.0).then_inc(s_const, 1)
            pool.memset(meanw[:, :], 1.0 / C).then_inc(s_const, 1)
            pool.memset(sel[:, :, :], 0.0).then_inc(s_const, 1)
            pool.memset(tri[:, :], 1.0)
            pool.memset(one96[:, :], 1.0)
            pool.memset(low[:, :, :], 1.0)
            pool.memset(tokh[:, 0:HIST - 1], 0.0)
            pool.memset(zrow[:, :], 0.0).then_inc(s_const, 1)
            pool.wait_ge(s_const, 4)
            pool.affine_select(out=ident[:, :], in_=ident[:, :], compare_op=ALU.not_equal, fill=1.0,
                               base=0, pattern=[[-1, P]], channel_multiplier=1).then_inc(s_const, 1)
            pool.affine_select(out=tri[:, :], in_=tri[:, :], compare_op=ALU.is_gt, fill=0.0,
                               base=0, pattern=[[1, CP]], channel_multiplier=-1)
            pool.affine_select(out=low[:, :, :], in_=low[:, :, :], compare_op=ALU.is_gt, fill=0.0,
                               base=0, pattern=[[1, E], [-1, E]], channel_multiplier=0)
            pool.iota(tileno[:, :], pattern=[[1, RTT]], base=0, channel_multiplier=0)
            for q in range(3):
                if q:
                    pool.wait_ge(s_const, 5 + q)
                pool.affine_select(out=sel[:, :, :], in_=sel[:, :, :], compare_op=ALU.not_equal, fill=1.0,
                                   base=-BC * q, pattern=[[-1, BC], [0, P]], channel_multiplier=1)\
                    .then_inc(s_const, 1)
            pool.memset(carry[:, :, :], 0.0).then_inc(s_const, 1)

            def on_a_count():
                pool.sem_inc(s_passed, 1)

            def softplus_tail(n, g, k):
                if n == 13:
                    pool.wait_ge(f_ln1, g + 1)
                    pool.wait_ge(f_nd, g + 1)
                    if not (isinstance(g, int) and g < 2):
                        pool.wait_ge(m_dA, NS * (g - 1))
                        pool.wait_ge(m_dBu, NS * (g - 1))
                    pool.tensor_tensor(dt[k][:, :, :], lnx[:, :, :], onex[:, :, :], ALU.subtract).then_inc(f_dt1, 1)
                if n == 14:
                    pool.wait_ge(f_dt1, g + 1)
                    pool.tensor_tensor(dt[k][:, :, :], dt[k][:, :, :], relx[:, :, :], ALU.add).then_inc(f_dt, 1)
                if n == 15:
                    pool.wait_ge(f_dt, g + 1)
                    pool.wait_ge(f_u, 2 * g + 2)
                    pool.tensor_tensor(dtu[k][:, :, :], dt[k][:, :, :], u[k][:, :, :], ALU.mult).then_inc(f_dtu, 1)

            def history(g, k, start):
                if not (isinstance(g, int) and g < 2):
                    pool.wait_ge(f_zps, 2 * (g - 1))
                if start:
                    on_a_count()
                    pool.tensor_copy(seq[k][:, 0:HIST], tokh[:, :]).then_inc(f_hist, 1)
                else:
                    pool.wait_ge(f_seq, g)
                    on_a_count()
                    pool.tensor_copy(seq[k][:, 0:HIST], seq[1 - k][:, T:T + HIST]).then_inc(f_hist, 1)

            for dst, src in weights_of(0, WS0):
                pool.dma_start(dst, src).then_inc(s_w, 16)
            pool.wait_ge(s_in, 16 * 14)
            history(0, 0, True)
            for n in range(NS):
                softplus_tail(n, 0, 0)

            def batch(b, first, last):
                for j in range(JC):
                    g, k = b * JC + j, j % 2
                    front = not (last and j == JC - 1)
                    for n in range(NS):
                        i = NS * g + n
                        m = (NS * j + n) % 3
                        if front and n == 1:
                            history(g + 1, 1 - k, j == JC - 1)
                        pool.wait_ge(m_h, i + 1)
                        pool.wait_ge(m_Cs, i + 1)
                        if not (first and j == 0 and n < 3):
                            pool.wait_ge(m_y, i - 2)
                        pool.tensor_tensor(hC[m], hs[m], Cs[n % 2].unsqueeze(1).to_broadcast([P, HALF, T]),
                                           ALU.mult).then_inc(m_hC, 1)
                        pool.tensor_copy(carry[:, n, :], hs[m][:, :, T - 1]).then_inc(m_carry, 1)
                        if front:
                            softplus_tail(n, g + 1, 1 - k)
            batches(pool, batch)

            pool.wait_ge(b_x, NCH)
            pool.wait_ge(b_lps, NCH)
            pool.wait_ge(m_carry, NS * NCH)
            pool.wait_ge(m_y, NS * NCH)
            pool.wait_ge(s_w, 48)
            for dst, src in weights_of(1, WS1):
                pool.dma_start(dst, src).then_inc(s_w, 16)

            pool.wait_ge(r_done, 1)
            pool.wait_ge(s_zero, 16 * RTT)
            def scatter(g2):
                for k in range(2):
                    if started(g2):
                        pool.wait_ge(r_sc[k], 32 * g2)
                    on_a_count()
                    pool.tensor_copy(ixc[:, :, k], dsti[:, :, ds(2 * g2 + k, 1)].rearrange("p s g -> p (s g)"))\
                        .then_inc(r_ix, 1)
                    pool.wait_ge(r_ix, 2 * g2 + k + 1)
                    pool.wait_ge(r_ld[k], 16 * g2 + 16)
                    on_a_count()
                    for s in range(2):
                        pool.indirect_dma_start(
                            out=xrows, out_offset=bass.IndirectOffsetOnAxis(ap=ixc[:, s, k:k + 1], axis=0),
                            in_=rows[k][:, :], in_offset=None).then_inc(r_sc[k], 16)
            peeled(pool, NCH // 2, scatter)

            for q in range(2, E + 1):
                if q == 2:
                    pool.wait_ge(t_yps, SHT)
                else:
                    pool.wait_ge(t_yps, pool.value_load(endt[0:1, q - 3:q - 2], min_val=SHT, max_val=NT))
                pool.wait_ge(s_w, 48 * q)
                on_a_count()
                for dst, src in weights_of(q, (WS0, WS1)[q % 2]):
                    pool.dma_start(dst, src).then_inc(s_w, 16)

            pool.wait_ge(t_out[0], 16 * ((NT + 1) // 2))
            pool.wait_ge(t_out[1], 16 * (NT // 2))
            pool.wait_ge(r_sc[0], 32 * (NCH // 2))
            pool.wait_ge(r_sc[1], 32 * (NCH // 2))
            pool.wait_ge(t_act, 2 * NT)
            def gather(g2):
                for k in range(2):
                    if started(g2):
                        pool.wait_ge(c_g[k], 32 * g2)
                        pool.wait_ge(c_s, 2 * g2)
                    on_a_count()
                    pool.tensor_copy(ixc[:, :, k], dsti[:, :, ds(2 * g2 + k, 1)].rearrange("p s g -> p (s g)"))\
                        .then_inc(c_ix, 1)
                    pool.wait_ge(c_ix, 2 * g2 + k + 1)
                    on_a_count()
                    for s, dst in enumerate((y0, y1)):
                        pool.indirect_dma_start(
                            out=dst[k], out_offset=None, in_=yrows,
                            in_offset=bass.IndirectOffsetOnAxis(ap=ixc[:, s, k:k + 1], axis=0)).then_inc(c_g[k], 16)
            peeled(pool, NCH // 2, gather)

        @block.scalar
        def _(sc):
            nsc = nc.scalar
            sc.wait_ge(s_in, 16 * 14)
            nsc.activation(An[:, :, :], al_raw, ACT.Exp).then_inc(s_setup, 1)

            def silu_u(g, k):
                for h in range(HALF):
                    sc.wait_ge(f_ups, 2 * g + h + 1)
                    if h == 0 and not (isinstance(g, int) and g < 2):
                        sc.wait_ge(b_yd, g - 1)
                        sc.wait_ge(f_dtu, g - 1)
                        sc.wait_ge(b_ydz, g - 1)
                    nsc.activation(u[k][:, h, :], (M0, M2)[h][:, 0:T], ACT.Silu, bias=cb[:, h:h + 1])\
                       .then_inc(f_u, 1)
                for h in range(HALF):
                    sc.wait_ge(f_zps, 2 * g + h + 1)
                    nsc.activation(z[k][:, h, :], (M0, M2)[h][:, 0:T], ACT.Silu).then_inc(f_z, 1)

            def bc_hi(g, k):
                sc.wait_ge(f_bcps, g + 1)
                if not (isinstance(g, int) and g < 2):
                    sc.wait_ge(m_B, NS * (g - 1))
                    sc.wait_ge(m_C, NS * (g - 1))
                nsc.activation(S[k][:, :], M0[0:3 * BC, 0:T], ACT.Copy).then_inc(f_hi, 1)
                sc.wait_ge(f_rps, g + 1)
                if not (isinstance(g, int) and g < 1):
                    sc.wait_ge(f_dtps, 2 * g)
                nsc.activation(dtr[:, :], M2[0:RANK, 0:T], ACT.Copy).then_inc(f_rank, 1)

            def bc_mid(g, k):
                sc.wait_ge(f_res, g + 1)
                nsc.activation(S[k][0:2 * BC, :], Rm[:, :], ACT.Copy).then_inc(f_mid, 1)

            def softplus_head(g):
                if not (isinstance(g, int) and g < 1):
                    sc.wait_ge(f_nd, g)
                    sc.wait_ge(f_dt, g)
                for h in range(HALF):
                    sc.wait_ge(f_dtps, 2 * g + h + 1)
                    nsc.activation(absx[:, h, :], (M0, M2)[h][:, 0:T], ACT.Abs, bias=db[:, h:h + 1])
                    nsc.activation(relx[:, h, :], (M0, M2)[h][:, 0:T], ACT.Relu, bias=db[:, h:h + 1])\
                       .then_inc(f_abs, 1)
                sc.wait_ge(f_abs, 2 * g + 2)
                nsc.activation(expx[:, :, :], absx[:, :, :], ACT.Exp, scale=-1.0).then_inc(f_exp, 1)
                sc.wait_ge(f_exp, g + 1)
                nsc.activation(onex[:, :, :], expx[:, :, :], ACT.Identity, bias=1.0)
                nsc.activation(lnx[:, :, :], expx[:, :, :], ACT.Ln, bias=1.0).then_inc(f_ln1, 1)

            def square(g, cen_done, sq_done, src, dst, var_done):
                sc.wait_ge(cen_done, g + 1)
                if not (isinstance(g, int) and g < 1):
                    sc.wait_ge(var_done, g)
                nsc.activation(dst, src, ACT.Square).then_inc(sq_done, 1)

            def rsqrt(g, stat, st_sem, ln_sem, rsq_sem):
                sc.wait_ge(st_sem, 5 * g + 1)
                nsc.activation(stat[:, 1, :], stat[:, 0, :], ACT.Ln).then_inc(ln_sem, 1)
                sc.wait_ge(ln_sem, g + 1)
                nsc.activation(stat[:, 2, :], stat[:, 1, :], ACT.Exp, scale=-0.5).then_inc(rsq_sem, 1)

            def rows_copy(g, k):
                sc.wait_ge(b_tr, g + 1)
                if not (isinstance(g, int) and g < 2):
                    sc.wait_ge(b_out[k], ((g - k) // 2) * 16 if isinstance(g, int) else (g - k) * 8)
                nsc.activation(rows[k][:, :], M1[0:CP, :], ACT.Copy).then_inc(b_rows, 1)

            def logits(g):
                sc.wait_ge(b_lps, g + 1)
                dst = Lg[:, g, :] if isinstance(g, int) else Lg[:, ds(g, 1), :].rearrange("p a e -> p (a e)")
                nsc.activation(dst, M1[0:CP, 0:E], ACT.Copy).then_inc(b_log, 1)

            sc.wait_ge(s_setup, SETUP + 1)
            for h in range(HALF):
                nsc.activation(u[1][:, h, 0:1], M0[:, h:h + 1], ACT.Silu, bias=cb[:, h:h + 1])\
                   .then_inc(s_setup, 1)
            sc.wait_ge(s_setup, SETUP + 4)
            nsc.activation(S[1][:, 0:1], M0[0:3 * BC, 4:5], ACT.Copy)
            nsc.activation(dtr[:, 0:1], M0[0:RANK, 8:9], ACT.Copy).then_inc(s_setup, 1)
            sc.wait_ge(s_setup, SETUP + 6)
            nsc.activation(S[1][0:2 * BC, 0:1], Rm[:, 0:1], ACT.Copy).then_inc(s_setup, 1)
            sc.wait_ge(s_setup, SETUP + 9)
            for h in range(HALF):
                nsc.activation(absx[:, h, 0:1], M0[:, 12 + h:13 + h], ACT.Abs, bias=db[:, h:h + 1])
                nsc.activation(relx[:, h, 0:1], M0[:, 12 + h:13 + h], ACT.Relu, bias=db[:, h:h + 1])\
                   .then_inc(s_setup, 1)
            sc.wait_ge(s_setup, SETUP + 11)
            nsc.activation(expx[:, :, 0:1], absx[:, :, 0:1], ACT.Exp, scale=-1.0).then_inc(s_setup, 1)
            sc.wait_ge(s_setup, SETUP + 12)
            nsc.activation(onex[:, :, 0:1], expx[:, :, 0:1], ACT.Identity, bias=1.0)
            nsc.activation(lnx[:, :, 0:1], expx[:, :, 0:1], ACT.Ln, bias=1.0).then_inc(s_setup, 1)
            sc.wait_ge(s_setup, TOKEN_DONE)

            square(0, f_cen, f_sq, cen, sq, f_var)
            rsqrt(0, st, f_st, f_ln, f_rsq)
            silu_u(0, 0)
            bc_hi(0, 0)
            bc_mid(0, 0)
            softplus_head(0)

            def back_piece(n, g, k):
                if n == 7:
                    square(g, b_cen, b_sq, cen2, sq2, b_var)
                if n == 10:
                    rsqrt(g, st2, b_st, b_ln, b_rsq)
                if n == 13:
                    rows_copy(g, k)
                if n == 15:
                    logits(g)

            def batch(b, first, last):
                for j in range(JC):
                    g, k = b * JC + j, j % 2
                    front = not (last and j == JC - 1)
                    for n in range(NS):
                        i = NS * g + n
                        m = (NS * j + n) % 3
                        if n == 0:
                            sc.wait_ge(f_dt, g + 1)
                        if not (first and j == 0 and n < 3):
                            sc.wait_ge(m_h, i - 2)
                        for h in range(HALF):
                            a = nsc.activation(dA[m][:, h, :], dt[k][:, h, :], ACT.Exp, scale=An[:, h, n:n + 1])
                        a.then_inc(m_dA, 1)
                        sc.wait_ge(m_C, i + 1)
                        if not (first and j == 0 and n < 2):
                            sc.wait_ge(m_hC, i - 1)
                        nsc.activation(Cs[n % 2], Cb[:, 0:T], ACT.Copy).then_inc(m_Cs, 1)
                        if front:
                            if n == 4:
                                square(g + 1, f_cen, f_sq, cen, sq, f_var)
                            if n == 6:
                                rsqrt(g + 1, st, f_st, f_ln, f_rsq)
                            if n == 9:
                                silu_u(g + 1, 1 - k)
                            if n == 11:
                                bc_hi(g + 1, 1 - k)
                            if n == 12:
                                bc_mid(g + 1, 1 - k)
                            if n == 13:
                                softplus_head(g + 1)
                        if not (first and j == 0):
                            back_piece(n, g - 1, 1 - k)
            batches(sc, batch)
            for n in range(NS):
                back_piece(n, NCH - 1, 1)

            sc.wait_ge(r_ch, 2)
            nsc.activation(rt[1], rt[0], ACT.Exp).then_inc(r_exp, 1)

            def xT_copy(t, k):
                sc.wait_ge(t_xps, t + 1)
                nsc.activation(xT[k].rearrange("p r t -> p (r t)"), bank[4][:, :], ACT.Copy).then_inc(t_xT, 1)

            def silu(t, q):
                sc.wait_ge(t_h, 2 * t + q + 1)
                if not (isinstance(t, int) and t == 0):
                    sc.wait_ge(t_act, 2 * t + q - 1)
                nsc.activation(sil[q], bank[q][:, :], ACT.Silu).then_inc(t_silu, 1)

            def y_copy(t, k):
                sc.wait_ge(t_yps, t + 1)
                if not (isinstance(t, int) and t < 2):
                    sc.wait_ge(t_out[k], (t - k) * 8)
                nsc.activation(yout[k], bank[7][:, :], ACT.Copy).then_inc(t_y, 1)

            def tile(t, k, behind, ahead):
                silu(t, 0)
                silu(t, 1)
                if behind:
                    y_copy(t - 1, 1 - k)
                if ahead:
                    xT_copy(t + 1, 1 - k)
            sc.wait_ge(s_setup, TOKEN_DONE)
            xT_copy(0, 0)
            tile(0, 0, False, True)
            tile(1, 1, True, True)
            tile(2, 0, True, True)
            with sc.Fori(1, (NT - 3) // 2) as t2:
                tile(2 * t2 + 1, 1, True, True)
                tile(2 * t2 + 2, 0, True, True)
            tile(NT - 2, 1, True, True)
            tile(NT - 1, 0, True, False)
            y_copy(NT - 1, 0)

        @block.vector
        def _(v):
            nv = nc.vector
            v.wait_ge(s_setup, 1)
            nv.tensor_scalar(An[:, :, :], An[:, :, :], -1.0, None, ALU.mult).then_inc(s_setup, 1)
            step = 2
            for h in range(HALF):
                for tap in range(TAPS):
                    v.wait_ge(s_setup, step)
                    nv.tensor_scalar(wsc, in_raw[:, h, :], cw[:, h, tap:tap + 1], None, ALU.mult)\
                      .then_inc(s_setup, 1)
                    step += 2
                    v.wait_ge(s_setup, step)
                    nv.tensor_copy(Wu[:, h, tap, :], M0[:, 0:P]).then_inc(s_setup, 1)
                    step += 1
            for dst, src in [
                    *[(Wz[:, h, :], M0[:, 0:P]) for h in range(HALF)],
                    *[(Wx[:, h, :], M0[:, 0:3 * BC]) for h in range(HALF)],
                    *[(Wr[:, h, :], M0[:, 0:RANK]) for h in range(HALF)],
                    *[(Wd[:, h, :], M0[0:RANK, 0:P]) for h in range(HALF)],
                    *[(Wo[:, h, :], M0[:, 0:P]) for h in range(HALF)],
                    *[(gT[:, r, :], M0[:, 0:E]) for r in range(RR)]]:
                step += 1
                v.wait_ge(s_setup, step)
                nv.tensor_copy(dst, src).then_inc(s_setup, 1)
                step += 1
            assert step == SETUP, (step, SETUP)
            v.wait_ge(s_setup, SETUP + 5)
            nv.tensor_tensor(Rm[:, 0:1], M0[0:2 * BC, 4:5], S[1][0:2 * BC, 0:1], ALU.subtract).then_inc(s_setup, 1)
            v.wait_ge(s_setup, SETUP + 7)
            nv.tensor_tensor(S[1][0:BC, 0:1], Rm[0:BC, 0:1], S[1][0:BC, 0:1], ALU.subtract).then_inc(s_setup, 1)
            v.wait_ge(s_setup, SETUP + 13)
            nv.scalar_tensor_tensor(out=onex[:, :, 0], in0=onex[:, :, 0], scalar=-1.0, in1=expx[:, :, 0],
                                    op0=ALU.add, op1=ALU.subtract).then_inc(s_setup, 1)
            v.wait_ge(s_setup, SETUP + 14)
            nv.tensor_tensor(lnx[:, :, 0], lnx[:, :, 0], onex[:, :, 0], ALU.subtract).then_inc(s_setup, 1)
            v.wait_ge(s_setup, SETUP + 15)
            nv.tensor_tensor(lnx[:, :, 0], lnx[:, :, 0], relx[:, :, 0], ALU.add).then_inc(s_setup, 1)
            v.wait_ge(s_setup, SETUP + 16)
            nv.tensor_tensor(lnx[:, :, 0], lnx[:, :, 0], u[1][:, :, 0], ALU.mult).then_inc(s_setup, 1)
            v.wait_ge(s_setup, SETUP + 18)
            for h in range(HALF):
                last = nv.tensor_scalar(h0[:, :, h], M0[:, 16:16 + NS], lnx[:, h, 0:1], None, ALU.mult)
            last.then_inc(s_setup, 1)

            def newton(g, stat, rsq_sem, st_sem, used):
                v.wait_ge(rsq_sem, g + 1)
                if not (isinstance(g, int) and g < 1):
                    v.wait_ge(used, g)
                nv.tensor_tensor(stat[:, 3, :], stat[:, 2, :], stat[:, 2, :], ALU.mult).then_inc(st_sem, 1)
                v.wait_ge(st_sem, 5 * g + 2)
                nv.tensor_tensor(stat[:, 3, :], stat[:, 3, :], stat[:, 0, :], ALU.mult).then_inc(st_sem, 1)
                v.wait_ge(st_sem, 5 * g + 3)
                nv.tensor_scalar(stat[:, 3, :], stat[:, 3, :], -0.5, 1.5, ALU.mult, ALU.add).then_inc(st_sem, 1)
                v.wait_ge(st_sem, 5 * g + 4)
                nv.tensor_tensor(stat[:, 3, :], stat[:, 3, :], stat[:, 2, :], ALU.mult).then_inc(st_sem, 1)
                v.wait_ge(st_sem, 5 * g + 5)

            def centre(g, b, j, mean_sem, done, dst, ps):
                v.wait_ge(mean_sem, g + 1)
                nv.tensor_tensor(dst, xchunk(b, j), ps[:, 0:CP].unsqueeze(1).to_broadcast([P, RR, CP]),
                                 ALU.subtract).then_inc(done, 1)

            def front_piece(n, g, b, j, k):
                if n == 1:
                    if not (isinstance(g, int) and g < 1):
                        v.wait_ge(f_seq, g)
                    centre(g, b, j, f_mean, f_cen, cen, M0)
                if n == 3:
                    v.wait_ge(f_var, g + 1)
                    if not (isinstance(g, int) and g < 1):
                        v.wait_ge(f_st, 5 * g)
                    nv.tensor_scalar(st[:, 0, :], M0[:, P:P + CP], EPS_C, None, ALU.add).then_inc(f_st, 1)
                if n == 5:
                    newton(g, st, f_rsq, f_st, f_seq)
                    if not (isinstance(g, int) and g < 2):
                        v.wait_ge(f_zps, 2 * (g - 1))
                        v.wait_ge(f_hist, g)
                    sview = seq[k][:, HIST:].rearrange("p (h a w e) -> p a e h w", h=HC, a=R, w=W)
                    cview = cen.rearrange("p (a e) (h w) -> p a e h w", a=R, h=HC)
                    rview = st[:, 3, :].rearrange("p (h w) -> p h w", h=HC).unsqueeze(1).to_broadcast([P, R, HC, W])
                    for a in range(R):
                        last = nv.tensor_tensor(sview[:, a], cview[:, a], rview, ALU.mult)
                    last.then_inc(f_seq, 1)
                if n == 9:
                    v.wait_ge(f_hi, g + 1)
                    if not (isinstance(g, int) and g < 1):
                        v.wait_ge(f_mid, g)
                        v.wait_ge(f_lo, g)
                    nv.tensor_tensor(Rm[:, :], M0[0:2 * BC, 0:T], S[k][0:2 * BC, :], ALU.subtract).then_inc(f_res, 1)
                if n == 10:
                    v.wait_ge(f_mid, g + 1)
                    nv.tensor_tensor(S[k][0:BC, :], Rm[0:BC, :], S[k][0:BC, :], ALU.subtract).then_inc(f_lo, 1)
                if n == 12:
                    v.wait_ge(f_ln1, g + 1)
                    nv.scalar_tensor_tensor(out=onex[:, :, :], in0=onex[:, :, :], scalar=-1.0, in1=expx[:, :, :],
                                            op0=ALU.add, op1=ALU.subtract).then_inc(f_nd, 1)

            def back_piece(n, g, b, j, k):
                if n == 1:
                    v.wait_ge(m_y, NS * (g + 1))
                    if not (isinstance(g, int) and g < 1):
                        v.wait_ge(b_ops, g)
                    for h in range(HALF):
                        last = nv.scalar_tensor_tensor(out=yd[:, h, :], in0=u[k][:, h, :], scalar=Dk[:, h:h + 1],
                                                       in1=Yb[h][:, 0:T], op0=ALU.mult, op1=ALU.add)
                    last.then_inc(b_yd, 1)
                    v.wait_ge(b_yd, g + 1)
                    v.wait_ge(f_z, 2 * g + 2)
                    nv.tensor_tensor(yd[:, :, :], yd[:, :, :], z[k][:, :, :], ALU.mult).then_inc(b_ydz, 1)
                if n == 3:
                    v.wait_ge(b_ops, g + 1)
                    ov = M1[:, 0:T].rearrange("p (h a w e) -> p a e h w", h=HC, a=R, w=W)
                    for a in range(R):
                        xv = X[:, ds(b * RR + a * R, R), j * CP:(j + 1) * CP].rearrange("p e (h w) -> p e h w", h=HC)
                        last = nv.tensor_tensor(xv, xv, ov[:, a], ALU.add)
                    last.then_inc(b_x, 1)
                if n == 4:
                    if not (isinstance(g, int) and g < 1):
                        v.wait_ge(b_lps, g)
                    centre(g, b, j, b_mean, b_cen, cen2, M1)
                if n == 7:
                    v.wait_ge(b_var, g + 1)
                    if not (isinstance(g, int) and g < 1):
                        v.wait_ge(b_st, 5 * g)
                    nv.tensor_scalar(st2[:, 0, :], M1[:, P:P + CP], EPS_T, None, ALU.add).then_inc(b_st, 1)
                if n == 9:
                    newton(g, st2, b_rsq, b_st, b_xn)
                    nv.tensor_tensor(cen2, cen2, st2[:, 3, :].unsqueeze(1).to_broadcast([P, RR, CP]),
                                     ALU.mult).then_inc(b_xn, 1)

            v.wait_ge(s_setup, TOKEN_DONE)
            v.wait_ge(s_x, 16 * B)
            for n in range(NS):
                front_piece(n, 0, 0, 0, 0)

            def batch(b, first, last):
                for j in range(JC):
                    g, k = b * JC + j, j % 2
                    front = not (last and j == JC - 1)

                    def times_B(n):
                        i = NS * g + n
                        v.wait_ge(m_B, i + 1)
                        if n == 0:
                            v.wait_ge(f_dtu, g + 1)
                        if not (first and j == 0 and n < 3):
                            v.wait_ge(m_h, i - 2)
                        nv.tensor_tensor(dBu[(NS * j + n) % 3], dtu[k][:, :, :],
                                         Bb[n % 2][:, 0:T].unsqueeze(1).to_broadcast([P, HALF, T]),
                                         ALU.mult).then_inc(m_dBu, 1)
                    times_B(0)
                    for n in range(NS):
                        i = NS * g + n
                        m = (NS * j + n) % 3
                        if n < NS - 1:
                            times_B(n + 1)
                        v.wait_ge(m_dBu, i + 1)
                        v.wait_ge(m_dA, i + 1)
                        if not (first and j == 0 and n < 3):
                            v.wait_ge(m_hC, i - 2)
                            v.wait_ge(m_carry, i - 2)
                        if j > 0:
                            v.wait_ge(m_carry, NS * (g - 1) + n + 1)
                        for h in range(HALF):
                            init = (h0 if j == 0 else carry)[:, n, h:h + 1]
                            last_scan = nv.tensor_tensor_scan(hs[m][:, h, :], dA[m][:, h, :], dBu[m][:, h, :],
                                                              init, ALU.mult, ALU.add)
                        last_scan.then_inc(m_h, 1)
                        if not (first and j == 0):
                            back_piece(n, g - 1, b if j else b - 1, (j - 1) % JC, 1 - k)
                        if front:
                            front_piece(n, g + 1, b if j < JC - 1 else b + 1, (j + 1) % JC, 1 - k)
            batches(v, batch)
            for n in range(NS):
                back_piece(n, NCH - 1, B - 1, JC - 1, 1)

            step = [0]

            def link(ins):
                step[0] += 1
                ins.then_inc(r_ch, 1)
                v.wait_ge(r_ch, step[0])
            v.wait_ge(b_log, NCH)
            Lv = Lg[:, :, :]
            ge = "p (g e) -> p g e"
            q0, q1, q2, q3, q4, q5 = rt

            def g3(t):
                return t.rearrange(ge, e=E)

            def wide(t):
                return t.unsqueeze(2).to_broadcast([CP, NCH, E])
            mx = small[:, 0, 0:NCH]
            link(nv.reduce_max(mx, Lv, AX.X))
            link(nv.tensor_tensor(g3(q0), Lv, wide(mx), ALU.subtract))
            v.wait_ge(r_exp, 1)
            link(nv.reduce_sum(mx, g3(q1), AX.X))
            link(nv.reciprocal(mx, mx))
            link(nv.tensor_tensor(g3(q1), g3(q1), wide(mx), ALU.mult))
            c4 = cmp3.rearrange("p (g e f) -> p g e f", e=E, f=E)
            rank = q2
            for e in range(E):
                s_e = g3(q1)[:, :, e:e + 1].to_broadcast([CP, NCH, E])
                link(nv.tensor_tensor(c4[:, :, e, :], g3(q1), s_e, ALU.is_gt))
            link(nv.reduce_sum(g3(q2), c4, AX.X))
            for e in range(E):
                s_e = g3(q1)[:, :, e:e + 1].to_broadcast([CP, NCH, E])
                link(nv.tensor_tensor(c4[:, :, e, :], g3(q1), s_e, ALU.is_equal))
                link(nv.tensor_tensor(c4[:, :, e, :], c4[:, :, e, :],
                                      low[:, e, :].unsqueeze(1).to_broadcast([CP, NCH, E]), ALU.mult))
            link(nv.reduce_sum(g3(q3), c4, AX.X))
            link(nv.tensor_tensor(q2, q2, q3, ALU.add))
            link(nv.tensor_scalar(q3, q2, 1.0, None, ALU.is_le))
            for s in range(2):
                link(nv.tensor_scalar(q4, q2, float(s), None, ALU.is_equal))
                link(nv.tensor_tensor(q4, q4, q1, ALU.mult))
                link(nv.reduce_sum(wgt[:, s, :], g3(q4), AX.X))
            link(nv.tensor_tensor(mx, wgt[:, 0, :], wgt[:, 1, :], ALU.add))
            link(nv.tensor_scalar(mx, mx, 1e-20, None, ALU.add))
            link(nv.reciprocal(mx, mx))
            for s in range(2):
                link(nv.tensor_tensor(wgt[:, s, :], wgt[:, s, :], mx, ALU.mult))
            v.wait_ge(r_ps, 1)
            eg = "p (e g) -> p e g"
            tot = M2[0:CP, 0:NCH * E].rearrange("p (g e) -> p e g", e=E)
            link(nv.memset(q4, 1.0))
            link(nv.memset(q4.rearrange(eg, e=E)[:, :, 0:1], 0.0))
            link(nv.tensor_copy(q0.rearrange(eg, e=E), tot))
            link(nv.tensor_tensor_scan(q5, q4, q0, 0.0, ALU.mult, ALU.add))
            cnt = q5.rearrange(eg, e=E)[:, :, NCH - 1]
            link(nv.tensor_scalar(smalli[:, :], cnt, float(P - 1), None, ALU.add))
            link(nv.tensor_scalar(smalli[:, :], smalli[:, :], P.bit_length() - 1, None, ALU.logical_shift_right))
            til, end, base, one8 = (small[:, a, 0:E] for a in range(1, 5))
            link(nv.tensor_copy(til, smalli[:, :]))
            link(nv.memset(one8, 1.0))
            link(nv.tensor_tensor_scan(end, one8, til, 0.0, ALU.mult, ALU.add))
            link(nv.tensor_tensor(base, end, til, ALU.subtract))
            link(nv.tensor_scalar(base, base, float(P), float(SHT * P), ALU.mult, ALU.add))
            link(nv.tensor_tensor(q5, q5, q0, ALU.subtract))
            link(nv.tensor_tensor(q5.rearrange(eg, e=E), q5.rearrange(eg, e=E),
                                  base.unsqueeze(2).to_broadcast([CP, E, NCH]), ALU.add))
            link(nv.tensor_tensor(g3(q0), q5.rearrange("p (e g) -> p g e", e=E),
                                  M0[0:CP, 0:NCH * E].rearrange(ge, e=E), ALU.add))
            for s in range(2):
                link(nv.tensor_scalar(q4, q2, float(s), None, ALU.is_equal))
                link(nv.tensor_tensor(q4, q4, q0, ALU.mult))
                link(nv.reduce_sum(mx, g3(q4), AX.X))
                link(nv.tensor_copy(dsti[:, s, :], mx))
            link(nv.tensor_scalar(endt[:, :], end[0:1, :], float(SHT), None, ALU.add))
            tf, et = small[:, 5, 0:RTT], small[:, 6, 0:RTT]
            link(nv.tensor_copy(tf, tileno[:, :]))
            c2 = cmp3[:, 0:RTT * E].rearrange("p (t e) -> p t e", e=E)
            link(nv.tensor_tensor(c2, end.unsqueeze(1).to_broadcast([CP, RTT, E]),
                                  tf.unsqueeze(2).to_broadcast([CP, RTT, E]), ALU.is_le))
            link(nv.reduce_sum(et, c2, AX.X))
            link(nv.memset(tset[:, 0:SHT], 0))
            link(nv.tensor_scalar(tset[:, SHT:NT], et[0:1, :], float(E - 1), 1.0, ALU.min, ALU.add))
            link(nv.tensor_scalar(twait[:, :], tset[:, :], 48.0, 48.0, ALU.mult, ALU.add))
            link(nv.tensor_scalar(toff[:, :], tset[:, :], 1, None, ALU.bitwise_and))
            link(nv.tensor_scalar(toff[:, :], toff[:, :], float(SETW), None, ALU.mult))
            nv.memset(small[:, 7, :], 0.0).then_inc(r_done, 1)

            def gate(t, q):
                v.wait_ge(t_silu, 2 * t + q + 1)
                if not (isinstance(t, int) and t == 0):
                    v.wait_ge(t_aps, 2 * t + q - 1)
                nv.tensor_tensor(act[q], sil[q], bank[2 + q][:, :], ALU.mult).then_inc(t_act, 1)

            def actT_copy(t, q):
                v.wait_ge(t_aps, 2 * t + q + 1)
                if not (isinstance(t, int) and t == 0):
                    v.wait_ge(t_yps, t)
                nv.tensor_copy(actT[q].rearrange("p k t -> p (k t)"), bank[5 + q][:, :]).then_inc(t_aT, 1)

            def tile(t):
                gate(t, 0)
                gate(t, 1)
                actT_copy(t, 0)
                actT_copy(t, 1)
            tile(0)
            with v.Fori(1, NT) as t:
                tile(t)

            def add_sum(b, j):
                g, k = b * JC + j, j % 2
                v.wait_ge(c_ps, g + 1)
                xv = xchunk(b, j)
                nv.tensor_tensor(xv, xv, bank[k][:, 0:T].rearrange("p (r q) -> p r q", r=RR),
                                 ALU.add).then_inc(c_x, 1)
            def combine(b):
                for j in range(JC):
                    g, k = b * JC + j, j % 2
                    g2 = b * (JC // 2) + j // 2
                    v.wait_ge(c_g[k], 32 * g2 + 32)
                    v.wait_ge(c_sh[k], 16 * g2 + 16)
                    if started(b) or j > 1:
                        v.wait_ge(c_ps, g if j == 0 else g - 1)
                    w0s = wgt[:, 0, ds(g, 1)]
                    w1s = wgt[:, 1, ds(g, 1)]
                    nv.scalar_tensor_tensor(out=ysh[k], in0=y0[k], scalar=w0s, in1=ysh[k],
                                            op0=ALU.mult, op1=ALU.add).then_inc(c_a, 1)
                    v.wait_ge(c_a, g + 1)
                    nv.scalar_tensor_tensor(out=ysum[k], in0=y1[k], scalar=w1s, in1=ysh[k],
                                            op0=ALU.mult, op1=ALU.add).then_inc(c_s, 1)
                    if j:
                        add_sum(b, j - 1)
                add_sum(b, JC - 1)
            peeled(v, B, combine)

        @block.tensor
        def _(pe):
            te = nc.tensor
            mm = te.matmul
            pe.wait_ge(s_const, NCONST)
            pe.wait_ge(s_in, 16 * 14)
            step = 2
            for h in range(HALF):
                for tap in range(TAPS):
                    step += 1
                    pe.wait_ge(s_setup, step)
                    te.transpose(M0[:, 0:P], wsc, ident[:, :]).then_inc(s_setup, 1)
                    step += 2
            for dst, src, idn in [
                    *[(M0[:, 0:P], in_raw[:, HALF + h, :], ident[:, :]) for h in range(HALF)],
                    *[(M0[:, 0:3 * BC], xp_raw[:, h * P:(h + 1) * P], ident[0:3 * BC, 0:3 * BC]) for h in range(HALF)],
                    *[(M0[:, 0:RANK], xr_raw[:, h * P:(h + 1) * P], ident[0:RANK, 0:RANK]) for h in range(HALF)],
                    *[(M0[0:RANK, 0:P], dp_raw[:, h, :], ident[:, :]) for h in range(HALF)],
                    *[(M0[:, 0:P], ow_raw[:, h * P:(h + 1) * P], ident[:, :]) for h in range(HALF)],
                    *[(M0[:, 0:E], gw_raw[:, r::RR], ident[0:E, 0:E]) for r in range(RR)]]:
                pe.wait_ge(s_setup, step)
                te.transpose(dst, src, idn).then_inc(s_setup, 1)
                step += 2
            assert step == SETUP, (step, SETUP)
            pe.wait_ge(s_setup, SETUP)
            for h in range(HALF):
                last = mm(M0[:, h:h + 1], Wu[:, h, TAPS - 1, :], tokh[:, HIST - 1:HIST], start=True, stop=True)
            last.then_inc(s_setup, 1)
            pe.wait_ge(s_setup, SETUP + 3)
            for h in range(HALF):
                mm(M0[0:3 * BC, 4:5], Wx[:, h, :], u[1][:, h, 0:1], start=(h == 0), stop=(h == HALF - 1))
            for h in range(HALF):
                last = mm(M0[0:RANK, 8:9], Wr[:, h, :], u[1][:, h, 0:1], start=(h == 0), stop=(h == HALF - 1))
            last.then_inc(s_setup, 1)
            pe.wait_ge(s_setup, SETUP + 8)
            for h in range(HALF):
                last = mm(M0[:, 12 + h:13 + h], Wd[:, h, :], dtr[:, 0:1], start=True, stop=True)
            last.then_inc(s_setup, 1)
            pe.wait_ge(s_setup, SETUP + 17)
            for n in range(NS):
                last = mm(M0[:, 16 + n:17 + n], sel[:, n, :], S[1][:, 0:1], start=True, stop=True)
            last.then_inc(s_setup, 1)

            def front_piece(n, g, b, j, k):
                if n == 0:
                    if not (isinstance(g, int) and g < 1):
                        pe.wait_ge(f_abs, 2 * g)
                    for r in range(RR):
                        xv = xchunk(b, j)[:, r, :]
                        last = mm(M0[:, 0:CP], meanw[:, :], xv, start=(r == 0), stop=(r == RR - 1))
                    last.then_inc(f_mean, 1)
                if n == 4:
                    pe.wait_ge(f_sq, g + 1)
                    for r in range(RR):
                        last = mm(M0[:, P:P + CP], meanw[:, :], sq[:, r, :], start=(r == 0), stop=(r == RR - 1))
                    last.then_inc(f_var, 1)
                if n in (7, 8):
                    h = n - 7
                    if h == 0:
                        pe.wait_ge(f_seq, g + 1)
                        pe.wait_ge(f_hist, g + 1)
                    for tap in range(TAPS):
                        last = mm((M0, M2)[h][:, 0:T], Wu[:, h, tap, :], seq[k][:, tap:tap + T],
                                  start=(tap == 0), stop=(tap == TAPS - 1))
                    last.then_inc(f_ups, 1)
                if n == 9:
                    for h in range(HALF):
                        pe.wait_ge(f_u, 2 * g + h + 1)
                        mm((M0, M2)[h][:, 0:T], Wz[:, h, :], seq[k][:, HIST:HIST + T], start=True, stop=True)\
                            .then_inc(f_zps, 1)
                if n == 10:
                    pe.wait_ge(f_z, 2 * g + 2)
                    for h in range(HALF):
                        last = mm(M0[0:3 * BC, 0:T], Wx[:, h, :], u[k][:, h, :], start=(h == 0), stop=(h == HALF - 1))
                    last.then_inc(f_bcps, 1)
                    for h in range(HALF):
                        last = mm(M2[0:RANK, 0:T], Wr[:, h, :], u[k][:, h, :], start=(h == 0), stop=(h == HALF - 1))
                    last.then_inc(f_rps, 1)
                if n == 12:
                    pe.wait_ge(f_rank, g + 1)
                    pe.wait_ge(f_res, g + 1)
                    for h in range(HALF):
                        mm((M0, M2)[h][:, 0:T], Wd[:, h, :], dtr[:, :], start=True, stop=True).then_inc(f_dtps, 1)

            def back_piece(n, g, b, j):
                if n == 3:
                    pe.wait_ge(b_ydz, g + 1)
                    if not (isinstance(g, int) and g < 1):
                        pe.wait_ge(b_log, g)
                    for h in range(HALF):
                        last = mm(M1[:, 0:T], Wo[:, h, :], yd[:, h, :], start=(h == 0), stop=(h == HALF - 1))
                    last.then_inc(b_ops, 1)
                if n == 5:
                    pe.wait_ge(b_x, g + 1)
                    for r in range(RR):
                        last = mm(M1[:, 0:CP], meanw[:, :], xchunk(b, j)[:, r, :], start=(r == 0), stop=(r == RR - 1))
                    last.then_inc(b_mean, 1)
                if n == 7:
                    pe.wait_ge(b_sq, g + 1)
                    for r in range(RR):
                        last = mm(M1[:, P:P + CP], meanw[:, :], sq2[:, r, :], start=(r == 0), stop=(r == RR - 1))
                    last.then_inc(b_var, 1)
                if n == 11:
                    pe.wait_ge(b_xn, g + 1)
                    for r in range(RR):
                        last = te.transpose(M1[0:CP, r * P:(r + 1) * P], cen2[:, r, :], ident[:, :])
                    last.then_inc(b_tr, 1)
                if n == 13:
                    pe.wait_ge(b_rows, g + 1)
                    for r in range(RR):
                        last = mm(M1[0:CP, 0:E], cen2[:, r, :], gT[:, r, :], start=(r == 0), stop=(r == RR - 1))
                    last.then_inc(b_lps, 1)

            pe.wait_ge(s_setup, TOKEN_DONE)
            pe.wait_ge(s_x, 16 * B)
            for n in range(NS):
                front_piece(n, 0, 0, 0, 0)

            def batch(b, first, last):
                for j in range(JC):
                    g, k = b * JC + j, j % 2
                    front = not (last and j == JC - 1)

                    def spread(n):
                        i = NS * g + n
                        if n == 0:
                            pe.wait_ge(f_lo, g + 1)
                        if not (first and j == 0 and n < 2):
                            pe.wait_ge(m_dBu, i - 1)
                        mm(Bb[n % 2][:, 0:T], sel[:, n, :], S[k][:, :], start=True, stop=True).then_inc(m_B, 1)
                        if not (first and j == 0 and n < 1):
                            pe.wait_ge(m_Cs, i)
                        mm(Cb[:, 0:T], sel[:, NS + n, :], S[k][:, :], start=True, stop=True).then_inc(m_C, 1)

                    def add_y(n):
                        i = NS * g + n
                        pe.wait_ge(m_hC, i + 1)
                        if n == 0 and not (first and j == 0):
                            pe.wait_ge(b_yd, g)
                        for h in range(HALF):
                            last_mm = mm(Yb[h][:, 0:T], ident[:, :], hC[(NS * j + n) % 3][:, h, :],
                                         start=(n == 0), stop=(n == NS - 1))
                        last_mm.then_inc(m_y, 1)
                    spread(0)
                    for n in range(NS):
                        if n < NS - 1:
                            spread(n + 1)
                        if n >= 2:
                            add_y(n - 2)
                        if not (first and j == 0):
                            back_piece(n, g - 1, b if j else b - 1, (j - 1) % JC)
                        if front:
                            front_piece(n, g + 1, b if j < JC - 1 else b + 1, (j + 1) % JC, 1 - k)
                    add_y(NS - 2)
                    add_y(NS - 1)
            batches(pe, batch)
            for n in range(NS):
                back_piece(n, NCH - 1, B - 1, JC - 1)

            pe.wait_ge(r_ch, R_CHOSEN)
            mm(M0[0:CP, 0:NCH * E], tri[:, :], rt[3], start=True, stop=True)
            mm(M2[0:CP, 0:NCH * E], one96[:, :], rt[3], start=True, stop=True).then_inc(r_ps, 1)

            pe.wait_ge(r_done, 1)

            def x_transpose(t, k):
                pe.wait_ge(t_x[k], (t - k) * 8 + 16)
                if not (isinstance(t, int) and t == 0):
                    pe.wait_ge(t_xT, t)
                for r in range(RR):
                    last = te.transpose(bank[4][:, r * P:(r + 1) * P], xin[k][:, r * P:(r + 1) * P], ident[:, :])
                last.then_inc(t_xps, 1)

            def set_of(t):
                return pe.value_load(toff[0:1, ds(t, 1)], min_val=0, max_val=SETW)

            def up(t, k):
                loaded = pe.value_load(twait[0:1, ds(t, 1)], min_val=48, max_val=48 * (E + 1))
                off = set_of(t)
                pe.wait_ge(s_w, loaded)
                pe.wait_ge(t_xT, t + 1)
                for q in range(2):
                    if not (isinstance(t, int) and t == 0):
                        pe.wait_ge(t_act, 2 * t + q - 1)
                    for w in range(2):
                        for r in range(RR):
                            last = mm(bank[2 * w + q][:, :], xT[k][:, r, :],
                                      WALL[:, ds(off + (w * RR * I + r * I + q * 512), 512)],
                                      start=(r == 0), stop=(r == RR - 1))
                    last.then_inc(t_h, 1)

            def down(t):
                off = set_of(t)
                for q in range(2):
                    pe.wait_ge(t_aT, 2 * t + q + 1)
                if not (isinstance(t, int) and t == 0):
                    pe.wait_ge(t_y, t)
                for c in range(IK):
                    last = mm(bank[7][:, :], actT[c // 4][:, c % 4, :],
                              WALL[:, ds(off + (2 * RR * I + c * C), C)],
                              start=(c == 0), stop=(c == IK - 1))
                last.then_inc(t_yps, 1)

            def act_transpose(t):
                for q in range(2):
                    pe.wait_ge(t_act, 2 * t + q + 1)
                    if not (isinstance(t, int) and t == 0):
                        pe.wait_ge(t_aT, 2 * t + q - 1)
                    for c in range(4):
                        last = te.transpose(bank[5 + q][:, c * P:(c + 1) * P], act[q][:, c * P:(c + 1) * P],
                                            ident[:, :])
                    last.then_inc(t_aps, 1)

            def tile(t, k, behind, ahead):
                up(t, k)
                if ahead:
                    x_transpose(t + 1, 1 - k)
                if behind:
                    down(t - 1)
                act_transpose(t)
            x_transpose(0, 0)
            tile(0, 0, False, True)
            with pe.Fori(0, (NT - 3) // 2) as t2:
                tile(2 * t2 + 1, 1, True, True)
                tile(2 * t2 + 2, 0, True, True)
            tile(NT - 2, 1, True, True)
            tile(NT - 1, 0, True, False)
            down(NT - 1)

            def transpose_sums(b):
                for j in range(JC):
                    g, k = b * JC + j, j % 2
                    pe.wait_ge(c_s, g + 1)
                    if started(b) or j > 1:
                        pe.wait_ge(c_x, g if j == 0 else g - 1)
                    for r in range(RR):
                        last = te.transpose(bank[k][:, r * CP:(r + 1) * CP], ysum[k][:, r::RR], ident[0:CP, 0:CP])
                    last.then_inc(c_ps, 1)
            peeled(pe, B, transpose_sums)


_INS = ['x', 'L0_conv_global_token', 'L0_conv_in_proj_w', 'L0_conv_conv_w', 'L0_conv_conv_b', 'L0_conv_x_proj_w',
        'L0_conv_dt_proj_w', 'L0_conv_dt_proj_b', 'L0_conv_A_log', 'L0_conv_D', 'L0_conv_out_proj_w',
        'L0_ffn_gate_w', 'L0_ffn_w1', 'L0_ffn_w2', 'L0_ffn_w3', 'L0_ffn_sw1', 'L0_ffn_sw2', 'L0_ffn_sw3']


def kernel(**inputs):
    import numpy as _np
    import concourse.bacc as _bacc
    from concourse import mybir as _mybir
    from concourse.bass_utils import run_bass_kernel_spmd as _run

    nc = _bacc.Bacc("TRN2", target_bir_lowering=False, num_devices=1)
    arrays, args = {}, []
    for name in _INS:
        a = _np.ascontiguousarray(inputs[name])
        arrays[f"in_{name}_dram"] = a
        args.append(nc.dram_tensor(f"in_{name}_dram", a.shape, _mybir.dt.from_np(a.dtype), kind="ExternalInput").ap())
    shape = inputs['x'].shape
    args.append(nc.dram_tensor("out_0_dram", shape, _mybir.dt.float32, kind="ExternalOutput").ap())
    bass_metaformer_mamba_moe_kernel(nc, *args)
    r = _run(nc, [arrays], core_ids=[0])
    return r.results[0]["out_0_dram"]
```

```python
import concourse.bass as bass
from concourse import mybir
from contextlib import ExitStack


def bass_metaformer_mamba_moe_kernel(nc, x, token, in_w, conv_w, conv_b, xp_w, dtp_w, dtp_b,
                                     A_log, D_skip, out_w, gate_w, w1, w2, w3, sw1, sw2, sw3, out):
    fp32, bf16, i32 = mybir.dt.float32, mybir.dt.bfloat16, mybir.dt.int32
    ALU, ACT, AX = mybir.AluOpType, mybir.ActivationFunctionType, mybir.AxisListType
    ds = bass.ds

    P = 128
    B, C, H, W = x.shape
    R = 2
    RR = R * R
    PIX = H * W
    HALF = in_w.shape[0] // 2 // P
    NS = A_log.shape[1]
    RANK = dtp_w.shape[1]
    TAPS = conv_w.shape[1]
    HIST = TAPS - 1
    JC = 6
    HC = H // JC
    CP = HC * W
    T = CP * RR
    NCH = B * JC
    BC = 2 * NS
    E = gate_w.shape[0]
    I = w1.shape[2]
    IK = I // P
    TOK = B * PIX
    SHT = TOK // P
    RTT = (2 * TOK + E * (P - 1)) // P
    NT = SHT + RTT
    SETW = 3 * I * RR
    SCAN0 = 2 * I * RR
    EPS_C, EPS_T = 1e-6, 1e-5
    RING = 4
    RK = 3 * BC
    SETUP = 7
    TOKEN_DONE = SETUP + 19
    R_CHOSEN = 33

    xrows = nc.dram_tensor("xrows", (NT * P, C), fp32, kind="Internal").ap()
    yrows = nc.dram_tensor("yrows", (NT * P, C), fp32, kind="Internal").ap()

    ctx = ExitStack()
    with ctx:
        def sb(name, shape, dt=fp32):
            return ctx.enter_context(nc.sbuf_tensor(name, shape, dt))

        def sem(name):
            return ctx.enter_context(nc.semaphore(name))

        X = sb("X", [P, B * RR, PIX])
        WALL = sb("WALL", [P, 2 * SETW])
        WS0, WS1 = WALL[:, 0:SETW], WALL[:, SETW:2 * SETW]
        ident = sb("ident", [P, P])
        meanw = sb("meanw", [P, P])
        Lg = sb("Lg", [CP, NCH, E])
        gT = sb("gT", [P, RR, E])
        dsti = sb("dsti", [CP, 2, NCH], i32)
        wgt = sb("wgt", [CP, 2, NCH])
        tset = sb("tset", [1, NT], i32)
        toff = sb("toff", [1, NT], i32)
        twait = sb("twait", [1, NT], i32)
        endt = sb("endt", [1, E], i32)

        at = [0]

        def part(n):
            v = WALL[:, SCAN0 + at[0]:SCAN0 + at[0] + n]
            at[0] += n
            assert SCAN0 + at[0] <= 2 * SETW
            return v

        def halves():
            return part(HALF * T).rearrange("p (h t) -> p h t", h=HALF)
        dA = [halves() for _ in range(RING)]
        dBu = [halves() for _ in range(3)]
        hs = [halves() for _ in range(RING)]
        hC = [halves() for _ in range(RING)]
        Cs = [part(T) for _ in range(RING)]
        yd = halves()
        cen, sq, cen2, sq2 = (part(T).rearrange("p (r q) -> p r q", r=RR) for _ in range(4))
        u2 = sb("u2", [P, 2, HALF * T])
        u = [u2[:, k, :].rearrange("p (h t) -> p h t", h=HALF) for k in range(2)]
        z = [sb(f"z{k}", [P, HALF, T]) for k in range(2)]
        dt = [sb(f"dt{k}", [P, HALF, T]) for k in range(2)]
        dtu = [sb(f"dtu{k}", [P, HALF, T]) for k in range(2)]
        seq = [sb(f"seq{k}", [P, HIST + T]) for k in range(2)]
        S = [sb(f"S{k}", [3 * BC, T], bf16) for k in range(2)]
        Rm = sb("Rm", [2 * BC, T])
        dtr = sb("dtr", [RANK, T])
        absx = sb("absx", [P, HALF, T])
        relx = sb("relx", [P, HALF, T])
        expx = sb("expx", [P, HALF, T])
        lnx = sb("lnx", [P, HALF, T])
        onex = sb("onex", [P, HALF, T])
        st = sb("st", [P, 4, CP])
        st2 = sb("st2", [P, 4, CP])
        rows = [sb(f"rows{k}", [CP, C]) for k in range(2)]
        carry = sb("carry", [P, NS, HALF])
        h0 = sb("h0", [P, NS, HALF])
        tokh = sb("tokh", [P, HIST])
        sel = sb("sel", [3 * BC, BC, P], bf16)
        Wu = sb("Wu", [P, HALF, TAPS, P])
        Wz = sb("Wz", [P, HALF, P])
        Wx = sb("Wx", [P, HALF, RK + RANK])
        Wd = sb("Wd", [RANK, HALF, P])
        Wo = sb("Wo", [P, HALF, P])
        cb = sb("cb", [P, HALF])
        db = sb("db", [P, HALF])
        Dk = sb("Dk", [P, HALF])
        An = sb("An", [P, HALF, NS])
        def raw(t, lo, n, parts=P):
            return t.rearrange("p h t -> p (h t)")[0:parts, lo:lo + n]
        in_raw = raw(dA[0], 0, 512).rearrange("p (k d) -> p k d", k=4)
        wsc = [raw(dA[1 + h], 0, TAPS * P).rearrange("p (k d) -> p k d", k=TAPS) for h in range(HALF)]
        cw = raw(dA[3], 0, HALF * TAPS).rearrange("p (h k) -> p h k", h=HALF)
        xp_raw = raw(dBu[0], 0, 256, RK + RANK)
        dp_raw = raw(dBu[1], 0, HALF * RANK).rearrange("p (h k) -> p h k", h=HALF)
        ow_raw = raw(dBu[1], 16, 256)
        gw_raw = raw(dBu[2], 0, 512, E)
        al_raw = raw(hs[0], 0, HALF * NS).rearrange("p (h k) -> p h k", h=HALF)

        zrow = sb("zrow", [P, P])

        bank = [ctx.enter_context(nc.psum_tensor(f"bank{k}", [P, 512], fp32)) for k in range(8)]
        Yb = [bank[0], bank[1]]
        Bb = [bank[2], bank[3]]
        Cb = bank[4]
        M0, M2, M1 = bank[5], bank[6], bank[7]

        s_in = sem("inputs_loaded")
        s_const = sem("constants_made")
        s_setup = sem("setup_step")
        s_passed = sem("pool_passed_its_waits")
        s_zero = sem("zero_rows_written")
        s_x0, s_x = sem("x_of_image_0_loaded"), sem("x_loaded")
        s_w = sem("expert_weights_loaded")
        f_mean, f_cen, f_sq, f_var, f_ln, f_rsq = (sem("f_" + n) for n in
                                                   "mean centred squared var ln rsqrt".split())
        f_st = sem("f_stat_step")
        f_seq = sem("f_seq_written")
        f_hist = sem("f_hist_copied")
        f_ups, f_zps = sem("f_u_in_psum"), sem("f_z_in_psum")
        f_u, f_z = sem("f_u_silu"), sem("f_z_silu")
        f_bcps, f_dtps = sem("f_bc_in_psum"), sem("f_dt_in_psum")
        f_hi, f_res, f_mid, f_lo = (sem("f_bc_" + n) for n in "hi residue mid lo".split())
        f_rank = sem("f_rank_copied")
        f_abs = sem("f_abs_relu")
        f_exp = sem("f_exp")
        f_ln1 = sem("f_ln1p")
        f_nd = sem("f_rounding_of_1p")
        f_dt1 = sem("f_dt_small")
        f_dt, f_dtu = sem("f_dt"), sem("f_dtu")
        m_B, m_C = sem("m_B_in_psum"), sem("m_C_in_psum")
        m_dA, m_Cs = sem("m_dA"), sem("m_C_copied")
        m_dBu, m_h = sem("m_dBu"), sem("m_h_scanned")
        m_hC, m_carry = sem("m_hC"), sem("m_carry")
        m_y = sem("m_y_added")
        b_yd, b_ydz, b_ops, b_x = (sem("b_" + n) for n in "y_read gated out_in_psum residual".split())
        b_mean, b_cen, b_sq, b_var, b_ln, b_rsq = (sem("b_" + n) for n in
                                                   "mean centred squared var ln rsqrt".split())
        b_st = sem("b_stat_step")
        b_xn = sem("b_normalised")
        b_tr, b_rows, b_lps, b_log = (sem("b_" + n) for n in
                                      "transposed rows_copied logits_in_psum logits".split())
        b_out = [sem("b_rows_stored0"), sem("b_rows_stored1")]
        r_ch = sem("routing_step")
        r_exp = sem("r_exp")
        r_ps = sem("r_counts_in_psum")
        r_cp = sem("r_counts_copied")
        r_done = sem("routed")
        r_ld = [sem("r_rows_loaded0"), sem("r_rows_loaded1")]
        r_ix = sem("r_index_copied")
        r_sc = [sem("r_scattered0"), sem("r_scattered1")]
        t_x = [sem("t_x_loaded0"), sem("t_x_loaded1")]
        t_xps, t_xT = sem("t_x_transposed"), sem("t_xT_copied")
        t_h, t_silu, t_act = sem("t_h_in_psum"), sem("t_silu"), sem("t_act")
        t_aps, t_aT = sem("t_act_transposed"), sem("t_actT_copied")
        t_yps, t_y = sem("t_y_in_psum"), sem("t_y_copied")
        t_out = [sem("t_y_stored0"), sem("t_y_stored1")]
        c_sh = [sem("c_shared_loaded0"), sem("c_shared_loaded1")]
        c_ix = sem("c_index_copied")
        c_g = [sem("c_gathered0"), sem("c_gathered1")]
        c_a, c_s = sem("c_first_added"), sem("c_summed")
        c_ps, c_x = sem("c_transposed"), sem("c_added")
        c_out = sem("c_out_stored")

        def flat(t):
            return t[:, :, :].rearrange("p h t -> p (h t)")
        xin = [flat(u[k])[:, 0:C] for k in range(2)]
        xT = [flat(z[k])[:, 0:C].rearrange("p (r t) -> p r t", r=RR) for k in range(2)]
        sil = [flat(dt[k])[:, 0:512] for k in range(2)]
        act = [flat(dtu[k])[:, 0:512] for k in range(2)]
        actT = [flat(absx)[:, 0:512].rearrange("p (k t) -> p k t", k=4),
                flat(relx)[:, 0:512].rearrange("p (k t) -> p k t", k=4)]
        yout = [flat(expx)[:, 0:512], flat(lnx)[:, 0:512]]
        ysh = [flat(u[k])[0:CP, 0:C] for k in range(2)]
        y0 = [flat(z[k])[0:CP, 0:C] for k in range(2)]
        y1 = [flat(dt[k])[0:CP, 0:C] for k in range(2)]
        ysum = [flat(dtu[k])[0:CP, 0:C] for k in range(2)]
        ixc = sb("ixc", [CP, 2, 2], i32)
        rt = [WS1[0:CP, k * NCH * E:(k + 1) * NCH * E] for k in range(6)]
        cmp3 = WS1[0:CP, 2048:2048 + NCH * E * E]
        tri = sb("tri", [CP, CP])
        one96 = sb("one96", [CP, CP])
        low = sb("low", [CP, E, E])
        tileno = sb("tileno", [CP, RTT], i32)
        small = WS1[0:CP, 4096:4096 + 8 * RTT].rearrange("p (a t) -> p a t", a=8)
        smalli = sb("smalli", [CP, E], i32)

        NLOAD = [0]
        NCONST = 9

        def weights_of(q, ws):
            a, b3, b2 = (sw1[0], sw3[0], sw2[0]) if q == 0 else (w1[q - 1], w3[q - 1], w2[q - 1])
            return ((ws[:, 0:4096].rearrange("p (r i) -> p r i", r=RR), a.rearrange("(c r) i -> c r i", r=RR)),
                    (ws[:, 4096:8192].rearrange("p (r i) -> p r i", r=RR), b3.rearrange("(c r) i -> c r i", r=RR)),
                    (ws[:, 8192:12288].rearrange("p (k n) -> p k n", k=IK), b2.rearrange("(k p) n -> p k n", p=P)))

        def peeled(eng, stop, body):
            body(0)
            with eng.Fori(1, stop) as i:
                body(i)

        def started(i):
            return not (isinstance(i, int) and i == 0)

        block = ctx.enter_context(nc.Block())

        def xchunk(b, j):
            return X[:, ds(b * RR, RR), j * CP:(j + 1) * CP] if not isinstance(b, int) else \
                X[:, b * RR:(b + 1) * RR, j * CP:(j + 1) * CP]

        def batches(eng, body):
            body(0, True, False)
            with eng.Fori(1, B - 1) as b:
                body(b, False, False)
            body(B - 1, False, True)

        @block.sync
        def _(sp):
            loads = [
                (in_raw, in_w.rearrange("(k e) d -> e k d", e=P)),
                (cw, conv_w.rearrange("(h p) k -> p h k", p=P)),
                (xp_raw[0:BC, :], xp_w[RANK:RANK + BC, :]),
                (xp_raw[BC:2 * BC, :], xp_w[RANK:RANK + BC, :]),
                (xp_raw[2 * BC:3 * BC, :], xp_w[RANK:RANK + BC, :]),
                (xp_raw[RK:RK + RANK, :], xp_w[0:RANK, :]),
                (dp_raw, dtp_w.rearrange("(h p) k -> p h k", p=P)),
                (ow_raw, out_w),
                (gw_raw, gate_w),
                (al_raw, A_log.rearrange("(h p) k -> p h k", p=P)),
                (cb[:, :], conv_b.rearrange("(h p) -> p h", p=P)),
                (db[:, :], dtp_b.rearrange("(h p) -> p h", p=P)),
                (Dk[:, :], D_skip.rearrange("(h p) -> p h", p=P)),
                (tokh[:, HIST - 1:HIST], token.rearrange("a b c -> c (a b)")),
            ]
            NLOAD[0] = 16 * len(loads)

            def load_x(b, done):
                sp.dma_start(X[:, b * RR:(b + 1) * RR, :].rearrange("p r q -> p (r q)"),
                             x[b].rearrange("(c r) h w -> c (r h w)", r=RR)).then_inc(done, 16)
            load_x(0, s_x0)
            with nc.allow_non_contiguous_dma(reason="a few vectors of 256 entries"):
                for dst, src in loads:
                    sp.dma_start(dst, src).then_inc(s_in, 16)
            for b in range(1, B):
                load_x(b, s_x)
            sp.wait_ge(s_const, NCONST)
            with sp.Fori(SHT, NT) as t:
                sp.dma_start(xrows[ds(t * P, P), :].rearrange("p (r c) -> p r c", r=RR),
                             zrow[:, :].unsqueeze(1).to_broadcast([P, RR, P])).then_inc(s_zero, 16)

            def batch(b, first, last):
                for j in range(JC):
                    g = b * JC + j
                    if first and j == 0:
                        continue
                    sp.wait_ge(b_rows, g)
                    sp.dma_start(xrows[ds((g - 1) * CP, CP), :], rows[(j + 1) % 2][:, :])\
                      .then_inc(b_out[(j + 1) % 2], 16)
            batches(sp, batch)
            sp.wait_ge(b_rows, NCH)
            sp.dma_start(xrows[(NCH - 1) * CP:NCH * CP, :], rows[1][:, :]).then_inc(b_out[1], 16)

            sp.wait_ge(b_out[0], 16 * (NCH // 2))
            sp.wait_ge(b_out[1], 16 * (NCH // 2))
            sp.wait_ge(b_yd, NCH)

            def load_tile(t, k):
                sp.dma_start(xin[k], xrows[ds(t * P, P), :]).then_inc(t_x[k], 16)

            def store_tile(t, k):
                sp.wait_ge(t_y, t + 1)
                sp.dma_start(yrows[ds(t * P, P), :], yout[k]).then_inc(t_out[k], 16)

            def two_tiles(t2):
                for k in range(2):
                    sp.wait_ge(t_xps, 2 * t2 + k + 1)
                    load_tile(2 * t2 + k + 2, k)
                    store_tile(2 * t2 + k, k)
            load_tile(0, 0)
            load_tile(1, 1)
            with sp.Fori(0, SHT // 2 - 1) as t2:
                two_tiles(t2)
            sp.wait_ge(r_sc[0], 32 * (NCH // 2))
            sp.wait_ge(r_sc[1], 32 * (NCH // 2))
            with sp.Fori(SHT // 2 - 1, (NT - 3) // 2) as t2:
                two_tiles(t2)
            sp.wait_ge(t_xps, NT - 2)
            load_tile(NT - 1, 0)
            for t in range(NT - 3, NT):
                store_tile(t, t % 2)

            sp.wait_ge(t_out[0], 16 * ((NT + 1) // 2))
            sp.wait_ge(t_out[1], 16 * (NT // 2))
            sp.wait_ge(t_y, NT)
            def load_shared(b):
                for j in range(JC):
                    g = b * JC + j
                    k = j % 2
                    if started(b) or j > 1:
                        sp.wait_ge(c_s, g if j == 0 else g - 1)
                    sp.dma_start(ysh[k], yrows[ds(g * CP, CP), :]).then_inc(c_sh[k], 16)
                sp.wait_ge(c_x, (b + 1) * JC)
                sp.dma_start(out[ds(b, 1), :, :, :].rearrange("a (c r) h w -> c (a r h w)", r=RR),
                             X[:, ds(b * RR, RR), :].rearrange("p r q -> p (r q)")).then_inc(c_out, 16)
            peeled(sp, B, load_shared)
            sp.wait_ge(c_out, 16 * B)

        @block.gpsimd
        def _(pool):
            pool.memset(ident[:, :], 0.0).then_inc(s_const, 1)
            pool.memset(meanw[:, :], 1.0 / C).then_inc(s_const, 1)
            pool.memset(sel[:, :, :], 0.0).then_inc(s_const, 1)
            pool.memset(tri[:, :], 1.0)
            pool.memset(one96[:, :], 1.0)
            pool.memset(low[:, :, :], 1.0)
            pool.memset(tokh[:, 0:HIST - 1], 0.0)
            pool.memset(zrow[:, :], 0.0).then_inc(s_const, 1)
            pool.wait_ge(s_const, 4)
            pool.affine_select(out=ident[:, :], in_=ident[:, :], compare_op=ALU.not_equal, fill=1.0,
                               base=0, pattern=[[-1, P]], channel_multiplier=1).then_inc(s_const, 1)
            pool.affine_select(out=tri[:, :], in_=tri[:, :], compare_op=ALU.is_gt, fill=0.0,
                               base=0, pattern=[[1, CP]], channel_multiplier=-1)
            pool.affine_select(out=low[:, :, :], in_=low[:, :, :], compare_op=ALU.is_gt, fill=0.0,
                               base=0, pattern=[[1, E], [-1, E]], channel_multiplier=0)
            pool.iota(tileno[:, :], pattern=[[1, RTT]], base=0, channel_multiplier=0)
            for q in range(3):
                if q:
                    pool.wait_ge(s_const, 5 + q)
                pool.affine_select(out=sel[:, :, :], in_=sel[:, :, :], compare_op=ALU.not_equal, fill=1.0,
                                   base=-BC * q, pattern=[[-1, BC], [0, P]], channel_multiplier=1)\
                    .then_inc(s_const, 1)
            pool.memset(carry[:, :, :], 0.0).then_inc(s_const, 1)

            def on_a_count():
                pool.sem_inc(s_passed, 1)

            def softplus_tail(n, g, k):
                if n == 11:
                    pool.wait_ge(f_ln1, g + 1)
                    pool.wait_ge(f_nd, g + 1)
                    if not (isinstance(g, int) and g < 2):
                        pool.wait_ge(m_dA, NS * (g - 1))
                        pool.wait_ge(m_dBu, NS * (g - 1))
                    pool.tensor_tensor(dt[k][:, :, :], lnx[:, :, :], onex[:, :, :], ALU.subtract).then_inc(f_dt1, 1)
                if n == 12:
                    pool.wait_ge(f_dt1, g + 1)
                    pool.tensor_tensor(dt[k][:, :, :], dt[k][:, :, :], relx[:, :, :], ALU.add).then_inc(f_dt, 1)
                if n == 13:
                    pool.wait_ge(f_dt, g + 1)
                    pool.wait_ge(f_u, 2 * g + 2)
                    pool.tensor_tensor(dtu[k][:, :, :], dt[k][:, :, :], u[k][:, :, :], ALU.mult).then_inc(f_dtu, 1)

            def history(g, k, start):
                if not (isinstance(g, int) and g < 2):
                    pool.wait_ge(f_zps, 2 * (g - 1))
                if start:
                    on_a_count()
                    pool.tensor_copy(seq[k][:, 0:HIST], tokh[:, :]).then_inc(f_hist, 1)
                else:
                    pool.wait_ge(f_seq, g)
                    on_a_count()
                    pool.tensor_copy(seq[k][:, 0:HIST], seq[1 - k][:, T:T + HIST]).then_inc(f_hist, 1)

            for dst, src in weights_of(0, WS0)[0:2]:
                pool.dma_start(dst, src).then_inc(s_w, 16)
            pool.wait_ge(s_in, 16 * 14)
            history(0, 0, True)
            history(1, 1, False)
            for n in range(NS):
                softplus_tail(n, 0, 0)

            def batch(b, first, last):
                for j in range(JC):
                    g, k = b * JC + j, j % 2
                    front = not (last and j == JC - 1)
                    front1 = not (last and j >= JC - 2)
                    for n in range(NS):
                        i = NS * g + n
                        m = n % RING
                        if front1 and n == 9:
                            history(g + 2, k, j == JC - 2)
                        pool.wait_ge(m_h, i + 1)
                        pool.wait_ge(m_Cs, i + 1)
                        if not (first and j == 0 and n < RING):
                            pool.wait_ge(m_y, i - RING + 1)
                        pool.tensor_tensor(hC[m], hs[m], Cs[m].unsqueeze(1).to_broadcast([P, HALF, T]),
                                           ALU.mult).then_inc(m_hC, 1)
                        pool.tensor_copy(carry[:, n, :], hs[m][:, :, T - 1]).then_inc(m_carry, 1)
                        if front:
                            softplus_tail(n, g + 1, 1 - k)
            batches(pool, batch)

            pool.wait_ge(b_x, NCH)
            pool.wait_ge(b_lps, NCH)
            pool.wait_ge(m_carry, NS * NCH)
            pool.wait_ge(m_y, NS * NCH)
            pool.wait_ge(s_w, 32)
            dst, src = weights_of(0, WS0)[2]
            pool.dma_start(dst, src).then_inc(s_w, 16)

            def load_rows(g, k):
                pool.dma_start(rows[k][:, :], xrows[ds(g * CP, CP), :]).then_inc(r_ld[k], 16)
            pool.wait_ge(b_out[0], 16 * (NCH // 2))
            pool.wait_ge(b_out[1], 16 * (NCH // 2))
            load_rows(0, 0)
            load_rows(1, 1)

            pool.wait_ge(r_done, 1)
            pool.wait_ge(s_zero, 16 * RTT)
            pool.wait_ge(s_w, 48)
            for dst, src in weights_of(1, WS1):
                pool.dma_start(dst, src).then_inc(s_w, 16)

            def scatter(g2):
                for k in range(2):
                    if started(g2):
                        pool.wait_ge(r_sc[k], 32 * g2)
                        on_a_count()
                        load_rows(2 * g2 + k, k)
                    pool.tensor_copy(ixc[:, :, k], dsti[:, :, ds(2 * g2 + k, 1)].rearrange("p s g -> p (s g)"))\
                        .then_inc(r_ix, 1)
                    pool.wait_ge(r_ix, 2 * g2 + k + 1)
                    pool.wait_ge(r_ld[k], 16 * g2 + 16)
                    on_a_count()
                    for s in range(2):
                        pool.indirect_dma_start(
                            out=xrows, out_offset=bass.IndirectOffsetOnAxis(ap=ixc[:, s, k:k + 1], axis=0),
                            in_=rows[k][:, :], in_offset=None).then_inc(r_sc[k], 16)
            peeled(pool, NCH // 2, scatter)

            for q in range(2, E + 1):
                if q == 2:
                    pool.wait_ge(t_yps, SHT)
                else:
                    pool.wait_ge(t_yps, pool.value_load(endt[0:1, q - 3:q - 2], min_val=SHT, max_val=NT))
                pool.wait_ge(s_w, 48 * q)
                on_a_count()
                for dst, src in weights_of(q, (WS0, WS1)[q % 2]):
                    pool.dma_start(dst, src).then_inc(s_w, 16)

            pool.wait_ge(t_out[0], 16 * ((NT + 1) // 2))
            pool.wait_ge(t_out[1], 16 * (NT // 2))
            pool.wait_ge(r_sc[0], 32 * (NCH // 2))
            pool.wait_ge(r_sc[1], 32 * (NCH // 2))
            pool.wait_ge(t_act, 2 * NT)
            def gather(g2):
                for k in range(2):
                    if started(g2):
                        pool.wait_ge(c_g[k], 32 * g2)
                        pool.wait_ge(c_s, 2 * g2)
                    on_a_count()
                    pool.tensor_copy(ixc[:, :, k], dsti[:, :, ds(2 * g2 + k, 1)].rearrange("p s g -> p (s g)"))\
                        .then_inc(c_ix, 1)
                    pool.wait_ge(c_ix, 2 * g2 + k + 1)
                    on_a_count()
                    for s, dst in enumerate((y0, y1)):
                        pool.indirect_dma_start(
                            out=dst[k], out_offset=None, in_=yrows,
                            in_offset=bass.IndirectOffsetOnAxis(ap=ixc[:, s, k:k + 1], axis=0)).then_inc(c_g[k], 16)
            peeled(pool, NCH // 2, gather)

        @block.scalar
        def _(sc):
            nsc = nc.scalar
            sc.wait_ge(s_in, 16 * 14)
            nsc.activation(An[:, :, :], al_raw, ACT.Exp).then_inc(s_setup, 1)

            def silu_uz(g, k):
                for h in range(HALF):
                    sc.wait_ge(f_ups, 2 * g + h + 1)
                    if h == 0 and not (isinstance(g, int) and g < 2):
                        sc.wait_ge(b_yd, g - 1)
                        sc.wait_ge(f_dtu, g - 1)
                        sc.wait_ge(b_ydz, g - 1)
                    nsc.activation(u[k][:, h, :], (M0, M2)[h][:, 0:T], ACT.Silu, bias=cb[:, h:h + 1])\
                       .then_inc(f_u, 1)
                for h in range(HALF):
                    sc.wait_ge(f_zps, 2 * g + h + 1)
                    nsc.activation(z[k][:, h, :], (M0, M2)[h][:, 0:T], ACT.Silu).then_inc(f_z, 1)

            def bc_hi(g, k):
                sc.wait_ge(f_bcps, g + 1)
                if not (isinstance(g, int) and g < 2):
                    sc.wait_ge(m_B, NS * (g - 1))
                    sc.wait_ge(m_C, NS * (g - 1))
                nsc.activation(S[k][:, :], M0[0:3 * BC, 0:T], ACT.Copy).then_inc(f_hi, 1)
                if not (isinstance(g, int) and g < 1):
                    sc.wait_ge(f_dtps, 2 * g)
                nsc.activation(dtr[:, :], M0[RK:RK + RANK, 0:T], ACT.Copy).then_inc(f_rank, 1)

            def bc_mid(g, k):
                sc.wait_ge(f_res, g + 1)
                nsc.activation(S[k][0:2 * BC, :], Rm[:, :], ACT.Copy).then_inc(f_mid, 1)

            def softplus_head(g):
                if not (isinstance(g, int) and g < 1):
                    sc.wait_ge(f_nd, g)
                    sc.wait_ge(f_dt, g)
                for h in range(HALF):
                    sc.wait_ge(f_dtps, 2 * g + h + 1)
                    nsc.activation(absx[:, h, :], (M0, M2)[h][:, 0:T], ACT.Abs, bias=db[:, h:h + 1])
                    nsc.activation(relx[:, h, :], (M0, M2)[h][:, 0:T], ACT.Relu, bias=db[:, h:h + 1])\
                       .then_inc(f_abs, 1)
                sc.wait_ge(f_abs, 2 * g + 2)
                nsc.activation(expx[:, :, :], absx[:, :, :], ACT.Exp, scale=-1.0).then_inc(f_exp, 1)
                sc.wait_ge(f_exp, g + 1)
                nsc.activation(onex[:, :, :], expx[:, :, :], ACT.Identity, bias=1.0)
                nsc.activation(lnx[:, :, :], expx[:, :, :], ACT.Ln, bias=1.0).then_inc(f_ln1, 1)

            def square(g, cen_done, sq_done, src, dst, var_done):
                sc.wait_ge(cen_done, g + 1)
                if not (isinstance(g, int) and g < 1):
                    sc.wait_ge(var_done, g)
                nsc.activation(dst, src, ACT.Square).then_inc(sq_done, 1)

            def rsqrt(g, stat, st_sem, ln_sem, rsq_sem):
                sc.wait_ge(st_sem, 5 * g + 1)
                nsc.activation(stat[:, 1, :], stat[:, 0, :], ACT.Ln).then_inc(ln_sem, 1)
                sc.wait_ge(ln_sem, g + 1)
                nsc.activation(stat[:, 2, :], stat[:, 1, :], ACT.Exp, scale=-0.5).then_inc(rsq_sem, 1)

            def rows_copy(g, k):
                sc.wait_ge(b_tr, g + 1)
                if not (isinstance(g, int) and g < 2):
                    sc.wait_ge(b_out[k], ((g - k) // 2) * 16 if isinstance(g, int) else (g - k) * 8)
                nsc.activation(rows[k][:, :], M1[0:CP, :], ACT.Copy).then_inc(b_rows, 1)

            def logits(g):
                sc.wait_ge(b_lps, g + 1)
                dst = Lg[:, g, :] if isinstance(g, int) else Lg[:, ds(g, 1), :].rearrange("p a e -> p (a e)")
                nsc.activation(dst, M1[0:CP, 0:E], ACT.Copy).then_inc(b_log, 1)

            sc.wait_ge(s_setup, SETUP + 1)
            for h in range(HALF):
                nsc.activation(u[1][:, h, 0:1], M0[:, h:h + 1], ACT.Silu, bias=cb[:, h:h + 1])\
                   .then_inc(s_setup, 1)
            sc.wait_ge(s_setup, SETUP + 4)
            nsc.activation(S[1][:, 0:1], M0[0:3 * BC, 4:5], ACT.Copy)
            nsc.activation(dtr[:, 0:1], M0[RK:RK + RANK, 4:5], ACT.Copy).then_inc(s_setup, 1)
            sc.wait_ge(s_setup, SETUP + 6)
            nsc.activation(S[1][0:2 * BC, 0:1], Rm[:, 0:1], ACT.Copy).then_inc(s_setup, 1)
            sc.wait_ge(s_setup, SETUP + 9)
            for h in range(HALF):
                nsc.activation(absx[:, h, 0:1], M0[:, 12 + h:13 + h], ACT.Abs, bias=db[:, h:h + 1])
                nsc.activation(relx[:, h, 0:1], M0[:, 12 + h:13 + h], ACT.Relu, bias=db[:, h:h + 1])\
                   .then_inc(s_setup, 1)
            sc.wait_ge(s_setup, SETUP + 11)
            nsc.activation(expx[:, :, 0:1], absx[:, :, 0:1], ACT.Exp, scale=-1.0).then_inc(s_setup, 1)
            sc.wait_ge(s_setup, SETUP + 12)
            nsc.activation(onex[:, :, 0:1], expx[:, :, 0:1], ACT.Identity, bias=1.0)
            nsc.activation(lnx[:, :, 0:1], expx[:, :, 0:1], ACT.Ln, bias=1.0).then_inc(s_setup, 1)
            sc.wait_ge(s_setup, TOKEN_DONE)

            square(0, f_cen, f_sq, cen, sq, f_var)
            rsqrt(0, st, f_st, f_ln, f_rsq)
            square(1, f_cen, f_sq, cen, sq, f_var)
            rsqrt(1, st, f_st, f_ln, f_rsq)
            silu_uz(0, 0)
            bc_hi(0, 0)
            bc_mid(0, 0)
            softplus_head(0)

            def back_piece(n, g, k):
                if n == 9:
                    square(g, b_cen, b_sq, cen2, sq2, b_var)
                if n == 11:
                    rsqrt(g, st2, b_st, b_ln, b_rsq)
                if n == 14:
                    rows_copy(g, k)
                if n == 15:
                    logits(g)

            def batch(b, first, last):
                for j in range(JC):
                    g, k = b * JC + j, j % 2
                    front = not (last and j == JC - 1)
                    front1 = not (last and j >= JC - 2)
                    for n in range(NS):
                        i = NS * g + n
                        m = n % RING
                        if n == 0:
                            sc.wait_ge(f_dt, g + 1)
                        if not (first and j == 0 and n < RING):
                            sc.wait_ge(m_h, i - RING + 1)
                        for h in range(HALF):
                            a = nsc.activation(dA[m][:, h, :], dt[k][:, h, :], ACT.Exp, scale=An[:, h, n:n + 1])
                        a.then_inc(m_dA, 1)
                        sc.wait_ge(m_C, i + 1)
                        if not (first and j == 0 and n < RING):
                            sc.wait_ge(m_hC, i - RING + 1)
                        nsc.activation(Cs[m], Cb[:, 0:T], ACT.Copy).then_inc(m_Cs, 1)
                        if front:
                            if n == 4:
                                silu_uz(g + 1, 1 - k)
                            if n == 7:
                                bc_hi(g + 1, 1 - k)
                            if n == 9:
                                bc_mid(g + 1, 1 - k)
                            if n == 10:
                                softplus_head(g + 1)
                        if front1:
                            if n == 13:
                                square(g + 2, f_cen, f_sq, cen, sq, f_var)
                            if n == 15:
                                rsqrt(g + 2, st, f_st, f_ln, f_rsq)
                        if not (first and j == 0):
                            back_piece(n, g - 1, 1 - k)
            batches(sc, batch)
            for n in range(NS):
                back_piece(n, NCH - 1, 1)

            sc.wait_ge(r_ch, 2)
            nsc.activation(rt[1], rt[0], ACT.Exp).then_inc(r_exp, 1)

            def xT_copy(t, k):
                sc.wait_ge(t_xps, t + 1)
                nsc.activation(xT[k].rearrange("p r t -> p (r t)"), bank[4][:, :], ACT.Copy).then_inc(t_xT, 1)

            def silu(t, q):
                sc.wait_ge(t_h, 2 * t + q + 1)
                if not (isinstance(t, int) and t == 0):
                    sc.wait_ge(t_act, 2 * t + q - 1)
                nsc.activation(sil[q], bank[q][:, :], ACT.Silu).then_inc(t_silu, 1)

            def y_copy(t, k):
                sc.wait_ge(t_yps, t + 1)
                if not (isinstance(t, int) and t < 2):
                    sc.wait_ge(t_out[k], (t - k) * 8)
                nsc.activation(yout[k], bank[7][:, :], ACT.Copy).then_inc(t_y, 1)

            def tile(t, k, behind, ahead):
                silu(t, 0)
                silu(t, 1)
                if behind:
                    y_copy(t - 1, 1 - k)
                if ahead:
                    xT_copy(t + 1, 1 - k)
            sc.wait_ge(s_setup, TOKEN_DONE)
            xT_copy(0, 0)
            tile(0, 0, False, True)
            tile(1, 1, True, True)
            tile(2, 0, True, True)
            with sc.Fori(1, (NT - 3) // 2) as t2:
                tile(2 * t2 + 1, 1, True, True)
                tile(2 * t2 + 2, 0, True, True)
            tile(NT - 2, 1, True, True)
            tile(NT - 1, 0, True, False)
            y_copy(NT - 1, 0)

        @block.vector
        def _(v):
            nv = nc.vector
            v.wait_ge(s_setup, 1)
            nv.tensor_scalar(An[:, :, :], An[:, :, :], -1.0, None, ALU.mult).then_inc(s_setup, 1)
            for h in range(HALF):
                for tap in range(TAPS):
                    last = nv.tensor_scalar(wsc[h][:, tap, :], in_raw[:, h, :], cw[:, h, tap:tap + 1], None, ALU.mult)
            last.then_inc(s_setup, 1)
            v.wait_ge(s_setup, 4)
            for h in range(HALF):
                nv.tensor_copy(Wu[:, h, :, :].rearrange("p k d -> p (k d)"), bank[h][:, :])
                nv.tensor_copy(Wz[:, h, :], bank[2][:, h * P:(h + 1) * P])
                nv.tensor_copy(Wo[:, h, :], bank[2][:, (2 + h) * P:(3 + h) * P])
                nv.tensor_copy(Wx[:, h, :], bank[3][:, h * P:h * P + RK + RANK])
                nv.tensor_copy(Wd[:, h, :], bank[4][0:RANK, h * P:(h + 1) * P])
            nv.tensor_copy(gT[:, :, :].rearrange("p r e -> p (r e)"), bank[3][:, 256:256 + RR * E])\
              .then_inc(s_setup, SETUP - 4)
            v.wait_ge(s_setup, SETUP + 5)
            nv.tensor_tensor(Rm[:, 0:1], M0[0:2 * BC, 4:5], S[1][0:2 * BC, 0:1], ALU.subtract).then_inc(s_setup, 1)
            v.wait_ge(s_setup, SETUP + 7)
            nv.tensor_tensor(S[1][0:BC, 0:1], Rm[0:BC, 0:1], S[1][0:BC, 0:1], ALU.subtract).then_inc(s_setup, 1)
            v.wait_ge(s_setup, SETUP + 13)
            nv.scalar_tensor_tensor(out=onex[:, :, 0], in0=onex[:, :, 0], scalar=-1.0, in1=expx[:, :, 0],
                                    op0=ALU.add, op1=ALU.subtract).then_inc(s_setup, 1)
            v.wait_ge(s_setup, SETUP + 14)
            nv.tensor_tensor(lnx[:, :, 0], lnx[:, :, 0], onex[:, :, 0], ALU.subtract).then_inc(s_setup, 1)
            v.wait_ge(s_setup, SETUP + 15)
            nv.tensor_tensor(lnx[:, :, 0], lnx[:, :, 0], relx[:, :, 0], ALU.add).then_inc(s_setup, 1)
            v.wait_ge(s_setup, SETUP + 16)
            nv.tensor_tensor(lnx[:, :, 0], lnx[:, :, 0], u[1][:, :, 0], ALU.mult).then_inc(s_setup, 1)
            v.wait_ge(s_setup, SETUP + 18)
            for h in range(HALF):
                last = nv.tensor_scalar(h0[:, :, h], M0[:, 16:16 + NS], lnx[:, h, 0:1], None, ALU.mult)
            last.then_inc(s_setup, 1)

            def newton(g, stat, rsq_sem, st_sem, used):
                v.wait_ge(rsq_sem, g + 1)
                if not (isinstance(g, int) and g < 1):
                    v.wait_ge(used, g)
                nv.tensor_tensor(stat[:, 3, :], stat[:, 2, :], stat[:, 2, :], ALU.mult).then_inc(st_sem, 1)
                v.wait_ge(st_sem, 5 * g + 2)
                nv.tensor_tensor(stat[:, 3, :], stat[:, 3, :], stat[:, 0, :], ALU.mult).then_inc(st_sem, 1)
                v.wait_ge(st_sem, 5 * g + 3)
                nv.tensor_scalar(stat[:, 3, :], stat[:, 3, :], -0.5, 1.5, ALU.mult, ALU.add).then_inc(st_sem, 1)
                v.wait_ge(st_sem, 5 * g + 4)
                nv.tensor_tensor(stat[:, 3, :], stat[:, 3, :], stat[:, 2, :], ALU.mult).then_inc(st_sem, 1)
                v.wait_ge(st_sem, 5 * g + 5)

            def centre(g, b, j, mean_sem, done, dst, ps):
                v.wait_ge(mean_sem, g + 1)
                nv.tensor_tensor(dst, xchunk(b, j), ps[:, 0:CP].unsqueeze(1).to_broadcast([P, RR, CP]),
                                 ALU.subtract).then_inc(done, 1)

            def front1_piece(n, g, b, j, k):
                if n == 10:
                    if not (isinstance(g, int) and g < 1):
                        v.wait_ge(f_seq, g)
                    centre(g, b, j, f_mean, f_cen, cen, M0)
                if n == 12:
                    v.wait_ge(f_var, g + 1)
                    if not (isinstance(g, int) and g < 1):
                        v.wait_ge(f_st, 5 * g)
                    nv.tensor_scalar(st[:, 0, :], M0[:, P:P + CP], EPS_C, None, ALU.add).then_inc(f_st, 1)
                if n == 14:
                    newton(g, st, f_rsq, f_st, f_seq)
                    if not (isinstance(g, int) and g < 2):
                        v.wait_ge(f_zps, 2 * (g - 1))
                        v.wait_ge(f_hist, g)
                    sview = seq[k][:, HIST:].rearrange("p (h a w e) -> p a e h w", h=HC, a=R, w=W)
                    cview = cen.rearrange("p (a e) (h w) -> p a e h w", a=R, h=HC)
                    rview = st[:, 3, :].rearrange("p (h w) -> p h w", h=HC).unsqueeze(1).to_broadcast([P, R, HC, W])
                    for a in range(R):
                        last = nv.tensor_tensor(sview[:, a], cview[:, a], rview, ALU.mult)
                    last.then_inc(f_seq, 1)

            def front2_piece(n, g, k):
                if n == 6:
                    v.wait_ge(f_hi, g + 1)
                    if not (isinstance(g, int) and g < 1):
                        v.wait_ge(f_mid, g)
                        v.wait_ge(f_lo, g)
                    nv.tensor_tensor(Rm[:, :], M0[0:2 * BC, 0:T], S[k][0:2 * BC, :], ALU.subtract).then_inc(f_res, 1)
                if n == 8:
                    v.wait_ge(f_mid, g + 1)
                    nv.tensor_tensor(S[k][0:BC, :], Rm[0:BC, :], S[k][0:BC, :], ALU.subtract).then_inc(f_lo, 1)
                if n == 9:
                    v.wait_ge(f_ln1, g + 1)
                    nv.scalar_tensor_tensor(out=onex[:, :, :], in0=onex[:, :, :], scalar=-1.0, in1=expx[:, :, :],
                                            op0=ALU.add, op1=ALU.subtract).then_inc(f_nd, 1)

            def back_piece(n, g, b, j, k):
                if n == 1:
                    v.wait_ge(m_y, NS * (g + 1))
                    if not (isinstance(g, int) and g < 1):
                        v.wait_ge(b_ops, g)
                    for h in range(HALF):
                        last = nv.scalar_tensor_tensor(out=yd[:, h, :], in0=u[k][:, h, :], scalar=Dk[:, h:h + 1],
                                                       in1=Yb[h][:, 0:T], op0=ALU.mult, op1=ALU.add)
                    last.then_inc(b_yd, 1)
                    v.wait_ge(b_yd, g + 1)
                    v.wait_ge(f_z, 2 * g + 2)
                    nv.tensor_tensor(yd[:, :, :], yd[:, :, :], z[k][:, :, :], ALU.mult).then_inc(b_ydz, 1)
                if n == 4:
                    v.wait_ge(b_ops, g + 1)
                    ov = M1[:, 0:T].rearrange("p (h a w e) -> p a e h w", h=HC, a=R, w=W)
                    for a in range(R):
                        xv = X[:, ds(b * RR + a * R, R), j * CP:(j + 1) * CP].rearrange("p e (h w) -> p e h w", h=HC)
                        last = nv.tensor_tensor(xv, xv, ov[:, a], ALU.add)
                    last.then_inc(b_x, 1)
                if n == 6:
                    if not (isinstance(g, int) and g < 1):
                        v.wait_ge(b_lps, g)
                    centre(g, b, j, b_mean, b_cen, cen2, M1)
                if n == 8:
                    v.wait_ge(b_var, g + 1)
                    if not (isinstance(g, int) and g < 1):
                        v.wait_ge(b_st, 5 * g)
                    nv.tensor_scalar(st2[:, 0, :], M1[:, P:P + CP], EPS_T, None, ALU.add).then_inc(b_st, 1)
                if n == 10:
                    newton(g, st2, b_rsq, b_st, b_xn)
                    nv.tensor_tensor(cen2, cen2, st2[:, 3, :].unsqueeze(1).to_broadcast([P, RR, CP]),
                                     ALU.mult).then_inc(b_xn, 1)

            v.wait_ge(s_setup, TOKEN_DONE)
            v.wait_ge(s_x0, 16)
            for g in range(2):
                for n in range(NS):
                    front1_piece(n, g, 0, g, g)
            for n in range(NS):
                front2_piece(n, 0, 0)
            v.wait_ge(s_x, 16 * (B - 1))

            def batch(b, first, last):
                for j in range(JC):
                    g, k = b * JC + j, j % 2
                    front = not (last and j == JC - 1)
                    front1 = not (last and j >= JC - 2)

                    def times_B(n):
                        i = NS * g + n
                        v.wait_ge(m_B, i + 1)
                        if n == 0:
                            v.wait_ge(f_dtu, g + 1)
                        if not (first and j == 0 and n < 3):
                            v.wait_ge(m_h, i - 2)
                        nv.tensor_tensor(dBu[(NS * j + n) % 3], dtu[k][:, :, :],
                                         Bb[n % 2][:, 0:T].unsqueeze(1).to_broadcast([P, HALF, T]),
                                         ALU.mult).then_inc(m_dBu, 1)
                    times_B(0)
                    for n in range(NS):
                        i = NS * g + n
                        m = n % RING
                        if n < NS - 1:
                            times_B(n + 1)
                        v.wait_ge(m_dBu, i + 1)
                        v.wait_ge(m_dA, i + 1)
                        if not (first and j == 0 and n < RING):
                            v.wait_ge(m_hC, i - RING + 1)
                            v.wait_ge(m_carry, i - RING + 1)
                        for h in range(HALF):
                            init = (h0 if j == 0 else carry)[:, n, h:h + 1]
                            last_scan = nv.tensor_tensor_scan(hs[m][:, h, :], dA[m][:, h, :], dBu[(NS * j + n) % 3][:, h, :],
                                                              init, ALU.mult, ALU.add)
                        last_scan.then_inc(m_h, 1)
                        if not (first and j == 0):
                            back_piece(n, g - 1, b if j else b - 1, (j - 1) % JC, 1 - k)
                        if front:
                            front2_piece(n, g + 1, 1 - k)
                        if front1:
                            front1_piece(n, g + 2, b if j < JC - 2 else b + 1, (j + 2) % JC, k)
            batches(v, batch)
            for n in range(NS):
                back_piece(n, NCH - 1, B - 1, JC - 1, 1)

            step = [0]

            def link(ins):
                step[0] += 1
                ins.then_inc(r_ch, 1)
                v.wait_ge(r_ch, step[0])
            v.wait_ge(b_log, NCH)
            v.wait_ge(m_carry, NS * NCH)
            Lv = Lg[:, :, :]
            ge, eg = "p (g e) -> p g e", "p (e g) -> p e g"
            q0, q1, q2, q3, q4, q5 = rt

            def g3(t):
                return t.rearrange(ge, e=E)

            def wide(t):
                return t.unsqueeze(2).to_broadcast([CP, NCH, E])
            mx = small[:, 0, 0:NCH]
            c4 = cmp3.rearrange("p (g e f) -> p g e f", e=E, f=E)
            til, end, base, one8 = (small[:, a, 0:E] for a in range(1, 5))

            def softmax_and_greater():
                link(nv.reduce_max(mx, Lv, AX.X))
                link(nv.tensor_tensor(g3(q0), Lv, wide(mx), ALU.subtract))
                v.wait_ge(r_exp, 1)
                link(nv.reduce_sum(mx, g3(q1), AX.X))
                link(nv.reciprocal(mx, mx))
                link(nv.tensor_tensor(g3(q1), g3(q1), wide(mx), ALU.mult))
                for e in range(E):
                    s_e = g3(q1)[:, :, e:e + 1].to_broadcast([CP, NCH, E])
                    link(nv.tensor_tensor(c4[:, :, e, :], g3(q1), s_e, ALU.is_gt))
                link(nv.reduce_sum(g3(q2), c4, AX.X))

            def choose():
                for e in range(E):
                    s_e = g3(q1)[:, :, e:e + 1].to_broadcast([CP, NCH, E])
                    link(nv.tensor_tensor(c4[:, :, e, :], g3(q1), s_e, ALU.is_equal))
                    link(nv.tensor_tensor(c4[:, :, e, :], c4[:, :, e, :],
                                          low[:, e, :].unsqueeze(1).to_broadcast([CP, NCH, E]), ALU.mult))
                link(nv.reduce_sum(g3(q3), c4, AX.X))
                link(nv.tensor_tensor(q2, q2, q3, ALU.add))
                link(nv.tensor_scalar(q3, q2, 1.0, None, ALU.is_le))

            def weights_of_the_two():
                for s in range(2):
                    link(nv.tensor_scalar(q4, q2, float(s), None, ALU.is_equal))
                    link(nv.tensor_tensor(q4, q4, q1, ALU.mult))
                    link(nv.reduce_sum(wgt[:, s, :], g3(q4), AX.X))
                link(nv.tensor_tensor(mx, wgt[:, 0, :], wgt[:, 1, :], ALU.add))
                link(nv.tensor_scalar(mx, mx, 1e-20, None, ALU.add))
                link(nv.reciprocal(mx, mx))
                for s in range(2):
                    link(nv.tensor_tensor(wgt[:, s, :], wgt[:, s, :], mx, ALU.mult))

            def take_counts():
                v.wait_ge(r_ps, 1)
                link(nv.tensor_copy(q3, M0[0:CP, 0:NCH * E]))
                nv.tensor_copy(q0.rearrange(eg, e=E), M2[0:CP, 0:NCH * E].rearrange("p (g e) -> p e g", e=E))\
                  .then_inc(r_cp, 1)
                v.wait_ge(r_cp, 1)

            def places():
                link(nv.memset(q4, 1.0))
                link(nv.memset(q4.rearrange(eg, e=E)[:, :, 0:1], 0.0))
                link(nv.tensor_tensor_scan(q5, q4, q0, 0.0, ALU.mult, ALU.add))
                cnt = q5.rearrange(eg, e=E)[:, :, NCH - 1]
                link(nv.tensor_scalar(smalli[:, :], cnt, float(P - 1), None, ALU.add))
                link(nv.tensor_scalar(smalli[:, :], smalli[:, :], P.bit_length() - 1, None, ALU.logical_shift_right))
                link(nv.tensor_copy(til, smalli[:, :]))
                link(nv.memset(one8, 1.0))
                link(nv.tensor_tensor_scan(end, one8, til, 0.0, ALU.mult, ALU.add))
                link(nv.tensor_tensor(base, end, til, ALU.subtract))
                link(nv.tensor_scalar(base, base, float(P), float(SHT * P), ALU.mult, ALU.add))
                link(nv.tensor_tensor(q5, q5, q0, ALU.subtract))
                link(nv.tensor_tensor(q5.rearrange(eg, e=E), q5.rearrange(eg, e=E),
                                      base.unsqueeze(2).to_broadcast([CP, E, NCH]), ALU.add))
                link(nv.tensor_tensor(g3(q0), q5.rearrange("p (e g) -> p g e", e=E),
                                      g3(q3), ALU.add))
                for s in range(2):
                    link(nv.tensor_scalar(q4, q2, float(s), None, ALU.is_equal))
                    link(nv.tensor_tensor(q4, q4, q0, ALU.mult))
                    link(nv.reduce_sum(mx, g3(q4), AX.X))
                    link(nv.tensor_copy(dsti[:, s, :], mx))
                link(nv.tensor_scalar(endt[:, :], end[0:1, :], float(SHT), None, ALU.add))

            def tables():
                tf, et = small[:, 5, 0:RTT], small[:, 6, 0:RTT]
                link(nv.tensor_copy(tf, tileno[:, :]))
                c2 = cmp3[:, 0:RTT * E].rearrange("p (t e) -> p t e", e=E)
                link(nv.tensor_tensor(c2, end.unsqueeze(1).to_broadcast([CP, RTT, E]),
                                      tf.unsqueeze(2).to_broadcast([CP, RTT, E]), ALU.is_le))
                link(nv.reduce_sum(et, c2, AX.X))
                link(nv.memset(tset[:, 0:SHT], 0))
                link(nv.tensor_scalar(tset[:, SHT:NT], et[0:1, :], float(E - 1), 1.0, ALU.min, ALU.add))
                link(nv.tensor_scalar(twait[:, :], tset[:, :], 48.0, 48.0, ALU.mult, ALU.add))
                link(nv.tensor_scalar(toff[:, :], tset[:, :], 1, None, ALU.bitwise_and))
                link(nv.tensor_scalar(toff[:, :], toff[:, :], float(SETW), None, ALU.mult))
                nv.memset(small[:, 7, :], 0.0).then_inc(r_done, 1)

            def gate(t, q):
                v.wait_ge(t_silu, 2 * t + q + 1)
                if not (isinstance(t, int) and t == 0):
                    v.wait_ge(t_aps, 2 * t + q - 1)
                nv.tensor_tensor(act[q], sil[q], bank[2 + q][:, :], ALU.mult).then_inc(t_act, 1)

            def actT_copy(t, q):
                v.wait_ge(t_aps, 2 * t + q + 1)
                if not (isinstance(t, int) and t == 0):
                    v.wait_ge(t_yps, t)
                nv.tensor_copy(actT[q].rearrange("p k t -> p (k t)"), bank[5 + q][:, :]).then_inc(t_aT, 1)

            def tile(t, between=None):
                gate(t, 0)
                gate(t, 1)
                if between:
                    between()
                actT_copy(t, 0)
                actT_copy(t, 1)
            softmax_and_greater()
            tile(0)
            choose()
            tile(1)
            weights_of_the_two()
            tile(2, take_counts)
            places()
            tile(3)
            tables()
            with v.Fori(4, NT) as t:
                tile(t)

            def add_sum(b, j):
                g, k = b * JC + j, j % 2
                v.wait_ge(c_ps, g + 1)
                xv = xchunk(b, j)
                nv.tensor_tensor(xv, xv, bank[k][:, 0:T].rearrange("p (r q) -> p r q", r=RR),
                                 ALU.add).then_inc(c_x, 1)
            def combine(b):
                for j in range(JC):
                    g, k = b * JC + j, j % 2
                    g2 = b * (JC // 2) + j // 2
                    v.wait_ge(c_g[k], 32 * g2 + 32)
                    v.wait_ge(c_sh[k], 16 * g2 + 16)
                    if started(b) or j > 1:
                        v.wait_ge(c_ps, g if j == 0 else g - 1)
                    w0s = wgt[:, 0, ds(g, 1)]
                    w1s = wgt[:, 1, ds(g, 1)]
                    nv.scalar_tensor_tensor(out=ysh[k], in0=y0[k], scalar=w0s, in1=ysh[k],
                                            op0=ALU.mult, op1=ALU.add).then_inc(c_a, 1)
                    v.wait_ge(c_a, g + 1)
                    nv.scalar_tensor_tensor(out=ysum[k], in0=y1[k], scalar=w1s, in1=ysh[k],
                                            op0=ALU.mult, op1=ALU.add).then_inc(c_s, 1)
                    if j:
                        add_sum(b, j - 1)
                add_sum(b, JC - 1)
            peeled(v, B, combine)

        @block.tensor
        def _(pe):
            te = nc.tensor
            mm = te.matmul
            pe.wait_ge(s_const, NCONST)
            pe.wait_ge(s_in, 16 * 14)
            pe.wait_ge(s_setup, 3)
            for h in range(HALF):
                for tap in range(TAPS):
                    te.transpose(bank[h][:, tap * P:(tap + 1) * P], wsc[h][:, tap, :], ident[:, :])
                te.transpose(bank[2][:, h * P:(h + 1) * P], in_raw[:, HALF + h, :], ident[:, :])
                te.transpose(bank[2][:, (2 + h) * P:(3 + h) * P], ow_raw[:, h * P:(h + 1) * P], ident[:, :])
                te.transpose(bank[3][:, h * P:h * P + RK + RANK], xp_raw[:, h * P:(h + 1) * P],
                             ident[0:RK + RANK, 0:RK + RANK])
                te.transpose(bank[4][0:RANK, h * P:(h + 1) * P], dp_raw[:, h, :], ident[:, :])
            for r in range(RR):
                last = te.transpose(bank[3][:, 256 + r * E:256 + (r + 1) * E], gw_raw[:, r::RR], ident[0:E, 0:E])
            last.then_inc(s_setup, 1)
            pe.wait_ge(s_setup, SETUP)
            for h in range(HALF):
                last = mm(M0[:, h:h + 1], Wu[:, h, TAPS - 1, :], tokh[:, HIST - 1:HIST], start=True, stop=True)
            last.then_inc(s_setup, 1)
            pe.wait_ge(s_setup, SETUP + 3)
            for h in range(HALF):
                last = mm(M0[0:RK + RANK, 4:5], Wx[:, h, :], u[1][:, h, 0:1], start=(h == 0), stop=(h == HALF - 1))
            last.then_inc(s_setup, 1)
            pe.wait_ge(s_setup, SETUP + 8)
            for h in range(HALF):
                last = mm(M0[:, 12 + h:13 + h], Wd[:, h, :], dtr[:, 0:1], start=True, stop=True)
            last.then_inc(s_setup, 1)
            pe.wait_ge(s_setup, SETUP + 17)
            for n in range(NS):
                last = mm(M0[:, 16 + n:17 + n], sel[:, n, :], S[1][:, 0:1], start=True, stop=True)
            last.then_inc(s_setup, 1)

            def front1_piece(n, g, b, j):
                if n == 11:
                    if isinstance(g, int) and g < 2:
                        if g:
                            pe.wait_ge(f_seq, g)
                    else:
                        pe.wait_ge(f_abs, 2 * g)
                    for r in range(RR):
                        last = mm(M0[:, 0:CP], meanw[:, :], xchunk(b, j)[:, r, :], start=(r == 0), stop=(r == RR - 1))
                    last.then_inc(f_mean, 1)
                if n == 13:
                    pe.wait_ge(f_sq, g + 1)
                    for r in range(RR):
                        last = mm(M0[:, P:P + CP], meanw[:, :], sq[:, r, :], start=(r == 0), stop=(r == RR - 1))
                    last.then_inc(f_var, 1)

            def front2_piece(n, g, k):
                if n in (0, 1, 2, 3):
                    h = n // 2
                    if n == 0:
                        pe.wait_ge(f_seq, g + 1 if started(g) else 2)
                        pe.wait_ge(f_hist, g + 1)
                    for tap in (n % 2 * 2, n % 2 * 2 + 1):
                        last = mm((M0, M2)[h][:, 0:T], Wu[:, h, tap, :], seq[k][:, tap:tap + T],
                                  start=(tap == 0), stop=(tap == TAPS - 1))
                    if n % 2:
                        last.then_inc(f_ups, 1)
                if n == 4:
                    for h in range(HALF):
                        pe.wait_ge(f_u, 2 * g + h + 1)
                        mm((M0, M2)[h][:, 0:T], Wz[:, h, :], seq[k][:, HIST:HIST + T], start=True, stop=True)\
                            .then_inc(f_zps, 1)
                if n == 6:
                    pe.wait_ge(f_z, 2 * g + 2)
                    for h in range(HALF):
                        last = mm(M0[0:RK + RANK, 0:T], Wx[:, h, :], u[k][:, h, :],
                                  start=(h == 0), stop=(h == HALF - 1))
                    last.then_inc(f_bcps, 1)
                if n == 8:
                    pe.wait_ge(f_rank, g + 1)
                    pe.wait_ge(f_res, g + 1)
                    for h in range(HALF):
                        mm((M0, M2)[h][:, 0:T], Wd[:, h, :], dtr[:, :], start=True, stop=True).then_inc(f_dtps, 1)

            def back_piece(n, g, b, j):
                if n == 5:
                    pe.wait_ge(b_ydz, g + 1)
                    if not (isinstance(g, int) and g < 1):
                        pe.wait_ge(b_log, g)
                    for h in range(HALF):
                        last = mm(M1[:, 0:T], Wo[:, h, :], yd[:, h, :], start=(h == 0), stop=(h == HALF - 1))
                    last.then_inc(b_ops, 1)
                if n == 7:
                    pe.wait_ge(b_x, g + 1)
                    for r in range(RR):
                        last = mm(M1[:, 0:CP], meanw[:, :], xchunk(b, j)[:, r, :], start=(r == 0), stop=(r == RR - 1))
                    last.then_inc(b_mean, 1)
                if n == 9:
                    pe.wait_ge(b_sq, g + 1)
                    for r in range(RR):
                        last = mm(M1[:, P:P + CP], meanw[:, :], sq2[:, r, :], start=(r == 0), stop=(r == RR - 1))
                    last.then_inc(b_var, 1)
                if n == 12:
                    pe.wait_ge(b_xn, g + 1)
                    for r in range(RR):
                        last = te.transpose(M1[0:CP, r * P:(r + 1) * P], cen2[:, r, :], ident[:, :])
                    last.then_inc(b_tr, 1)
                if n == 14:
                    pe.wait_ge(b_rows, g + 1)
                    for r in range(RR):
                        last = mm(M1[0:CP, 0:E], cen2[:, r, :], gT[:, r, :], start=(r == 0), stop=(r == RR - 1))
                    last.then_inc(b_lps, 1)

            pe.wait_ge(s_setup, TOKEN_DONE)
            pe.wait_ge(s_x0, 16)
            for g in range(2):
                for n in range(NS):
                    front1_piece(n, g, 0, g)
            for n in range(NS):
                front2_piece(n, 0, 0)
            pe.wait_ge(s_x, 16 * (B - 1))

            def batch(b, first, last):
                for j in range(JC):
                    g, k = b * JC + j, j % 2
                    front = not (last and j == JC - 1)
                    front1 = not (last and j >= JC - 2)

                    def spread(n):
                        i = NS * g + n
                        if n == 0:
                            pe.wait_ge(f_lo, g + 1)
                        if not (first and j == 0 and n < 2):
                            pe.wait_ge(m_dBu, i - 1)
                        mm(Bb[n % 2][:, 0:T], sel[:, n, :], S[k][:, :], start=True, stop=True).then_inc(m_B, 1)
                        if not (first and j == 0 and n < 1):
                            pe.wait_ge(m_Cs, i)
                        mm(Cb[:, 0:T], sel[:, NS + n, :], S[k][:, :], start=True, stop=True).then_inc(m_C, 1)

                    def add_y(n):
                        i = NS * g + n
                        pe.wait_ge(m_hC, i + 1)
                        if n == 0 and not (first and j == 0):
                            pe.wait_ge(b_yd, g)
                        for h in range(HALF):
                            last_mm = mm(Yb[h][:, 0:T], ident[:, :], hC[n % RING][:, h, :],
                                         start=(n == 0), stop=(n == NS - 1))
                        last_mm.then_inc(m_y, 1)
                    spread(0)
                    for n in range(NS):
                        if n < NS - 1:
                            spread(n + 1)
                        if n >= 2:
                            add_y(n - 2)
                        if not (first and j == 0):
                            back_piece(n, g - 1, b if j else b - 1, (j - 1) % JC)
                        if front:
                            front2_piece(n, g + 1, 1 - k)
                        if front1:
                            front1_piece(n, g + 2, b if j < JC - 2 else b + 1, (j + 2) % JC)
                    add_y(NS - 2)
                    add_y(NS - 1)
            batches(pe, batch)
            for n in range(NS):
                back_piece(n, NCH - 1, B - 1, JC - 1)

            def counts():
                pe.wait_ge(r_ch, R_CHOSEN)
                mm(M0[0:CP, 0:NCH * E], tri[:, :], rt[3], start=True, stop=True)
                mm(M2[0:CP, 0:NCH * E], one96[:, :], rt[3], start=True, stop=True).then_inc(r_ps, 1)

            def x_transpose(t, k):
                pe.wait_ge(t_x[k], (t - k) * 8 + 16)
                if not (isinstance(t, int) and t == 0):
                    pe.wait_ge(t_xT, t)
                for r in range(RR):
                    last = te.transpose(bank[4][:, r * P:(r + 1) * P], xin[k][:, r * P:(r + 1) * P], ident[:, :])
                last.then_inc(t_xps, 1)

            def set_of(t, routed):
                return pe.value_load(toff[0:1, ds(t, 1)], min_val=0, max_val=SETW) if routed else 0

            def up(t, k, routed):
                if routed:
                    loaded = pe.value_load(twait[0:1, ds(t, 1)], min_val=48, max_val=48 * (E + 1))
                off = set_of(t, routed)
                pe.wait_ge(s_w, loaded if routed else 48)
                pe.wait_ge(t_xT, t + 1)
                for q in range(2):
                    if not (isinstance(t, int) and t == 0):
                        pe.wait_ge(t_act, 2 * t + q - 1)
                    for w in range(2):
                        for r in range(RR):
                            last = mm(bank[2 * w + q][:, :], xT[k][:, r, :],
                                      WALL[:, ds(off + (w * RR * I + r * I + q * 512), 512)],
                                      start=(r == 0), stop=(r == RR - 1))
                    last.then_inc(t_h, 1)

            def down(t, routed):
                off = set_of(t, routed)
                for q in range(2):
                    pe.wait_ge(t_aT, 2 * t + q + 1)
                if not (isinstance(t, int) and t == 0):
                    pe.wait_ge(t_y, t)
                for c in range(IK):
                    last = mm(bank[7][:, :], actT[c // 4][:, c % 4, :],
                              WALL[:, ds(off + (2 * RR * I + c * C), C)],
                              start=(c == 0), stop=(c == IK - 1))
                last.then_inc(t_yps, 1)

            def act_transpose(t):
                for q in range(2):
                    pe.wait_ge(t_act, 2 * t + q + 1)
                    if not (isinstance(t, int) and t == 0):
                        pe.wait_ge(t_aT, 2 * t + q - 1)
                    for c in range(4):
                        last = te.transpose(bank[5 + q][:, c * P:(c + 1) * P], act[q][:, c * P:(c + 1) * P],
                                            ident[:, :])
                    last.then_inc(t_aps, 1)

            def tile(t, k, routed, behind=True, ahead=True, after_routed=None, with_counts=False):
                up(t, k, routed)
                if ahead:
                    x_transpose(t + 1, 1 - k)
                if behind:
                    down(t - 1, routed if after_routed is None else after_routed)
                if with_counts:
                    pe.wait_ge(t_aT, 2 * t)
                    counts()
                    pe.wait_ge(r_cp, 1)
                act_transpose(t)
            x_transpose(0, 0)
            tile(0, 0, False, behind=False)
            tile(1, 1, False)
            tile(2, 0, False, with_counts=True)
            with pe.Fori(1, SHT // 2 - 1) as t2:
                tile(2 * t2 + 1, 1, False)
                tile(2 * t2 + 2, 0, False)
            tile(SHT - 1, 1, False)
            pe.wait_ge(r_done, 1)
            tile(SHT, 0, True, after_routed=False)
            with pe.Fori(SHT // 2, (NT - 3) // 2) as t2:
                tile(2 * t2 + 1, 1, True)
                tile(2 * t2 + 2, 0, True)
            tile(NT - 2, 1, True)
            tile(NT - 1, 0, True, ahead=False)
            down(NT - 1, True)

            def transpose_sums(b):
                for j in range(JC):
                    g, k = b * JC + j, j % 2
                    pe.wait_ge(c_s, g + 1)
                    if started(b) or j > 1:
                        pe.wait_ge(c_x, g if j == 0 else g - 1)
                    for r in range(RR):
                        last = te.transpose(bank[k][:, r * CP:(r + 1) * CP], ysum[k][:, r::RR], ident[0:CP, 0:CP])
                    last.then_inc(c_ps, 1)
            peeled(pe, B, transpose_sums)


_INS = ['x', 'L0_conv_global_token', 'L0_conv_in_proj_w', 'L0_conv_conv_w', 'L0_conv_conv_b', 'L0_conv_x_proj_w',
        'L0_conv_dt_proj_w', 'L0_conv_dt_proj_b', 'L0_conv_A_log', 'L0_conv_D', 'L0_conv_out_proj_w',
        'L0_ffn_gate_w', 'L0_ffn_w1', 'L0_ffn_w2', 'L0_ffn_w3', 'L0_ffn_sw1', 'L0_ffn_sw2', 'L0_ffn_sw3']


def kernel(**inputs):
    import numpy as _np
    import concourse.bacc as _bacc
    from concourse import mybir as _mybir
    from concourse.bass_utils import run_bass_kernel_spmd as _run

    nc = _bacc.Bacc("TRN2", target_bir_lowering=False, num_devices=1)
    arrays, args = {}, []
    for name in _INS:
        a = _np.ascontiguousarray(inputs[name])
        arrays[f"in_{name}_dram"] = a
        args.append(nc.dram_tensor(f"in_{name}_dram", a.shape, _mybir.dt.from_np(a.dtype), kind="ExternalInput").ap())
    shape = inputs['x'].shape
    args.append(nc.dram_tensor("out_0_dram", shape, _mybir.dt.float32, kind="ExternalOutput").ap())
    bass_metaformer_mamba_moe_kernel(nc, *args)
    r = _run(nc, [arrays], core_ids=[0])
    return r.results[0]["out_0_dram"]
```

```python
import concourse.bass as bass
from concourse import mybir
from contextlib import ExitStack


def bass_metaformer_mamba_moe_kernel(nc, x, token, in_w, conv_w, conv_b, xp_w, dtp_w, dtp_b,
                                     A_log, D_skip, out_w, gate_w, w1, w2, w3, sw1, sw2, sw3, out):
    fp32, bf16, i32 = mybir.dt.float32, mybir.dt.bfloat16, mybir.dt.int32
    ALU, ACT, AX = mybir.AluOpType, mybir.ActivationFunctionType, mybir.AxisListType
    ds = bass.ds

    P = 128
    B, C, H, W = x.shape
    R = 2
    RR = R * R
    PIX = H * W
    HALF = in_w.shape[0] // 2 // P
    NS = A_log.shape[1]
    RANK = dtp_w.shape[1]
    TAPS = conv_w.shape[1]
    HIST = TAPS - 1
    JC = 6
    HC = H // JC
    CP = HC * W
    T = CP * RR
    NCH = B * JC
    BC = 2 * NS
    E = gate_w.shape[0]
    I = w1.shape[2]
    IK = I // P
    TOK = B * PIX
    SHT = TOK // P
    RTT = (2 * TOK + E * (P - 1)) // P
    NT = SHT + RTT
    SETW = 3 * I * RR
    SCAN0 = 2 * I * RR
    EPS_C, EPS_T = 1e-6, 1e-5
    AHEAD = 6
    RING = 4
    CG = 2
    RK = 3 * BC
    SETUP = 7
    TOKEN_DONE = SETUP + 19
    R_CHOSEN = 33

    xrows = nc.dram_tensor("xrows", (NT * P, C), fp32, kind="Internal").ap()
    crows = nc.dram_tensor("crows", (2, NS, T), fp32, kind="Internal").ap()
    yrows = nc.dram_tensor("yrows", (NT * P, C), fp32, kind="Internal").ap()

    ctx = ExitStack()
    with ctx:
        def sb(name, shape, dt=fp32):
            return ctx.enter_context(nc.sbuf_tensor(name, shape, dt))

        def sem(name):
            return ctx.enter_context(nc.semaphore(name))

        X = sb("X", [P, B * RR, PIX])
        WALL = sb("WALL", [P, 2 * SETW])
        WS0, WS1 = WALL[:, 0:SETW], WALL[:, SETW:2 * SETW]
        ident = sb("ident", [P, P])
        meanw = sb("meanw", [P, P])
        Lg = sb("Lg", [CP, NCH, E])
        gT = sb("gT", [P, RR, E])
        dsti = sb("dsti", [CP, 2, NCH], i32)
        wgt = sb("wgt", [CP, 2, NCH])
        tset = sb("tset", [1, NT], i32)
        toff = sb("toff", [1, NT], i32)
        twait = sb("twait", [1, NT], i32)
        endt = sb("endt", [1, E], i32)

        at = [0]

        def part(n):
            v = WALL[:, SCAN0 + at[0]:SCAN0 + at[0] + n]
            at[0] += n
            assert SCAN0 + at[0] <= 2 * SETW
            return v

        def halves():
            return part(HALF * T).rearrange("p (h t) -> p h t", h=HALF)
        dA = [halves() for _ in range(AHEAD - 1)] + [sb("dA5", [P, HALF, T])]
        dBu = [halves() for _ in range(2)] + [sb("dBu2", [P, HALF, T])[:, :, :]]
        hs = [halves() for _ in range(RING)]
        hC = [halves() for _ in range(RING)]
        Cs = [part(CG * T).rearrange("p (c t) -> p c t", c=CG) for _ in range(3)]
        yd = halves()
        cen, sq, cen2, sq2 = (part(T).rearrange("p (r q) -> p r q", r=RR) for _ in range(4))
        u2 = sb("u2", [P, 2, HALF * T])
        u = [u2[:, k, :].rearrange("p (h t) -> p h t", h=HALF) for k in range(2)]
        z = [sb(f"z{k}", [P, HALF, T]) for k in range(2)]
        dt = [sb(f"dt{k}", [P, HALF, T]) for k in range(2)]
        dtu = [sb(f"dtu{k}", [P, HALF, T]) for k in range(2)]
        seq = [sb(f"seq{k}", [P, HIST + T]) for k in range(2)]
        S = [sb(f"S{k}", [3 * BC, T], bf16) for k in range(2)]
        Rm = sb("Rm", [2 * BC, T])
        bcrow = sb("bcrow", [BC, T])
        dtr = sb("dtr", [RANK, T])
        absx = sb("absx", [P, HALF, T])
        relx = sb("relx", [P, HALF, T])
        expx = sb("expx", [P, HALF, T])
        lnx = absx
        onex = sb("onex", [P, HALF, T])
        st = sb("st", [P, 4, CP])
        st2 = sb("st2", [P, 4, CP])
        rows = [sb(f"rows{k}", [CP, C]) for k in range(2)]
        carry = sb("carry", [P, NS, HALF])
        h0 = sb("h0", [P, NS, HALF])
        tokh = sb("tokh", [P, HIST])
        sel = sb("sel", [3 * BC, NS, P], bf16)
        Wu = sb("Wu", [P, HALF, TAPS, P])
        Wz = sb("Wz", [P, HALF, P])
        Wx = sb("Wx", [P, HALF, RK + RANK])
        Wd = sb("Wd", [RANK, HALF, P])
        Wo = sb("Wo", [P, HALF, P])
        cb = sb("cb", [P, HALF])
        db = sb("db", [P, HALF])
        Dk = sb("Dk", [P, HALF])
        An = sb("An", [P, HALF, NS])

        def raw(t, lo, n, parts=P):
            return t.rearrange("p h t -> p (h t)")[0:parts, lo:lo + n]
        in_raw = raw(dA[0], 0, 512).rearrange("p (k d) -> p k d", k=4)
        wsc = [raw(dA[1 + h], 0, TAPS * P).rearrange("p (k d) -> p k d", k=TAPS) for h in range(HALF)]
        cw = raw(dA[3], 0, HALF * TAPS).rearrange("p (h k) -> p h k", h=HALF)
        xp_raw = raw(dBu[0], 0, 256, RK + RANK)
        dp_raw = raw(dBu[1], 0, HALF * RANK).rearrange("p (h k) -> p h k", h=HALF)
        ow_raw = raw(dBu[1], 16, 256)
        gw_raw = raw(hC[0], 0, 512, E)
        al_raw = raw(hs[0], 0, HALF * NS).rearrange("p (h k) -> p h k", h=HALF)

        zrow = sb("zrow", [P, P])

        bank = [ctx.enter_context(nc.psum_tensor(f"bank{k}", [P, 512], fp32)) for k in range(8)]
        Yb = [bank[0], bank[1]]
        Bb = [bank[2], bank[3], bank[4]]
        M0, M2, M1 = bank[5], bank[6], bank[7]

        s_in = sem("inputs_loaded")
        s_const = sem("constants_made")
        s_setup = sem("setup_step")
        s_passed = sem("pool_passed_its_waits")
        s_sp_passed = sem("sp_passed_its_wait")
        s_zero = sem("zero_rows_written")
        s_x0, s_x = sem("x_of_image_0_loaded"), sem("x_loaded")
        s_w = sem("expert_weights_loaded")
        s_w2 = sem("shared_w2_loaded")
        f_mean, f_cen, f_sq, f_var, f_ln, f_rsq = (sem("f_" + n) for n in
                                                   "mean centred squared var ln rsqrt".split())
        f_st = sem("f_stat_step")
        f_seq = sem("f_seq_written")
        f_hist = sem("f_hist_copied")
        f_ups, f_zps = sem("f_u_in_psum"), sem("f_z_in_psum")
        f_u, f_zc = sem("f_u_silu"), sem("f_z_copied")
        f_z = sem("f_z_silu")
        f_bcps, f_dtps = sem("f_bc_in_psum"), sem("f_dt_in_psum")
        f_hi, f_res, f_mid, f_lo = (sem("f_bc_" + n) for n in "hi residue mid lo".split())
        f_rank = sem("f_rank_copied")
        f_abs = sem("f_abs_relu")
        f_exp = sem("f_exp")
        f_ln1 = sem("f_ln1p")
        f_nd = sem("f_rounding_of_1p")
        f_dt1 = sem("f_dt_small")
        f_dt, f_dtu = sem("f_dt"), sem("f_dtu")
        m_B = sem("m_B_in_psum")
        m_dA = sem("m_dA")
        m_C = [sem("m_C_loaded" + str(r)) for r in range(3)]
        f_cr, f_cst = sem("f_c_rows_copied"), sem("f_c_rows_stored")
        m_dBu, m_h = sem("m_dBu"), sem("m_h_scanned")
        m_hC, m_carry = sem("m_hC"), sem("m_carry")
        m_y = sem("m_y_added")
        b_yd, b_ydz, b_ops, b_x = (sem("b_" + n) for n in "y_read gated out_in_psum residual".split())
        b_mean, b_cen, b_sq, b_var, b_ln, b_rsq = (sem("b_" + n) for n in
                                                   "mean centred squared var ln rsqrt".split())
        b_st = sem("b_stat_step")
        b_xn = sem("b_normalised")
        b_tr, b_rows, b_lps, b_log = (sem("b_" + n) for n in
                                      "transposed rows_copied logits_in_psum logits".split())
        b_out = [sem("b_rows_stored0"), sem("b_rows_stored1")]
        r_ch = sem("routing_step")
        r_exp = sem("r_exp")
        r_ps = sem("r_counts_in_psum")
        r_cp = sem("r_counts_copied")
        r_done = sem("routed")
        r_ld = [sem("r_rows_loaded0"), sem("r_rows_loaded1")]
        r_ix = sem("r_index_copied")
        r_sc = [sem("r_scattered0"), sem("r_scattered1")]
        t_x = [sem("t_x_loaded0"), sem("t_x_loaded1")]
        t_xps, t_xT = sem("t_x_transposed"), sem("t_xT_copied")
        t_h, t_silu, t_act = sem("t_h_in_psum"), sem("t_silu"), sem("t_act")
        t_aps, t_aT = sem("t_act_transposed"), sem("t_actT_copied")
        t_yps, t_y = sem("t_y_in_psum"), sem("t_y_copied")
        t_out = [sem("t_y_stored0"), sem("t_y_stored1")]
        c_sh = [sem(f"c_shared_loaded{j}") for j in range(JC)]
        c_ix = sem("c_index_copied")
        c_g = [sem(f"c_gathered{j}") for j in range(JC)]
        c_a, c_s = sem("c_first_added"), sem("c_summed")
        c_ps, c_x = sem("c_transposed"), sem("c_added")
        c_out = sem("c_out_stored")

        def flat(t):
            return t[:, :, :].rearrange("p h t -> p (h t)")
        xin = [flat(u[k])[:, 0:C] for k in range(2)]
        xT = [flat(z[k])[:, 0:C].rearrange("p (r t) -> p r t", r=RR) for k in range(2)]
        sil = [flat(dt[k])[:, 0:512] for k in range(2)]
        act = [flat(dtu[k])[:, 0:512] for k in range(2)]
        actT = [flat(absx)[:, 0:512].rearrange("p (k t) -> p k t", k=4),
                flat(relx)[:, 0:512].rearrange("p (k t) -> p k t", k=4)]
        yout = [flat(expx)[:, 0:512], flat(onex)[:, 0:512]]
        ysh, y0, y1, ysum = ([WALL[0:CP, (q * JC + j) * C:(q * JC + j + 1) * C] for j in range(JC)] for q in range(4))
        ixj = sb("ixj", [CP, 2, JC], i32)
        ixc = sb("ixc", [CP, 2, 2], i32)
        rt = [WS1[0:CP, k * NCH * E:(k + 1) * NCH * E] for k in range(6)]
        cmp3 = WS1[0:CP, 2048:2048 + NCH * E * E]
        tri = sb("tri", [CP, CP])
        one96 = sb("one96", [CP, CP])
        low = sb("low", [CP, E, E])
        tileno = sb("tileno", [CP, RTT], i32)
        small = WS1[0:CP, 4096:4096 + 8 * RTT].rearrange("p (a t) -> p a t", a=8)
        smalli = sb("smalli", [CP, E], i32)

        NCONST = 9

        def weights_of(q, ws):
            a, b3, b2 = (sw1[0], sw3[0], sw2[0]) if q == 0 else (w1[q - 1], w3[q - 1], w2[q - 1])
            return ((ws[:, 0:4096].rearrange("p (r i) -> p r i", r=RR), a.rearrange("(c r) i -> c r i", r=RR)),
                    (ws[:, 4096:8192].rearrange("p (r i) -> p r i", r=RR), b3.rearrange("(c r) i -> c r i", r=RR)),
                    (ws[:, 8192:12288].rearrange("p (k n) -> p k n", k=IK), b2.rearrange("(k p) n -> p k n", p=P)))

        def peeled(eng, stop, body):
            body(0)
            with eng.Fori(1, stop) as i:
                body(i)

        def started(i):
            return not (isinstance(i, int) and i == 0)

        block = ctx.enter_context(nc.Block())

        def xchunk(b, j):
            return X[:, ds(b * RR, RR), j * CP:(j + 1) * CP] if not isinstance(b, int) else \
                X[:, b * RR:(b + 1) * RR, j * CP:(j + 1) * CP]

        def batches(eng, body):
            body(0, True, False)
            with eng.Fori(1, B - 1) as b:
                body(b, False, False)
            body(B - 1, False, True)

        @block.sync
        def _(sp):
            loads = [
                (in_raw, in_w.rearrange("(k e) d -> e k d", e=P)),
                (cw, conv_w.rearrange("(h p) k -> p h k", p=P)),
                (xp_raw[0:BC, :], xp_w[RANK:RANK + BC, :]),
                (xp_raw[BC:2 * BC, :], xp_w[RANK:RANK + BC, :]),
                (xp_raw[2 * BC:3 * BC, :], xp_w[RANK:RANK + BC, :]),
                (xp_raw[RK:RK + RANK, :], xp_w[0:RANK, :]),
                (dp_raw, dtp_w.rearrange("(h p) k -> p h k", p=P)),
                (ow_raw, out_w),
                (gw_raw, gate_w),
                (al_raw, A_log.rearrange("(h p) k -> p h k", p=P)),
                (cb[:, :], conv_b.rearrange("(h p) -> p h", p=P)),
                (db[:, :], dtp_b.rearrange("(h p) -> p h", p=P)),
                (Dk[:, :], D_skip.rearrange("(h p) -> p h", p=P)),
                (tokh[:, HIST - 1:HIST], token.rearrange("a b c -> c (a b)")),
            ]
            assert len(loads) == 14

            def load_x(b, done):
                sp.dma_start(X[:, b * RR:(b + 1) * RR, :].rearrange("p r q -> p (r q)"),
                             x[b].rearrange("(c r) h w -> c (r h w)", r=RR)).then_inc(done, 16)
            load_x(0, s_x0)
            with nc.allow_non_contiguous_dma(reason="a few vectors of 256 entries"):
                for dst, src in loads:
                    sp.dma_start(dst, src).then_inc(s_in, 16)
            for b in range(1, B):
                load_x(b, s_x)
            sp.wait_ge(s_const, NCONST)
            with sp.Fori(SHT, NT) as t:
                sp.dma_start(xrows[ds(t * P, P), :].rearrange("p (r c) -> p r c", r=RR),
                             zrow[:, :].unsqueeze(1).to_broadcast([P, RR, P])).then_inc(s_zero, 16)

            def store_c(g, k):
                sp.wait_ge(f_cr, g + 1)
                sp.dma_start(crows[k], bcrow[NS:BC, :]).then_inc(f_cst, 16)

            def store_rows(g, k):
                sp.wait_ge(b_rows, g + 1)
                sp.dma_start(xrows[ds(g * CP, CP), :], rows[k][:, :]).then_inc(b_out[k], 16)
            store_c(0, 0)

            def batch(b, first, last):
                for j in range(JC):
                    g, k = b * JC + j, j % 2
                    for q in range(NS // CG):
                        G = j * (NS // CG) + q
                        if q == 0:
                            sp.wait_ge(f_cst, 16 * (g + 1))
                            sp.sem_inc(s_sp_passed, 1)
                        if not (first and G < 3):
                            sp.wait_ge(m_hC, NS * g + CG * (q - 2))
                        sp.dma_start(Cs[G % 3][:, :, :].rearrange("p c t -> p (c t)"),
                                     crows[k, q * CG:(q + 1) * CG, :].rearrange("c t -> (c t)").unsqueeze(0)
                                     .to_broadcast([P, CG * T])).then_inc(m_C[G % 3], 16)
                        if q == 4 and not (first and j < 2):
                            store_rows(g - 2, k)
                        if q == NS // CG - 2 and not (last and j == JC - 1):
                            store_c(g + 1, 1 - k)
            batches(sp, batch)
            for k in range(2):
                sp.wait_ge(b_out[k], 16 * (NCH // 2 - 1))
            sp.wait_ge(b_yd, NCH)

            def load_tile(t, k):
                sp.dma_start(xin[k], xrows[ds(t * P, P), :]).then_inc(t_x[k], 16)

            def store_tile(t, k):
                sp.wait_ge(t_y, t + 1)
                sp.dma_start(yrows[ds(t * P, P), :], yout[k]).then_inc(t_out[k], 16)

            def two_tiles(t2):
                for k in range(2):
                    sp.wait_ge(t_xps, 2 * t2 + k + 1)
                    load_tile(2 * t2 + k + 2, k)
                    store_tile(2 * t2 + k, k)
            load_tile(0, 0)
            load_tile(1, 1)
            store_rows(NCH - 2, 0)
            store_rows(NCH - 1, 1)
            for k in range(2):
                sp.wait_ge(b_out[k], 16 * (NCH // 2))
            with sp.Fori(0, SHT // 2 - 1) as t2:
                two_tiles(t2)
            sp.wait_ge(r_sc[0], 32 * (NCH // 2))
            sp.wait_ge(r_sc[1], 32 * (NCH // 2))
            with sp.Fori(SHT // 2 - 1, (NT - 3) // 2) as t2:
                two_tiles(t2)
            sp.wait_ge(t_xps, NT - 2)
            load_tile(NT - 1, 0)
            for t in range(NT - 3, NT):
                store_tile(t, t % 2)

            sp.wait_ge(t_out[0], 16 * ((NT + 1) // 2))
            sp.wait_ge(t_out[1], 16 * (NT // 2))
            sp.wait_ge(t_y, NT)
            def load_shared(b):
                for j in range(JC):
                    g = b * JC + j
                    if started(b):
                        sp.wait_ge(c_s, g - JC + 1)
                    sp.dma_start(ysh[j], yrows[ds(g * CP, CP), :]).then_inc(c_sh[j], 16)
                if started(b):
                    store_image(b - 1)

            def store_image(b):
                sp.wait_ge(c_x, (b + 1) * JC)
                sp.dma_start(out[ds(b, 1), :, :, :].rearrange("a (c r) h w -> c (a r h w)", r=RR),
                             X[:, ds(b * RR, RR), :].rearrange("p r q -> p (r q)")).then_inc(c_out, 16)
            peeled(sp, B, load_shared)
            store_image(B - 1)
            sp.wait_ge(c_out, 16 * B)

        @block.gpsimd
        def _(pool):
            pool.memset(ident[:, :], 0.0).then_inc(s_const, 1)
            pool.memset(meanw[:, :], 1.0 / C).then_inc(s_const, 1)
            pool.memset(sel[:, :, :], 0.0).then_inc(s_const, 1)
            pool.memset(tri[:, :], 1.0)
            pool.memset(one96[:, :], 1.0)
            pool.memset(low[:, :, :], 1.0)
            pool.memset(tokh[:, 0:HIST - 1], 0.0)
            pool.memset(zrow[:, :], 0.0).then_inc(s_const, 1)
            pool.wait_ge(s_const, 4)
            pool.affine_select(out=ident[:, :], in_=ident[:, :], compare_op=ALU.not_equal, fill=1.0,
                               base=0, pattern=[[-1, P]], channel_multiplier=1).then_inc(s_const, 1)
            pool.affine_select(out=tri[:, :], in_=tri[:, :], compare_op=ALU.is_gt, fill=0.0,
                               base=0, pattern=[[1, CP]], channel_multiplier=-1)
            pool.affine_select(out=low[:, :, :], in_=low[:, :, :], compare_op=ALU.is_gt, fill=0.0,
                               base=0, pattern=[[1, E], [-1, E]], channel_multiplier=0)
            pool.iota(tileno[:, :], pattern=[[1, RTT]], base=0, channel_multiplier=0)
            for q in range(3):
                if q:
                    pool.wait_ge(s_const, 5 + q)
                pool.affine_select(out=sel[:, :, :], in_=sel[:, :, :], compare_op=ALU.not_equal, fill=1.0,
                                   base=-BC * q, pattern=[[-1, NS], [0, P]], channel_multiplier=1)\
                    .then_inc(s_const, 1)
            pool.memset(carry[:, :, :], 0.0).then_inc(s_const, 1)

            def on_a_count():
                pool.sem_inc(s_passed, 1)

            def softplus_tail(n, g, k):
                if n == 11:
                    pool.wait_ge(f_ln1, g + 1)
                    pool.wait_ge(f_nd, g + 1)
                    if not (isinstance(g, int) and g < 2):
                        pool.wait_ge(m_dA, NS * (g - 1))
                        pool.wait_ge(m_dBu, NS * (g - 1))
                    pool.tensor_tensor(dt[k][:, :, :], lnx[:, :, :], onex[:, :, :], ALU.subtract).then_inc(f_dt1, 1)
                if n == 12:
                    pool.wait_ge(f_dt1, g + 1)
                    pool.tensor_tensor(dt[k][:, :, :], dt[k][:, :, :], relx[:, :, :], ALU.add).then_inc(f_dt, 1)
                if n == 13:
                    pool.wait_ge(f_dt, g + 1)
                    pool.wait_ge(f_u, 2 * g + 2)
                    pool.tensor_tensor(dtu[k][:, :, :], dt[k][:, :, :], u[k][:, :, :], ALU.mult).then_inc(f_dtu, 1)

            def history(g, k, start):
                if not (isinstance(g, int) and g < 2):
                    pool.wait_ge(f_zps, 2 * (g - 1))
                if start:
                    on_a_count()
                    pool.tensor_copy(seq[k][:, 0:HIST], tokh[:, :]).then_inc(f_hist, 1)
                else:
                    pool.wait_ge(f_seq, g)
                    on_a_count()
                    pool.tensor_copy(seq[k][:, 0:HIST], seq[1 - k][:, T:T + HIST]).then_inc(f_hist, 1)

            for dst, src in weights_of(0, WS0)[0:2]:
                pool.dma_start(dst, src).then_inc(s_w, 16)
            pool.wait_ge(s_in, 16 * 14)
            history(0, 0, True)
            history(1, 1, False)
            for n in range(NS):
                softplus_tail(n, 0, 0)

            def batch(b, first, last):
                for j in range(JC):
                    g, k = b * JC + j, j % 2
                    front = not (last and j == JC - 1)
                    front1 = not (last and j >= JC - 2)
                    front0 = not (last and j >= JC - 3)
                    for n in range(NS):
                        i = NS * g + n
                        m = n % RING
                        if front1 and n == 9:
                            history(g + 2, k, j == JC - 2)
                        pool.wait_ge(m_h, i + 1)
                        G = (NS * j + n) // CG
                        if n % CG == 0:
                            pool.wait_ge(m_C[G % 3], 16 * (b * (NS * JC // CG // 3) + G // 3 + 1))
                        if not (first and j == 0 and n < RING):
                            pool.wait_ge(m_y, i - RING + 1)
                        pool.tensor_tensor(hC[m], hs[m], Cs[G % 3][:, n % CG, :].unsqueeze(1).to_broadcast([P, HALF, T]),
                                           ALU.mult).then_inc(m_hC, 1)
                        pool.tensor_copy(carry[:, n, :], hs[m][:, :, T - 1]).then_inc(m_carry, 1)
                        if front:
                            softplus_tail(n, g + 1, 1 - k)
            batches(pool, batch)

            pool.wait_ge(m_carry, NS * NCH)
            pool.wait_ge(m_y, NS * NCH)
            dst, src = weights_of(0, WS0)[2]
            pool.dma_start(dst, src).then_inc(s_w2, 16)

            def load_rows(g, k):
                pool.dma_start(rows[k][:, :], xrows[ds(g * CP, CP), :]).then_inc(r_ld[k], 16)
            pool.wait_ge(b_out[0], 16 * (NCH // 2))
            pool.wait_ge(b_out[1], 16 * (NCH // 2))
            load_rows(0, 0)
            load_rows(1, 1)

            pool.wait_ge(r_done, 1)
            pool.wait_ge(s_zero, 16 * RTT)
            pool.wait_ge(s_w, 32)
            for dst, src in weights_of(1, WS1):
                pool.dma_start(dst, src).then_inc(s_w, 16)

            def scatter(g2):
                for k in range(2):
                    if started(g2):
                        pool.wait_ge(r_sc[k], 32 * g2)
                        on_a_count()
                        load_rows(2 * g2 + k, k)
                    pool.tensor_copy(ixc[:, :, k], dsti[:, :, ds(2 * g2 + k, 1)].rearrange("p s g -> p (s g)"))\
                        .then_inc(r_ix, 1)
                    pool.wait_ge(r_ix, 2 * g2 + k + 1)
                    pool.wait_ge(r_ld[k], 16 * g2 + 16)
                    on_a_count()
                    for s in range(2):
                        pool.indirect_dma_start(
                            out=xrows, out_offset=bass.IndirectOffsetOnAxis(ap=ixc[:, s, k:k + 1], axis=0),
                            in_=rows[k][:, :], in_offset=None).then_inc(r_sc[k], 16)
            peeled(pool, NCH // 2, scatter)

            for q in range(2, E + 1):
                if q == 2:
                    pool.wait_ge(t_yps, SHT)
                else:
                    pool.wait_ge(t_yps, pool.value_load(endt[0:1, q - 3:q - 2], min_val=SHT, max_val=NT))
                pool.wait_ge(s_w, 32 + 48 * (q - 1))
                on_a_count()
                for dst, src in weights_of(q, (WS0, WS1)[q % 2]):
                    pool.dma_start(dst, src).then_inc(s_w, 16)

            pool.wait_ge(t_out[0], 16 * ((NT + 1) // 2))
            pool.wait_ge(t_out[1], 16 * (NT // 2))
            pool.wait_ge(r_sc[0], 32 * (NCH // 2))
            pool.wait_ge(r_sc[1], 32 * (NCH // 2))
            pool.wait_ge(t_yps, NT)
            def gather(b):
                for j in range(JC):
                    g = b * JC + j
                    if started(b):
                        pool.wait_ge(c_g[j], 32 * b)
                        pool.wait_ge(c_s, g - JC + 1)
                    on_a_count()
                    pool.tensor_copy(ixj[:, :, j], dsti[:, :, ds(g, 1)].rearrange("p s g -> p (s g)"))\
                        .then_inc(c_ix, 1)
                    pool.wait_ge(c_ix, g + 1)
                    on_a_count()
                    for s, dst in enumerate((y0, y1)):
                        pool.indirect_dma_start(
                            out=dst[j], out_offset=None, in_=yrows,
                            in_offset=bass.IndirectOffsetOnAxis(ap=ixj[:, s, j:j + 1], axis=0)).then_inc(c_g[j], 16)
            peeled(pool, B, gather)

        @block.scalar
        def _(sc):
            nsc = nc.scalar
            sc.wait_ge(s_in, 16 * 14)
            nsc.activation(An[:, :, :], al_raw, ACT.Exp).then_inc(s_setup, 1)

            def silu_u(g, k):
                for e, h in enumerate((1, 0)):
                    sc.wait_ge(f_ups, 2 * g + e + 1)
                    if e == 0 and not (isinstance(g, int) and g < 2):
                        sc.wait_ge(b_yd, g - 1)
                        sc.wait_ge(f_dtu, g - 1)
                    nsc.activation(u[k][:, h, :], (M0, M2)[h][:, 0:T], ACT.Silu, bias=cb[:, h:h + 1])\
                       .then_inc(f_u, 1)

            def z_copy(g, k, h):
                sc.wait_ge(f_zps, 2 * g + h + 1)
                if h == 0 and not (isinstance(g, int) and g < 2):
                    sc.wait_ge(b_ydz, g - 1)
                nsc.activation(z[k][:, h, :], M2[:, 0:T], ACT.Copy).then_inc(f_zc, 1)

            def silu_z(g, k):
                sc.wait_ge(f_zc, 2 * g + 2)
                nsc.activation(z[k][:, :, :], z[k][:, :, :], ACT.Silu).then_inc(f_z, 1)

            def bc_hi(g, k):
                sc.wait_ge(f_bcps, g + 1)
                if not (isinstance(g, int) and g < 2):
                    sc.wait_ge(m_B, NS * (g - 1))
                nsc.activation(S[k][:, :], M0[0:3 * BC, 0:T], ACT.Copy).then_inc(f_hi, 1)
                if not (isinstance(g, int) and g < 1):
                    sc.wait_ge(f_cst, 16 * g)
                nsc.activation(bcrow[:, :], M0[0:BC, 0:T], ACT.Copy).then_inc(f_cr, 1)
                if not (isinstance(g, int) and g < 1):
                    sc.wait_ge(f_dtps, 2 * g)
                nsc.activation(dtr[:, :], M0[RK:RK + RANK, 0:T], ACT.Copy).then_inc(f_rank, 1)

            def bc_mid(g, k):
                sc.wait_ge(f_res, g + 1)
                nsc.activation(S[k][0:2 * BC, :], Rm[:, :], ACT.Copy).then_inc(f_mid, 1)

            def abs_relu(g):
                if not (isinstance(g, int) and g < 1):
                    sc.wait_ge(f_nd, g)
                    sc.wait_ge(f_dt, g)
                for h in range(HALF):
                    sc.wait_ge(f_dtps, 2 * g + h + 1)
                    nsc.activation(absx[:, h, :], (M0, M2)[h][:, 0:T], ACT.Abs, bias=db[:, h:h + 1])
                    nsc.activation(relx[:, h, :], (M0, M2)[h][:, 0:T], ACT.Relu, bias=db[:, h:h + 1])\
                       .then_inc(f_abs, 1)

            def exps(g):
                sc.wait_ge(f_abs, 2 * g + 2)
                nsc.activation(expx[:, :, :], absx[:, :, :], ACT.Exp, scale=-1.0).then_inc(f_exp, 1)
                sc.wait_ge(f_exp, g + 1)
                nsc.activation(onex[:, :, :], expx[:, :, :], ACT.Identity, bias=1.0)

            def ln_of_one_plus(g):
                sc.wait_ge(f_exp, g + 1)
                nsc.activation(lnx[:, :, :], expx[:, :, :], ACT.Ln, bias=1.0).then_inc(f_ln1, 1)

            def square(g, cen_done, sq_done, src, dst, var_done):
                sc.wait_ge(cen_done, g + 1)
                if not (isinstance(g, int) and g < 1):
                    sc.wait_ge(var_done, g)
                nsc.activation(dst, src, ACT.Square).then_inc(sq_done, 1)

            def rsqrt_ln(g, stat, st_sem, ln_sem):
                sc.wait_ge(st_sem, 5 * g + 1)
                nsc.activation(stat[:, 1, :], stat[:, 0, :], ACT.Ln).then_inc(ln_sem, 1)

            def rsqrt_exp(g, stat, ln_sem, rsq_sem):
                sc.wait_ge(ln_sem, g + 1)
                nsc.activation(stat[:, 2, :], stat[:, 1, :], ACT.Exp, scale=-0.5).then_inc(rsq_sem, 1)

            def rows_copy(g, k):
                sc.wait_ge(b_tr, g + 1)
                if not (isinstance(g, int) and g < 2):
                    sc.wait_ge(b_out[k], ((g - k) // 2) * 16 if isinstance(g, int) else (g - k) * 8)
                nsc.activation(rows[k][:, :], M1[0:CP, :], ACT.Copy).then_inc(b_rows, 1)

            def logits(g):
                sc.wait_ge(b_lps, g + 1)
                dst = Lg[:, g, :] if isinstance(g, int) else Lg[:, ds(g, 1), :].rearrange("p a e -> p (a e)")
                nsc.activation(dst, M1[0:CP, 0:E], ACT.Copy).then_inc(b_log, 1)

            sc.wait_ge(s_setup, SETUP + 1)
            for h in range(HALF):
                nsc.activation(u[1][:, h, 0:1], M0[:, h:h + 1], ACT.Silu, bias=cb[:, h:h + 1])\
                   .then_inc(s_setup, 1)
            sc.wait_ge(s_setup, SETUP + 4)
            nsc.activation(S[1][:, 0:1], M0[0:3 * BC, 4:5], ACT.Copy)
            nsc.activation(dtr[:, 0:1], M0[RK:RK + RANK, 4:5], ACT.Copy).then_inc(s_setup, 1)
            sc.wait_ge(s_setup, SETUP + 6)
            nsc.activation(S[1][0:2 * BC, 0:1], Rm[:, 0:1], ACT.Copy).then_inc(s_setup, 1)
            sc.wait_ge(s_setup, SETUP + 9)
            for h in range(HALF):
                nsc.activation(absx[:, h, 0:1], M0[:, 12 + h:13 + h], ACT.Abs, bias=db[:, h:h + 1])
                nsc.activation(relx[:, h, 0:1], M0[:, 12 + h:13 + h], ACT.Relu, bias=db[:, h:h + 1])\
                   .then_inc(s_setup, 1)
            sc.wait_ge(s_setup, SETUP + 11)
            nsc.activation(expx[:, :, 0:1], absx[:, :, 0:1], ACT.Exp, scale=-1.0).then_inc(s_setup, 1)
            sc.wait_ge(s_setup, SETUP + 12)
            nsc.activation(onex[:, :, 0:1], expx[:, :, 0:1], ACT.Identity, bias=1.0)
            nsc.activation(lnx[:, :, 0:1], expx[:, :, 0:1], ACT.Ln, bias=1.0).then_inc(s_setup, 1)
            sc.wait_ge(s_setup, TOKEN_DONE)

            for g in range(2):
                square(g, f_cen, f_sq, cen, sq, f_var)
                rsqrt_ln(g, st, f_st, f_ln)
                rsqrt_exp(g, st, f_ln, f_rsq)
            silu_u(0, 0)
            bc_hi(0, 0)
            z_copy(0, 0, 0)
            bc_mid(0, 0)
            z_copy(0, 0, 1)
            abs_relu(0)
            exps(0)
            ln_of_one_plus(0)
            square(2, f_cen, f_sq, cen, sq, f_var)
            def back_piece(n, g, k):
                if n == 15:
                    square(g, b_cen, b_sq, cen2, sq2, b_var)

            def late_piece(n, g, k):
                if n == 3:
                    rsqrt_ln(g, st2, b_st, b_ln)
                    rsqrt_exp(g, st2, b_ln, b_rsq)
                if n == 7:
                    rows_copy(g, k)
                if n == 9:
                    logits(g)

            def batch(b, first, last):
                for j in range(JC):
                    g, k = b * JC + j, j % 2
                    front = not (last and j == JC - 1)
                    front1 = not (last and j >= JC - 2)
                    front0 = not (last and j >= JC - 3)
                    for n in range(NS):
                        i = NS * g + n
                        m = (NS * j + n) % AHEAD
                        if n == 0:
                            sc.wait_ge(f_dt, g + 1)
                        if not (first and j == 0 and n < AHEAD):
                            sc.wait_ge(m_h, i - AHEAD + 1)
                        for h in range(HALF):
                            a = nsc.activation(dA[m][:, h, :], dt[k][:, h, :], ACT.Exp, scale=An[:, h, n:n + 1])
                        a.then_inc(m_dA, 1)
                        if not (first and j < 2):
                            late_piece(n, g - 2, k)
                        if n == 5:
                            if front:
                                silu_u(g + 1, 1 - k)
                            silu_z(g, k)
                        if front:
                            if n == 7:
                                bc_hi(g + 1, 1 - k)
                                z_copy(g + 1, 1 - k, 0)
                            if n == 8:
                                bc_mid(g + 1, 1 - k)
                            if n == 9:
                                z_copy(g + 1, 1 - k, 1)
                            if n == 10:
                                abs_relu(g + 1)
                        if front0 and n == 15:
                            square(g + 3, f_cen, f_sq, cen, sq, f_var)
                        if n == 11:
                            if front:
                                exps(g + 1)
                                ln_of_one_plus(g + 1)
                            if front1:
                                rsqrt_ln(g + 2, st, f_st, f_ln)
                                rsqrt_exp(g + 2, st, f_ln, f_rsq)
                        if not (first and j == 0):
                            back_piece(n, g - 1, 1 - k)
            batches(sc, batch)
            for n in range(NS):
                late_piece(n, NCH - 2, 0)
            for n in range(NS):
                back_piece(n, NCH - 1, 1)

            def xT_copy(t, k):
                sc.wait_ge(t_xps, t + 1)
                nsc.activation(xT[k].rearrange("p r t -> p (r t)"), bank[4][:, :], ACT.Copy).then_inc(t_xT, 1)

            def silu(t, q):
                sc.wait_ge(t_h, 2 * t + q + 1)
                if not (isinstance(t, int) and t == 0):
                    sc.wait_ge(t_act, 2 * t + q - 1)
                nsc.activation(sil[q], bank[q][:, :], ACT.Silu).then_inc(t_silu, 1)

            def y_copy(t, k):
                sc.wait_ge(t_yps, t + 1)
                if not (isinstance(t, int) and t < 2):
                    sc.wait_ge(t_out[k], (t - k) * 8)
                nsc.activation(yout[k], bank[7][:, :], ACT.Copy).then_inc(t_y, 1)

            def tile(t, k, behind, ahead):
                silu(t, 0)
                silu(t, 1)
                if behind:
                    y_copy(t - 1, 1 - k)
                if ahead:
                    xT_copy(t + 1, 1 - k)
            sc.wait_ge(s_setup, TOKEN_DONE)
            xT_copy(0, 0)
            silu(0, 0)
            silu(0, 1)
            for n in range(4):
                late_piece(n, NCH - 1, 1)
            xT_copy(1, 1)
            silu(1, 0)
            silu(1, 1)
            for n in range(4, NS):
                late_piece(n, NCH - 1, 1)
            y_copy(0, 0)
            xT_copy(2, 0)
            sc.wait_ge(r_ch, 2)
            nsc.activation(rt[1], rt[0], ACT.Exp).then_inc(r_exp, 1)

            tile(2, 0, True, True)
            with sc.Fori(1, (NT - 3) // 2) as t2:
                tile(2 * t2 + 1, 1, True, True)
                tile(2 * t2 + 2, 0, True, True)
            tile(NT - 2, 1, True, True)
            tile(NT - 1, 0, True, False)
            y_copy(NT - 1, 0)

        @block.vector
        def _(v):
            nv = nc.vector
            v.wait_ge(s_setup, 1)
            nv.tensor_scalar(An[:, :, :], An[:, :, :], -1.0, None, ALU.mult).then_inc(s_setup, 1)
            for h in range(HALF):
                for tap in range(TAPS):
                    last = nv.tensor_scalar(wsc[h][:, tap, :], in_raw[:, h, :], cw[:, h, tap:tap + 1], None, ALU.mult)
            last.then_inc(s_setup, 1)
            v.wait_ge(s_setup, 4)
            for h in range(HALF):
                nv.tensor_copy(Wu[:, h, :, :].rearrange("p k d -> p (k d)"), bank[h][:, :])
                nv.tensor_copy(Wz[:, h, :], bank[2][:, h * P:(h + 1) * P])
                nv.tensor_copy(Wo[:, h, :], bank[2][:, (2 + h) * P:(3 + h) * P])
                nv.tensor_copy(Wx[:, h, :], bank[3][:, h * P:h * P + RK + RANK])
                nv.tensor_copy(Wd[:, h, :], bank[4][0:RANK, h * P:(h + 1) * P])
            nv.tensor_copy(gT[:, :, :].rearrange("p r e -> p (r e)"), bank[3][:, 256:256 + RR * E])\
              .then_inc(s_setup, SETUP - 4)
            v.wait_ge(s_setup, SETUP + 5)
            nv.tensor_tensor(Rm[:, 0:1], M0[0:2 * BC, 4:5], S[1][0:2 * BC, 0:1], ALU.subtract).then_inc(s_setup, 1)
            v.wait_ge(s_setup, SETUP + 7)
            nv.tensor_tensor(S[1][0:BC, 0:1], Rm[0:BC, 0:1], S[1][0:BC, 0:1], ALU.subtract).then_inc(s_setup, 1)
            v.wait_ge(s_setup, SETUP + 13)
            nv.scalar_tensor_tensor(out=onex[:, :, 0], in0=onex[:, :, 0], scalar=-1.0, in1=expx[:, :, 0],
                                    op0=ALU.add, op1=ALU.subtract).then_inc(s_setup, 1)
            v.wait_ge(s_setup, SETUP + 14)
            nv.tensor_tensor(lnx[:, :, 0], lnx[:, :, 0], onex[:, :, 0], ALU.subtract).then_inc(s_setup, 1)
            v.wait_ge(s_setup, SETUP + 15)
            nv.tensor_tensor(lnx[:, :, 0], lnx[:, :, 0], relx[:, :, 0], ALU.add).then_inc(s_setup, 1)
            v.wait_ge(s_setup, SETUP + 16)
            nv.tensor_tensor(lnx[:, :, 0], lnx[:, :, 0], u[1][:, :, 0], ALU.mult).then_inc(s_setup, 1)
            v.wait_ge(s_setup, SETUP + 18)
            for h in range(HALF):
                last = nv.tensor_scalar(h0[:, :, h], M0[:, 16:16 + NS], lnx[:, h, 0:1], None, ALU.mult)
            last.then_inc(s_setup, 1)

            def newton(g, stat, rsq_sem, st_sem, used):
                v.wait_ge(rsq_sem, g + 1)
                if not (isinstance(g, int) and g < 1):
                    v.wait_ge(used, g)
                nv.tensor_tensor(stat[:, 3, :], stat[:, 2, :], stat[:, 2, :], ALU.mult).then_inc(st_sem, 1)
                v.wait_ge(st_sem, 5 * g + 2)
                nv.tensor_tensor(stat[:, 3, :], stat[:, 3, :], stat[:, 0, :], ALU.mult).then_inc(st_sem, 1)
                v.wait_ge(st_sem, 5 * g + 3)
                nv.tensor_scalar(stat[:, 3, :], stat[:, 3, :], -0.5, 1.5, ALU.mult, ALU.add).then_inc(st_sem, 1)
                v.wait_ge(st_sem, 5 * g + 4)
                nv.tensor_tensor(stat[:, 3, :], stat[:, 3, :], stat[:, 2, :], ALU.mult).then_inc(st_sem, 1)
                v.wait_ge(st_sem, 5 * g + 5)

            def centre(g, b, j, mean_sem, done, dst, ps):
                v.wait_ge(mean_sem, g + 1)
                nv.tensor_tensor(dst, xchunk(b, j), ps[:, 0:CP].unsqueeze(1).to_broadcast([P, RR, CP]),
                                 ALU.subtract).then_inc(done, 1)

            def front0_piece(n, g, b, j):
                if n == 13:
                    if not (isinstance(g, int) and g < 1):
                        v.wait_ge(f_seq, g)
                    centre(g, b, j, f_mean, f_cen, cen, M0)

            def front1_piece(n, g, k):
                if n == 0:
                    v.wait_ge(f_var, g + 1)
                    if not (isinstance(g, int) and g < 1):
                        v.wait_ge(f_st, 5 * g)
                    nv.tensor_scalar(st[:, 0, :], M0[:, P:P + CP], EPS_C, None, ALU.add).then_inc(f_st, 1)
                if n == 12:
                    newton(g, st, f_rsq, f_st, f_seq)
                    if not (isinstance(g, int) and g < 2):
                        v.wait_ge(f_zps, 2 * (g - 1))
                        v.wait_ge(f_hist, g)
                    sview = seq[k][:, HIST:].rearrange("p (h a w e) -> p a e h w", h=HC, a=R, w=W)
                    cview = cen.rearrange("p (a e) (h w) -> p a e h w", a=R, h=HC)
                    rview = st[:, 3, :].rearrange("p (h w) -> p h w", h=HC).unsqueeze(1).to_broadcast([P, R, HC, W])
                    for a in range(R):
                        last = nv.tensor_tensor(sview[:, a], cview[:, a], rview, ALU.mult)
                    last.then_inc(f_seq, 1)

            def front2_piece(n, g, k):
                if n == 6:
                    v.wait_ge(f_hi, g + 1)
                    v.wait_ge(f_rank, g + 1)
                    if not (isinstance(g, int) and g < 1):
                        v.wait_ge(f_mid, g)
                        v.wait_ge(f_lo, g)
                    nv.tensor_tensor(Rm[:, :], M0[0:2 * BC, 0:T], S[k][0:2 * BC, :], ALU.subtract).then_inc(f_res, 1)
                if n == 8:
                    v.wait_ge(f_mid, g + 1)
                    nv.tensor_tensor(S[k][0:BC, :], Rm[0:BC, :], S[k][0:BC, :], ALU.subtract).then_inc(f_lo, 1)
                if n == 11:
                    v.wait_ge(f_ln1, g + 1)
                    nv.scalar_tensor_tensor(out=onex[:, :, :], in0=onex[:, :, :], scalar=-1.0, in1=expx[:, :, :],
                                            op0=ALU.add, op1=ALU.subtract).then_inc(f_nd, 1)

            def back_piece(n, g, b, j, k):
                if n == 2:
                    v.wait_ge(m_y, NS * (g + 1))
                    if not (isinstance(g, int) and g < 1):
                        v.wait_ge(b_ops, g)
                    for h in range(HALF):
                        last = nv.scalar_tensor_tensor(out=yd[:, h, :], in0=u[k][:, h, :], scalar=Dk[:, h:h + 1],
                                                       in1=Yb[h][:, 0:T], op0=ALU.mult, op1=ALU.add)
                    last.then_inc(b_yd, 1)
                    v.wait_ge(b_yd, g + 1)
                    v.wait_ge(f_z, g + 1)
                    nv.tensor_tensor(yd[:, :, :], yd[:, :, :], z[k][:, :, :], ALU.mult).then_inc(b_ydz, 1)
                if n == 10:
                    v.wait_ge(b_ops, g + 1)
                    ov = M1[:, 0:T].rearrange("p (h a w e) -> p a e h w", h=HC, a=R, w=W)
                    for a in range(R):
                        xv = X[:, ds(b * RR + a * R, R), j * CP:(j + 1) * CP].rearrange("p e (h w) -> p e h w", h=HC)
                        last = nv.tensor_tensor(xv, xv, ov[:, a], ALU.add)
                    last.then_inc(b_x, 1)
                if n == 13:
                    if not (isinstance(g, int) and g < 1):
                        v.wait_ge(b_lps, g)
                    centre(g, b, j, b_mean, b_cen, cen2, M1)

            def late_piece(n, g):
                if n == 0:
                    v.wait_ge(b_var, g + 1)
                    if not (isinstance(g, int) and g < 1):
                        v.wait_ge(b_st, 5 * g)
                    nv.tensor_scalar(st2[:, 0, :], M1[:, P:P + CP], EPS_T, None, ALU.add).then_inc(b_st, 1)
                if n == 3:
                    newton(g, st2, b_rsq, b_st, b_xn)
                    nv.tensor_tensor(cen2, cen2, st2[:, 3, :].unsqueeze(1).to_broadcast([P, RR, CP]),
                                     ALU.mult).then_inc(b_xn, 1)

            v.wait_ge(s_setup, TOKEN_DONE)
            v.wait_ge(s_x0, 16)
            for g in range(2):
                for n in range(NS):
                    front0_piece(n, g, 0, g)
                for n in range(NS):
                    front1_piece(n, g, g)
            for n in range(NS):
                front2_piece(n, 0, 0)
            for n in range(NS):
                front0_piece(n, 2, 0, 2)
            v.wait_ge(s_x, 16 * (B - 1))

            def batch(b, first, last):
                for j in range(JC):
                    g, k = b * JC + j, j % 2
                    front = not (last and j == JC - 1)
                    front1 = not (last and j >= JC - 2)
                    front0 = not (last and j >= JC - 3)

                    def times_B(n):
                        i = NS * g + n
                        v.wait_ge(m_B, i + 1)
                        if n == 0:
                            v.wait_ge(f_dtu, g + 1)
                        if not (first and j == 0 and n < 3):
                            v.wait_ge(m_h, i - 2)
                        nv.tensor_tensor(dBu[(NS * j + n) % 3], dtu[k][:, :, :],
                                         Bb[(NS * j + n) % 3][:, 0:T].unsqueeze(1).to_broadcast([P, HALF, T]),
                                         ALU.mult).then_inc(m_dBu, 1)
                    times_B(0)
                    for n in range(NS):
                        i = NS * g + n
                        m = n % RING
                        if n < NS - 1:
                            times_B(n + 1)
                        v.wait_ge(m_dBu, i + 1)
                        v.wait_ge(m_dA, i + 1)
                        if not (first and j == 0 and n < RING):
                            v.wait_ge(m_hC, i - RING + 1)
                            v.wait_ge(m_carry, i - RING + 1)
                        for h in range(HALF):
                            init = (h0 if j == 0 else carry)[:, n, h:h + 1]
                            last_scan = nv.tensor_tensor_scan(hs[m][:, h, :], dA[(NS * j + n) % AHEAD][:, h, :], dBu[(NS * j + n) % 3][:, h, :],
                                                              init, ALU.mult, ALU.add)
                        last_scan.then_inc(m_h, 1)
                        if not (first and j < 2):
                            late_piece(n, g - 2)
                        if not (first and j == 0):
                            back_piece(n, g - 1, b if j else b - 1, (j - 1) % JC, 1 - k)
                        if front:
                            front2_piece(n, g + 1, 1 - k)
                        if front1:
                            front1_piece(n, g + 2, k)
                        if front0:
                            front0_piece(n, g + 3, b if j < JC - 3 else b + 1, (j + 3) % JC)
            batches(v, batch)
            for n in range(NS):
                late_piece(n, NCH - 2)
            for n in range(NS):
                back_piece(n, NCH - 1, B - 1, JC - 1, 1)

            step = [0]

            def link(ins):
                step[0] += 1
                ins.then_inc(r_ch, 1)
                v.wait_ge(r_ch, step[0])
            Lv = Lg[:, :, :]
            ge, eg = "p (g e) -> p g e", "p (e g) -> p e g"
            q0, q1, q2, q3, q4, q5 = rt

            def g3(t):
                return t.rearrange(ge, e=E)

            def wide(t):
                return t.unsqueeze(2).to_broadcast([CP, NCH, E])
            mx = small[:, 0, 0:NCH]
            c4 = cmp3.rearrange("p (g e f) -> p g e f", e=E, f=E)
            til, end, base, one8 = (small[:, a, 0:E] for a in range(1, 5))

            def softmax_and_greater():
                v.wait_ge(b_log, NCH)
                v.wait_ge(m_carry, NS * NCH)
                link(nv.reduce_max(mx, Lv, AX.X))
                link(nv.tensor_tensor(g3(q0), Lv, wide(mx), ALU.subtract))
                v.wait_ge(r_exp, 1)
                link(nv.reduce_sum(mx, g3(q1), AX.X))
                link(nv.reciprocal(mx, mx))
                link(nv.tensor_tensor(g3(q1), g3(q1), wide(mx), ALU.mult))
                for e in range(E):
                    s_e = g3(q1)[:, :, e:e + 1].to_broadcast([CP, NCH, E])
                    link(nv.tensor_tensor(c4[:, :, e, :], g3(q1), s_e, ALU.is_gt))
                link(nv.reduce_sum(g3(q2), c4, AX.X))

            def choose():
                for e in range(E):
                    s_e = g3(q1)[:, :, e:e + 1].to_broadcast([CP, NCH, E])
                    link(nv.tensor_tensor(c4[:, :, e, :], g3(q1), s_e, ALU.is_equal))
                    link(nv.tensor_tensor(c4[:, :, e, :], c4[:, :, e, :],
                                          low[:, e, :].unsqueeze(1).to_broadcast([CP, NCH, E]), ALU.mult))
                link(nv.reduce_sum(g3(q3), c4, AX.X))
                link(nv.tensor_tensor(q2, q2, q3, ALU.add))
                link(nv.tensor_scalar(q3, q2, 1.0, None, ALU.is_le))

            def weights_of_the_two():
                for s in range(2):
                    link(nv.tensor_scalar(q4, q2, float(s), None, ALU.is_equal))
                    link(nv.tensor_tensor(q4, q4, q1, ALU.mult))
                    link(nv.reduce_sum(wgt[:, s, :], g3(q4), AX.X))
                link(nv.tensor_tensor(mx, wgt[:, 0, :], wgt[:, 1, :], ALU.add))
                link(nv.tensor_scalar(mx, mx, 1e-20, None, ALU.add))
                link(nv.reciprocal(mx, mx))
                for s in range(2):
                    link(nv.tensor_tensor(wgt[:, s, :], wgt[:, s, :], mx, ALU.mult))

            def take_counts():
                v.wait_ge(r_ps, 1)
                link(nv.tensor_copy(q3, M0[0:CP, 0:NCH * E]))
                nv.tensor_copy(q0.rearrange(eg, e=E), M2[0:CP, 0:NCH * E].rearrange("p (g e) -> p e g", e=E))\
                  .then_inc(r_cp, 1)
                v.wait_ge(r_cp, 1)

            def places():
                link(nv.memset(q4, 1.0))
                link(nv.memset(q4.rearrange(eg, e=E)[:, :, 0:1], 0.0))
                link(nv.tensor_tensor_scan(q5, q4, q0, 0.0, ALU.mult, ALU.add))
                cnt = q5.rearrange(eg, e=E)[:, :, NCH - 1]
                link(nv.tensor_scalar(smalli[:, :], cnt, float(P - 1), None, ALU.add))
                link(nv.tensor_scalar(smalli[:, :], smalli[:, :], P.bit_length() - 1, None, ALU.logical_shift_right))
                link(nv.tensor_copy(til, smalli[:, :]))
                link(nv.memset(one8, 1.0))
                link(nv.tensor_tensor_scan(end, one8, til, 0.0, ALU.mult, ALU.add))
                link(nv.tensor_tensor(base, end, til, ALU.subtract))
                link(nv.tensor_scalar(base, base, float(P), float(SHT * P), ALU.mult, ALU.add))
                link(nv.tensor_tensor(q5, q5, q0, ALU.subtract))
                link(nv.tensor_tensor(q5.rearrange(eg, e=E), q5.rearrange(eg, e=E),
                                      base.unsqueeze(2).to_broadcast([CP, E, NCH]), ALU.add))
                link(nv.tensor_tensor(g3(q0), q5.rearrange("p (e g) -> p g e", e=E),
                                      g3(q3), ALU.add))
                for s in range(2):
                    link(nv.tensor_scalar(q4, q2, float(s), None, ALU.is_equal))
                    link(nv.tensor_tensor(q4, q4, q0, ALU.mult))
                    link(nv.reduce_sum(mx, g3(q4), AX.X))
                    link(nv.tensor_copy(dsti[:, s, :], mx))
                link(nv.tensor_scalar(endt[:, :], end[0:1, :], float(SHT), None, ALU.add))

            def tables():
                tf, et = small[:, 5, 0:RTT], small[:, 6, 0:RTT]
                link(nv.tensor_copy(tf, tileno[:, :]))
                c2 = cmp3[:, 0:RTT * E].rearrange("p (t e) -> p t e", e=E)
                link(nv.tensor_tensor(c2, end.unsqueeze(1).to_broadcast([CP, RTT, E]),
                                      tf.unsqueeze(2).to_broadcast([CP, RTT, E]), ALU.is_le))
                link(nv.reduce_sum(et, c2, AX.X))
                link(nv.memset(tset[:, 0:SHT], 0))
                link(nv.tensor_scalar(tset[:, SHT:NT], et[0:1, :], float(E - 1), 1.0, ALU.min, ALU.add))
                link(nv.tensor_scalar(twait[:, :], tset[:, :], 48.0, 32.0, ALU.mult, ALU.add))
                link(nv.tensor_scalar(toff[:, :], tset[:, :], 1, None, ALU.bitwise_and))
                link(nv.tensor_scalar(toff[:, :], toff[:, :], float(SETW), None, ALU.mult))
                nv.memset(small[:, 7, :], 0.0).then_inc(r_done, 1)

            def gate(t, q):
                v.wait_ge(t_silu, 2 * t + q + 1)
                if not (isinstance(t, int) and t == 0):
                    v.wait_ge(t_aps, 2 * t + q - 1)
                nv.tensor_tensor(act[q], sil[q], bank[2 + q][:, :], ALU.mult).then_inc(t_act, 1)

            def actT_copy(t, q):
                v.wait_ge(t_aps, 2 * t + q + 1)
                if not (isinstance(t, int) and t == 0):
                    v.wait_ge(t_yps, t)
                nv.tensor_copy(actT[q].rearrange("p k t -> p (k t)"), bank[5 + q][:, :]).then_inc(t_aT, 1)

            def tile(t, between=None):
                gate(t, 0)
                gate(t, 1)
                if between:
                    between()
                actT_copy(t, 0)
                actT_copy(t, 1)
            def last_norm():
                for n in range(NS):
                    late_piece(n, NCH - 1)
            tile(0, last_norm)
            tile(1)
            softmax_and_greater()
            tile(2)
            choose()
            tile(3)
            weights_of_the_two()
            tile(4, take_counts)
            places()
            tile(5)
            tables()
            with v.Fori(6, NT) as t:
                tile(t)

            def add_sum(b, j):
                v.wait_ge(c_ps, b * JC + j + 1)
                xv = xchunk(b, j)
                nv.tensor_tensor(xv, xv, bank[j][:, 0:T].rearrange("p (r q) -> p r q", r=RR),
                                 ALU.add).then_inc(c_x, 1)

            def combine(b):
                for j in range(JC):
                    g = b * JC + j
                    v.wait_ge(c_g[j], 32 * b + 32)
                    v.wait_ge(c_sh[j], 16 * b + 16)
                    if started(b):
                        v.wait_ge(c_ps, g - JC + 1)
                    w0s = wgt[:, 0, ds(g, 1)]
                    w1s = wgt[:, 1, ds(g, 1)]
                    nv.scalar_tensor_tensor(out=ysh[j], in0=y0[j], scalar=w0s, in1=ysh[j],
                                            op0=ALU.mult, op1=ALU.add).then_inc(c_a, 1)
                    v.wait_ge(c_a, g + 1)
                    nv.scalar_tensor_tensor(out=ysum[j], in0=y1[j], scalar=w1s, in1=ysh[j],
                                            op0=ALU.mult, op1=ALU.add).then_inc(c_s, 1)
                    if j:
                        add_sum(b, j - 1)
                add_sum(b, JC - 1)
            peeled(v, B, combine)

        @block.tensor
        def _(pe):
            te = nc.tensor
            mm = te.matmul
            pe.wait_ge(s_const, NCONST)
            pe.wait_ge(s_in, 16 * 14)
            pe.wait_ge(s_setup, 3)
            for h in range(HALF):
                for tap in range(TAPS):
                    te.transpose(bank[h][:, tap * P:(tap + 1) * P], wsc[h][:, tap, :], ident[:, :])
                te.transpose(bank[2][:, h * P:(h + 1) * P], in_raw[:, HALF + h, :], ident[:, :])
                te.transpose(bank[2][:, (2 + h) * P:(3 + h) * P], ow_raw[:, h * P:(h + 1) * P], ident[:, :])
                te.transpose(bank[3][:, h * P:h * P + RK + RANK], xp_raw[:, h * P:(h + 1) * P],
                             ident[0:RK + RANK, 0:RK + RANK])
                te.transpose(bank[4][0:RANK, h * P:(h + 1) * P], dp_raw[:, h, :], ident[:, :])
            for r in range(RR):
                last = te.transpose(bank[3][:, 256 + r * E:256 + (r + 1) * E], gw_raw[:, r::RR], ident[0:E, 0:E])
            last.then_inc(s_setup, 1)
            pe.wait_ge(s_setup, SETUP)
            for h in range(HALF):
                last = mm(M0[:, h:h + 1], Wu[:, h, TAPS - 1, :], tokh[:, HIST - 1:HIST], start=True, stop=True)
            last.then_inc(s_setup, 1)
            pe.wait_ge(s_setup, SETUP + 3)
            for h in range(HALF):
                last = mm(M0[0:RK + RANK, 4:5], Wx[:, h, :], u[1][:, h, 0:1], start=(h == 0), stop=(h == HALF - 1))
            last.then_inc(s_setup, 1)
            pe.wait_ge(s_setup, SETUP + 8)
            for h in range(HALF):
                last = mm(M0[:, 12 + h:13 + h], Wd[:, h, :], dtr[:, 0:1], start=True, stop=True)
            last.then_inc(s_setup, 1)
            pe.wait_ge(s_setup, SETUP + 17)
            for n in range(NS):
                last = mm(M0[:, 16 + n:17 + n], sel[:, n, :], S[1][:, 0:1], start=True, stop=True)
            last.then_inc(s_setup, 1)

            def front0_piece(n, g, b, j):
                if n == 12:
                    if isinstance(g, int) and g == 1:
                        pe.wait_ge(f_st, 1)
                    elif started(g):
                        pe.wait_ge(f_abs, 2 * (g - 1))
                    for r in range(RR):
                        last = mm(M0[:, 0:CP], meanw[:, :], xchunk(b, j)[:, r, :], start=(r == 0), stop=(r == RR - 1))
                    last.then_inc(f_mean, 1)

            def front1_piece(n, g):
                if n == 0:
                    pe.wait_ge(f_sq, g + 1)
                    for r in range(RR):
                        last = mm(M0[:, P:P + CP], meanw[:, :], sq[:, r, :], start=(r == 0), stop=(r == RR - 1))
                    last.then_inc(f_var, 1)

            def z_product(g, k, h):
                mm(M2[:, 0:T], Wz[:, h, :], seq[k][:, HIST:HIST + T], start=True, stop=True).then_inc(f_zps, 1)

            def front2_piece(n, g, k):
                if n in (0, 1, 2, 3):
                    h, two = 1 - n // 2, n % 2
                    if n == 0:
                        pe.wait_ge(f_seq, g + 1)
                        pe.wait_ge(f_hist, g + 1)
                        if started(g):
                            pe.wait_ge(f_abs, 2 * g)
                    if n == 2:
                        pe.wait_ge(f_st, 5 * NCH if isinstance(g, int) and g == NCH - 1 else 5 * (g + 1) + 1)
                    for tap in (2 * two, 2 * two + 1):
                        last = mm((M0, M2)[h][:, 0:T], Wu[:, h, tap, :], seq[k][:, tap:tap + T],
                                  start=(tap == 0), stop=(tap == TAPS - 1))
                    if two:
                        last.then_inc(f_ups, 1)
                if n == 5:
                    pe.wait_ge(f_u, 2 * g + 2)
                    for h in range(HALF):
                        last = mm(M0[0:RK + RANK, 0:T], Wx[:, h, :], u[k][:, h, :],
                                  start=(h == 0), stop=(h == HALF - 1))
                    last.then_inc(f_bcps, 1)
                    z_product(g, k, 0)
                if n == 8:
                    pe.wait_ge(f_zc, 2 * g + 1)
                    z_product(g, k, 1)
                if n == 9:
                    pe.wait_ge(f_rank, g + 1)
                    pe.wait_ge(f_cr, g + 1)
                    pe.wait_ge(f_res, g + 1)
                    pe.wait_ge(f_zc, 2 * g + 2)
                    for h in range(HALF):
                        mm((M0, M2)[h][:, 0:T], Wd[:, h, :], dtr[:, :], start=True, stop=True).then_inc(f_dtps, 1)

            def back_piece(n, g, b, j):
                if n == 10:
                    pe.wait_ge(b_ydz, g + 1)
                    if not (isinstance(g, int) and g < 1):
                        pe.wait_ge(b_log, g)
                    for h in range(HALF):
                        last = mm(M1[:, 0:T], Wo[:, h, :], yd[:, h, :], start=(h == 0), stop=(h == HALF - 1))
                    last.then_inc(b_ops, 1)
                if n == 12:
                    pe.wait_ge(b_x, g + 1)
                    for r in range(RR):
                        last = mm(M1[:, 0:CP], meanw[:, :], xchunk(b, j)[:, r, :], start=(r == 0), stop=(r == RR - 1))
                    last.then_inc(b_mean, 1)

            def late_piece(n, g):
                if n == 0:
                    pe.wait_ge(b_sq, g + 1)
                    for r in range(RR):
                        last = mm(M1[:, P:P + CP], meanw[:, :], sq2[:, r, :], start=(r == 0), stop=(r == RR - 1))
                    last.then_inc(b_var, 1)
                if n == 5:
                    pe.wait_ge(b_xn, g + 1)
                    for r in range(RR):
                        last = te.transpose(M1[0:CP, r * P:(r + 1) * P], cen2[:, r, :], ident[:, :])
                    last.then_inc(b_tr, 1)
                if n == 8:
                    pe.wait_ge(b_rows, g + 1)
                    for r in range(RR):
                        last = mm(M1[0:CP, 0:E], cen2[:, r, :], gT[:, r, :], start=(r == 0), stop=(r == RR - 1))
                    last.then_inc(b_lps, 1)

            pe.wait_ge(s_setup, TOKEN_DONE)
            pe.wait_ge(s_x0, 16)
            for g in range(2):
                for n in range(NS):
                    front0_piece(n, g, 0, g)
                for n in range(NS):
                    front1_piece(n, g)
            for n in range(NS):
                front2_piece(n, 0, 0)
            for n in range(NS):
                front0_piece(n, 2, 0, 2)
            pe.wait_ge(s_x, 16 * (B - 1))

            def spread(g, j, n, begun=True):
                i = NS * g + n
                if n == 0:
                    pe.wait_ge(f_lo, g + 1)
                if begun:
                    pe.wait_ge(m_dBu, i - 2)
                mm(Bb[(NS * j + n) % 3][:, 0:T], sel[:, n, :], S[j % 2][:, :], start=True, stop=True).then_inc(m_B, 1)

            def add_y(g, n, begun=True):
                pe.wait_ge(m_hC, NS * g + n + 1)
                if n == 0 and begun:
                    pe.wait_ge(b_yd, g)
                for h in range(HALF):
                    last = mm(Yb[h][:, 0:T], ident[:, :], hC[n % RING][:, h, :], start=(n == 0), stop=(n == NS - 1))
                last.then_inc(m_y, 1)
            spread(0, 0, 0, False)
            spread(0, 0, 1, False)

            def batch(b, first, last):
                for j in range(JC):
                    g, k = b * JC + j, j % 2
                    front = not (last and j == JC - 1)
                    front1 = not (last and j >= JC - 2)
                    front0 = not (last and j >= JC - 3)
                    for n in range(NS):
                        if n < NS - 2:
                            spread(g, j, n + 2, not (first and j == 0 and n == 0))
                        elif front:
                            spread(g + 1, j + 1, n + 2 - NS)
                        if n < 3:
                            if not (first and j == 0):
                                add_y(g - 1, NS - 3 + n)
                        elif n > 3:
                            if n == 4:
                                add_y(g, 0, not (first and j == 0))
                            add_y(g, n - 3)
                        if not (first and j < 2):
                            late_piece(n, g - 2)
                        if front:
                            front2_piece(n, g + 1, 1 - k)
                        if not (first and j == 0):
                            back_piece(n, g - 1, b if j else b - 1, (j - 1) % JC)
                        if front1:
                            front1_piece(n, g + 2)
                        if front0:
                            front0_piece(n, g + 3, b if j < JC - 3 else b + 1, (j + 3) % JC)
            batches(pe, batch)
            for n in range(NS - 3, NS):
                add_y(NCH - 1, n)
            for n in range(NS):
                late_piece(n, NCH - 2)
            for n in range(NS):
                back_piece(n, NCH - 1, B - 1, JC - 1)

            def counts():
                pe.wait_ge(r_ch, R_CHOSEN)
                mm(M0[0:CP, 0:NCH * E], tri[:, :], rt[3], start=True, stop=True)
                mm(M2[0:CP, 0:NCH * E], one96[:, :], rt[3], start=True, stop=True).then_inc(r_ps, 1)

            def x_transpose(t, k):
                pe.wait_ge(t_x[k], (t - k) * 8 + 16)
                if not (isinstance(t, int) and t == 0):
                    pe.wait_ge(t_xT, t)
                for r in range(RR):
                    last = te.transpose(bank[4][:, r * P:(r + 1) * P], xin[k][:, r * P:(r + 1) * P], ident[:, :])
                last.then_inc(t_xps, 1)

            def set_of(t, routed):
                return pe.value_load(toff[0:1, ds(t, 1)], min_val=0, max_val=SETW) if routed else 0

            def up(t, k, routed):
                off = set_of(t, routed)
                if routed:
                    loaded = pe.value_load(twait[0:1, ds(t, 1)], min_val=32, max_val=32 + 48 * E)
                    pe.wait_ge(s_w, loaded)
                pe.wait_ge(t_xT, t + 1)
                for q in range(2):
                    if not (isinstance(t, int) and t == 0):
                        pe.wait_ge(t_act, 2 * t + q - 1)
                    for w in range(2):
                        for r in range(RR):
                            last = mm(bank[2 * w + q][:, :], xT[k][:, r, :],
                                      WALL[:, ds(off + (w * RR * I + r * I + q * 512), 512)],
                                      start=(r == 0), stop=(r == RR - 1))
                    last.then_inc(t_h, 1)

            def down(t, routed):
                off = set_of(t, routed)
                for q in range(2):
                    pe.wait_ge(t_aT, 2 * t + q + 1)
                if not (isinstance(t, int) and t == 0):
                    pe.wait_ge(t_y, t)
                for c in range(IK):
                    last = mm(bank[7][:, :], actT[c // 4][:, c % 4, :],
                              WALL[:, ds(off + (2 * RR * I + c * C), C)],
                              start=(c == 0), stop=(c == IK - 1))
                last.then_inc(t_yps, 1)

            def act_transpose(t):
                for q in range(2):
                    pe.wait_ge(t_act, 2 * t + q + 1)
                    if not (isinstance(t, int) and t == 0):
                        pe.wait_ge(t_aT, 2 * t + q - 1)
                    for c in range(4):
                        last = te.transpose(bank[5 + q][:, c * P:(c + 1) * P], act[q][:, c * P:(c + 1) * P],
                                            ident[:, :])
                    last.then_inc(t_aps, 1)

            def tile(t, k, routed, behind=True, ahead=True, after_routed=None, with_counts=False):
                up(t, k, routed)
                if ahead:
                    x_transpose(t + 1, 1 - k)
                if behind:
                    down(t - 1, routed if after_routed is None else after_routed)
                if with_counts:
                    pe.wait_ge(t_aT, 2 * t)
                    counts()
                    pe.wait_ge(r_cp, 1)
                act_transpose(t)
            x_transpose(0, 0)
            pe.wait_ge(s_w, 32)
            up(0, 0, False)
            late_piece(0, NCH - 1)
            x_transpose(1, 1)
            act_transpose(0)
            up(1, 1, False)
            for n in range(1, NS):
                late_piece(n, NCH - 1)
            pe.wait_ge(s_w2, 16)
            pe.wait_ge(b_log, NCH)
            down(0, False)
            x_transpose(2, 0)
            act_transpose(1)
            tile(2, 0, False)
            tile(3, 1, False)
            tile(4, 0, False, with_counts=True)
            with pe.Fori(2, SHT // 2 - 1) as t2:
                tile(2 * t2 + 1, 1, False)
                tile(2 * t2 + 2, 0, False)
            tile(SHT - 1, 1, False)
            pe.wait_ge(r_done, 1)
            tile(SHT, 0, True, after_routed=False)
            with pe.Fori(SHT // 2, (NT - 3) // 2) as t2:
                tile(2 * t2 + 1, 1, True)
                tile(2 * t2 + 2, 0, True)
            tile(NT - 2, 1, True)
            tile(NT - 1, 0, True, ahead=False)
            down(NT - 1, True)

            def transpose_sums(b):
                for j in range(JC):
                    g = b * JC + j
                    pe.wait_ge(c_s, g + 1)
                    if started(b):
                        pe.wait_ge(c_x, g - JC + 1)
                    for r in range(RR):
                        last = te.transpose(bank[j][:, r * CP:(r + 1) * CP], ysum[j][:, r::RR], ident[0:CP, 0:CP])
                    last.then_inc(c_ps, 1)
            peeled(pe, B, transpose_sums)


_INS = ['x', 'L0_conv_global_token', 'L0_conv_in_proj_w', 'L0_conv_conv_w', 'L0_conv_conv_b', 'L0_conv_x_proj_w',
        'L0_conv_dt_proj_w', 'L0_conv_dt_proj_b', 'L0_conv_A_log', 'L0_conv_D', 'L0_conv_out_proj_w',
        'L0_ffn_gate_w', 'L0_ffn_w1', 'L0_ffn_w2', 'L0_ffn_w3', 'L0_ffn_sw1', 'L0_ffn_sw2', 'L0_ffn_sw3']


def kernel(**inputs):
    import numpy as _np
    import concourse.bacc as _bacc
    from concourse import mybir as _mybir
    from concourse.bass_utils import run_bass_kernel_spmd as _run

    nc = _bacc.Bacc("TRN2", target_bir_lowering=False, num_devices=1)
    arrays, args = {}, []
    for name in _INS:
        a = _np.ascontiguousarray(inputs[name])
        arrays[f"in_{name}_dram"] = a
        args.append(nc.dram_tensor(f"in_{name}_dram", a.shape, _mybir.dt.from_np(a.dtype), kind="ExternalInput").ap())
    shape = inputs['x'].shape
    args.append(nc.dram_tensor("out_0_dram", shape, _mybir.dt.float32, kind="ExternalOutput").ap())
    bass_metaformer_mamba_moe_kernel(nc, *args)
    r = _run(nc, [arrays], core_ids=[0])
    return r.results[0]["out_0_dram"]
```
